# Optimizing a Trainium2 kernel written in Bass

```python
import numpy as np
import jax
import jax.numpy as jnp

def _softmax(x, axis=-1):
    return jax.nn.softmax(x, axis=axis)

def _gelu(x):
    return jax.nn.gelu(x, approximate=True)

def _silu(x):
    return jax.nn.silu(x)

def _sigmoid(x):
    return jax.nn.sigmoid(x)

def _layernorm(x, axis=-1, eps=1e-05):
    m = jnp.mean(x, axis=axis, keepdims=True)
    v = jnp.var(x, axis=axis, keepdims=True)
    return (x - m) / jnp.sqrt(v + eps)

def _scatter_add(tgt, idx, src, axis=0):
    return tgt.at[idx].add(src)

def _segment_sum(src, seg, n):
    return jax.ops.segment_sum(src, seg, n)
kernel_name = 'mk_perceiver_d2_seqx_r4_3e1d93'

def setup_inputs(seed: int=0):
    np.random.seed(seed)
    _w = jnp.asarray

    def _rec_inputs():
        import jax
        import jax.numpy as jnp
        _rk = jax.random.key(seed)
        x = -0.000125 + 0.9999 * jax.random.normal(jax.random.fold_in(_rk, 1), (2, 64, 1024), jnp.float32)
        _lenS = 64 - jax.random.randint(jax.random.fold_in(_rk, 7), (2,), 0, max(1, 64 // 4) + 1, jnp.int32)
        _lenS2 = 1024 - jax.random.randint(jax.random.fold_in(_rk, 8), (2,), 0, max(1, 1024 // 4) + 1, jnp.int32)
        _ctx_4096P = jax.random.normal(jax.random.fold_in(_rk, 11), (2, 16, 1024), jnp.float32)
        _ctx_4096c = jax.random.dirichlet(jax.random.fold_in(_rk, 511), 0.3 * jnp.ones((16,), jnp.float32), (2, 1024))
        _ctx_4096t = jnp.einsum('bsk,bkd->bsd', _ctx_4096c, _ctx_4096P)
        _ctx_4096t = _ctx_4096t * jax.lax.rsqrt(jnp.mean(jnp.square(_ctx_4096t)) + 1e-12) * 0.953939
        ctx_4096 = -5.72187e-05 + 0.999849 * (_ctx_4096t + 0.3 * jax.random.normal(jax.random.fold_in(_rk, 611), (2, 1024, 1024), jnp.float32))
        return (x, ctx_4096)
    x, ctx_4096 = _rec_inputs()

    def _L0_xattn_setup():
        import jax, jax.numpy as jnp
        import numpy as np
        QMIN = 0.0
        QMAX = 255.0

        def fake_quant(x, scale, zp):
            s = scale.reshape(())
            z = zp.reshape(())
            q = jnp.clip(jnp.round(x / s + z), QMIN, QMAX)
            return (q - z) * s
        key = jax.random.key(seed)
        k1, k2 = jax.random.split(key)
        B, M, K, N = (4, 512, 1024, 1024)
        x1 = jax.random.normal(k1, (B, M, K), dtype=jnp.float32)
        x2 = jax.random.normal(k2, (B, K, N), dtype=jnp.float32)
        x1_scale = jnp.full((1,), 8.0 / 255.0, dtype=jnp.float32)
        x1_zp = jnp.full((1,), 128.0, dtype=jnp.float32)
        x2_scale = jnp.full((1,), 8.0 / 255.0, dtype=jnp.float32)
        x2_zp = jnp.full((1,), 128.0, dtype=jnp.float32)
        return {'x1': x1, 'x2': x2, 'x1_scale': x1_scale, 'x1_zp': x1_zp, 'x2_scale': x2_scale, 'x2_zp': x2_zp}
    _L0_xattn_all = _L0_xattn_setup()
    _L0_xattn_in = {k: v for k, v in _L0_xattn_all.items() if k in ('x1_scale', 'x1_zp', 'x2_scale', 'x2_zp')}
    del _L0_xattn_all

    def _L0_attn_setup():
        import jax, jax.numpy as jnp
        import numpy as np
        H = 1024
        D = 2048
        N = 16
        K = 4
        R = 64
        BATCH = 1
        L = 512
        EPS = 1e-06

        def _rmsnorm(x, w):
            return x * jax.lax.rsqrt(jnp.mean(x * x, axis=-1, keepdims=True) + EPS) * w
        key = jax.random.key(seed)
        ks = jax.random.split(key, 10)
        s = 0.02
        return {'hidden_states': jax.random.normal(ks[0], (BATCH, L, H), jnp.float32), 'W_in': jax.random.normal(ks[1], (2 * D, H), jnp.float32) * s, 'conv_w': jax.random.normal(ks[2], (D, K), jnp.float32) * s, 'conv_b': jax.random.normal(ks[3], (D,), jnp.float32) * s, 'Wx': jax.random.normal(ks[4], (R + 2 * N, D), jnp.float32) * s, 'dt_ln_w': jnp.ones((R,), jnp.float32), 'b_ln_w': jnp.ones((N,), jnp.float32), 'c_ln_w': jnp.ones((N,), jnp.float32), 'Wdt': jax.random.normal(ks[5], (D, R), jnp.float32) * s, 'dt_bias': jax.random.normal(ks[6], (D,), jnp.float32) * s, 'A': -jnp.exp(jax.random.normal(ks[7], (D, N), jnp.float32) * 0.5), 'D_param': jnp.ones((D,), jnp.float32), 'W_out': jax.random.normal(ks[8], (H, D), jnp.float32) * s}
    _L0_attn_all = _L0_attn_setup()
    _L0_attn_in = {k: v for k, v in _L0_attn_all.items() if k in ('W_in', 'conv_w', 'conv_b', 'Wx', 'dt_ln_w', 'b_ln_w', 'c_ln_w', 'Wdt', 'dt_bias', 'A', 'D_param', 'W_out')}
    del _L0_attn_all

    def _L0_ffn_setup():
        import jax, jax.numpy as jnp
        import numpy as np
        NUM_EXPERTS = 8
        TOP_K = 2
        RANK = 16
        LORA_ALPHA = 32
        SCALING = LORA_ALPHA / RANK
        key = jax.random.key(seed)
        ks = jax.random.split(key, 6)
        B, S, D_IN, D_OUT = (4, 512, 1024, 1024)
        x = jax.random.normal(ks[0], (B, S, D_IN), dtype=jnp.float32)
        W_base = jax.random.normal(ks[1], (D_OUT, D_IN), dtype=jnp.float32) * 0.02
        b_base = jax.random.normal(ks[2], (D_OUT,), dtype=jnp.float32) * 0.02
        W_router = jax.random.normal(ks[3], (NUM_EXPERTS, D_IN), dtype=jnp.float32) * 0.02
        A = jax.random.normal(ks[4], (NUM_EXPERTS, RANK, D_IN), dtype=jnp.float32) * 0.02
        Bm = jax.random.normal(ks[5], (D_OUT, RANK), dtype=jnp.float32) * 0.02
        Bm = jnp.broadcast_to(Bm, (NUM_EXPERTS, D_OUT, RANK)) * jnp.arange(1, NUM_EXPERTS + 1, dtype=jnp.float32)[:, None, None] * 0.2
        return {'x': x, 'W_base': W_base, 'b_base': b_base, 'W_router': W_router, 'A': A, 'B': Bm}
    _L0_ffn_all = _L0_ffn_setup()
    _L0_ffn_in = {k: v for k, v in _L0_ffn_all.items() if k in ('W_base', 'b_base', 'W_router', 'A', 'B')}
    del _L0_ffn_all

    def _L1_xattn_setup():
        import jax, jax.numpy as jnp
        import numpy as np
        TEXT_DIM = 1024
        FEATURE_DIM = 1024

        def _xavier_uniform(key, shape):
            fan_in, fan_out = (shape[1], shape[0])
            limit = float(np.sqrt(6.0 / (fan_in + fan_out)))
            return jax.random.uniform(key, shape, jnp.float32, -limit, limit)
        key = jax.random.key(seed)
        k1, k2, k3, k4 = jax.random.split(key, 4)
        text = jax.random.normal(k1, (8, 512, TEXT_DIM), jnp.float32)
        features = jax.random.normal(k2, (8, 144, FEATURE_DIM), jnp.float32)
        Wq = _xavier_uniform(k3, (FEATURE_DIM, TEXT_DIM))
        bq = jnp.zeros((FEATURE_DIM,), jnp.float32)
        Wk = _xavier_uniform(k4, (FEATURE_DIM, FEATURE_DIM))
        bk = jnp.zeros((FEATURE_DIM,), jnp.float32)
        return {'text': text, 'features': features, 'Wq': Wq, 'bq': bq, 'Wk': Wk, 'bk': bk}
    _L1_xattn_all = _L1_xattn_setup()
    _L1_xattn_in = {k: v for k, v in _L1_xattn_all.items() if k in ('Wq', 'bq', 'Wk', 'bk')}
    del _L1_xattn_all

    def _L1_attn_setup():
        import jax, jax.numpy as jnp
        import numpy as np
        DIM = 1024
        NUM_HEAD = 32
        NUM_KV_HEAD = 8
        ROPE_THETA = 10000.0
        B, T = (2, 512)

        def apply_rope(x, start_pos=0, theta=ROPE_THETA):
            d = x.shape[-1]
            half = d // 2
            inv_freq = 1.0 / theta ** (jnp.arange(0, half, dtype=jnp.float32) / half)
            pos = jnp.arange(x.shape[1], dtype=jnp.float32) + start_pos
            ang = pos[:, None] * inv_freq[None, :]
            cos = jnp.cos(ang)[None, :, None, :]
            sin = jnp.sin(ang)[None, :, None, :]
            x1, x2 = (x[..., :half], x[..., half:])
            return jnp.concatenate([x1 * cos - x2 * sin, x1 * sin + x2 * cos], axis=-1)
        key = jax.random.key(seed)
        ks = jax.random.split(key, 5)
        scale = 0.02
        X = jax.random.normal(ks[0], (B, T, DIM), dtype=jnp.float32)
        Wq = jax.random.normal(ks[1], (DIM, DIM), dtype=jnp.float32) * scale
        Wk = jax.random.normal(ks[2], (DIM, DIM // NUM_HEAD * NUM_KV_HEAD), dtype=jnp.float32) * scale
        Wv = jax.random.normal(ks[3], (DIM, DIM // NUM_HEAD * NUM_KV_HEAD), dtype=jnp.float32) * scale
        Wo = jax.random.normal(ks[4], (DIM, DIM), dtype=jnp.float32) * scale
        return {'X': X, 'Wq': Wq, 'Wk': Wk, 'Wv': Wv, 'Wo': Wo}
    _L1_attn_all = _L1_attn_setup()
    _L1_attn_in = {k: v for k, v in _L1_attn_all.items() if k in ('Wq', 'Wk', 'Wv', 'Wo')}
    del _L1_attn_all

    def _L1_ffn_setup():
        import jax, jax.numpy as jnp
        import numpy as np
        B, L, H, Dh, M = (4, 512, 16, 64, 256)
        D = H * Dh
        key = jax.random.key(seed)
        kx, ku, kd, kp = jax.random.split(key, 4)
        x = jax.random.normal(kx, (B, L, D), dtype=jnp.float32)
        up = jax.random.normal(ku, (H, Dh, M), dtype=jnp.float32)
        down = jax.random.normal(kd, (H, M, Dh), dtype=jnp.float32)
        perm = jax.random.permutation(kp, D)
        return {'x': x, 'up': up, 'down': down, 'perm': perm}
    _L1_ffn_all = _L1_ffn_setup()
    _L1_ffn_in = {k: v for k, v in _L1_ffn_all.items() if k in ('up', 'down', 'perm')}
    del _L1_ffn_all
    return {'x': x, 'ctx_4096': ctx_4096, 'L0_xattn_x1_scale': _L0_xattn_in['x1_scale'], 'L0_xattn_x1_zp': _L0_xattn_in['x1_zp'], 'L0_xattn_x2_scale': _L0_xattn_in['x2_scale'], 'L0_xattn_x2_zp': _L0_xattn_in['x2_zp'], 'L0_attn_W_in': _L0_attn_in['W_in'], 'L0_attn_conv_w': _L0_attn_in['conv_w'], 'L0_attn_conv_b': _L0_attn_in['conv_b'], 'L0_attn_Wx': _L0_attn_in['Wx'], 'L0_attn_dt_ln_w': _L0_attn_in['dt_ln_w'], 'L0_attn_b_ln_w': _L0_attn_in['b_ln_w'], 'L0_attn_c_ln_w': _L0_attn_in['c_ln_w'], 'L0_attn_Wdt': _L0_attn_in['Wdt'], 'L0_attn_dt_bias': _L0_attn_in['dt_bias'], 'L0_attn_A': _L0_attn_in['A'], 'L0_attn_D_param': _L0_attn_in['D_param'], 'L0_attn_W_out': _L0_attn_in['W_out'], 'L0_ffn_W_base': _L0_ffn_in['W_base'], 'L0_ffn_b_base': _L0_ffn_in['b_base'], 'L0_ffn_W_router': _L0_ffn_in['W_router'], 'L0_ffn_A': _L0_ffn_in['A'], 'L0_ffn_B': _L0_ffn_in['B'], 'L1_xattn_Wq': _L1_xattn_in['Wq'], 'L1_xattn_bq': _L1_xattn_in['bq'], 'L1_xattn_Wk': _L1_xattn_in['Wk'], 'L1_xattn_bk': _L1_xattn_in['bk'], 'L1_attn_Wq': _L1_attn_in['Wq'], 'L1_attn_Wk': _L1_attn_in['Wk'], 'L1_attn_Wv': _L1_attn_in['Wv'], 'L1_attn_Wo': _L1_attn_in['Wo'], 'L1_ffn_up': _L1_ffn_in['up'], 'L1_ffn_down': _L1_ffn_in['down'], 'L1_ffn_perm': _L1_ffn_in['perm']}

def reference(x, ctx_4096, L0_xattn_x1_scale, L0_xattn_x1_zp, L0_xattn_x2_scale, L0_xattn_x2_zp, L0_attn_W_in, L0_attn_conv_w, L0_attn_conv_b, L0_attn_Wx, L0_attn_dt_ln_w, L0_attn_b_ln_w, L0_attn_c_ln_w, L0_attn_Wdt, L0_attn_dt_bias, L0_attn_A, L0_attn_D_param, L0_attn_W_out, L0_ffn_W_base, L0_ffn_b_base, L0_ffn_W_router, L0_ffn_A, L0_ffn_B, L1_xattn_Wq, L1_xattn_bq, L1_xattn_Wk, L1_xattn_bk, L1_attn_Wq, L1_attn_Wk, L1_attn_Wv, L1_attn_Wo, L1_ffn_up, L1_ffn_down, L1_ffn_perm):
    import jax
    import jax.numpy as jnp

    def _L0_xattn_ref(x1, x2, x1_scale, x1_zp, x2_scale, x2_zp):
        import jax, jax.numpy as jnp
        import numpy as np
        QMIN = 0.0
        QMAX = 255.0

        def fake_quant(x, scale, zp):
            s = scale.reshape(())
            z = zp.reshape(())
            q = jnp.clip(jnp.round(x / s + z), QMIN, QMAX)
            return (q - z) * s
        q1 = fake_quant(x1, x1_scale, x1_zp)
        q2 = fake_quant(x2, x2_scale, x2_zp)
        return jnp.matmul(q1, q2)

    def _L0_attn_ref(hidden_states, W_in, conv_w, conv_b, Wx, dt_ln_w, b_ln_w, c_ln_w, Wdt, dt_bias, A, D_param, W_out):
        import jax, jax.numpy as jnp
        import numpy as np
        H = 1024
        D = 2048
        N = 16
        K = 4
        R = 64
        BATCH = 1
        L = 512
        EPS = 1e-06

        def _rmsnorm(x, w):
            return x * jax.lax.rsqrt(jnp.mean(x * x, axis=-1, keepdims=True) + EPS) * w
        proj = hidden_states @ W_in.T
        u, gate = jnp.split(proj, 2, axis=-1)
        x = jnp.transpose(u, (0, 2, 1))
        x = jax.lax.conv_general_dilated(x, conv_w[:, None, :], window_strides=(1,), padding=[(K - 1, 0)], dimension_numbers=('NCH', 'OIH', 'NCH'), feature_group_count=D)
        u = jax.nn.silu(jnp.transpose(x, (0, 2, 1)) + conv_b)
        ssm_p = u @ Wx.T
        dt, Bm, Cm = jnp.split(ssm_p, [R, R + N], axis=-1)
        dt = _rmsnorm(dt, dt_ln_w)
        Bm = _rmsnorm(Bm, b_ln_w)
        Cm = _rmsnorm(Cm, c_ln_w)
        delta = jax.nn.softplus(dt @ Wdt.T + dt_bias)

        def step(state, xs):
            d_t, B_t, C_t, u_t = xs
            dA = jnp.exp(d_t[..., None] * A)
            state = dA * state + (d_t * u_t)[..., None] * B_t[:, None, :]
            y_t = jnp.einsum('bdn,bn->bd', state, C_t)
            return (state, y_t)
        init = jnp.zeros((hidden_states.shape[0], D, N), hidden_states.dtype)
        xs = (jnp.swapaxes(delta, 0, 1), jnp.swapaxes(Bm, 0, 1), jnp.swapaxes(Cm, 0, 1), jnp.swapaxes(u, 0, 1))
        _, ys = jax.lax.scan(step, init, xs)
        y = jnp.swapaxes(ys, 0, 1) + u * D_param
        y = y * jax.nn.silu(gate)
        return y @ W_out.T

    def _L0_ffn_ref(x, W_base, b_base, W_router, A, B):
        import jax, jax.numpy as jnp
        import numpy as np
        NUM_EXPERTS = 8
        TOP_K = 2
        RANK = 16
        LORA_ALPHA = 32
        SCALING = LORA_ALPHA / RANK
        bs, seq, d_in = x.shape
        T = bs * seq
        xf = x.reshape(T, d_in)
        base = xf @ W_base.T + b_base
        logits = xf @ W_router.T
        rw, sel = jax.lax.top_k(logits, TOP_K)
        rw = jax.nn.softmax(rw, axis=-1)
        onehot = jax.nn.one_hot(sel, NUM_EXPERTS, dtype=rw.dtype)
        w = jnp.einsum('tk,tke->te', rw, onehot)
        h = jnp.einsum('td,erd->ter', xf, A)
        lora = jnp.einsum('ter,te,eor->to', h, w, B) * SCALING
        return (base + lora).reshape(bs, seq, -1)

    def _L1_xattn_ref(text, features, Wq, bq, Wk, bk):
        import jax, jax.numpy as jnp
        import numpy as np
        TEXT_DIM = 1024
        FEATURE_DIM = 1024

        def _xavier_uniform(key, shape):
            fan_in, fan_out = (shape[1], shape[0])
            limit = float(np.sqrt(6.0 / (fan_in + fan_out)))
            return jax.random.uniform(key, shape, jnp.float32, -limit, limit)
        Q = jnp.einsum('btx,dx->btd', text, Wq) + bq
        K = jnp.einsum('bpx,dx->bpd', features, Wk) + bk
        scale = 1.0 / jnp.sqrt(jnp.asarray(K.shape[-1], K.dtype))
        scores = jnp.einsum('btd,bpd->btp', Q, K) * scale
        attn = jax.nn.softmax(scores, axis=-1)
        attended = jnp.einsum('btp,bpd->btd', attn, features)
        return attended

    def _L1_attn_ref(X, Wq, Wk, Wv, Wo):
        import jax, jax.numpy as jnp
        import numpy as np
        DIM = 1024
        NUM_HEAD = 32
        NUM_KV_HEAD = 8
        ROPE_THETA = 10000.0
        B, T = (2, 512)

        def apply_rope(x, start_pos=0, theta=ROPE_THETA):
            d = x.shape[-1]
            half = d // 2
            inv_freq = 1.0 / theta ** (jnp.arange(0, half, dtype=jnp.float32) / half)
            pos = jnp.arange(x.shape[1], dtype=jnp.float32) + start_pos
            ang = pos[:, None] * inv_freq[None, :]
            cos = jnp.cos(ang)[None, :, None, :]
            sin = jnp.sin(ang)[None, :, None, :]
            x1, x2 = (x[..., :half], x[..., half:])
            return jnp.concatenate([x1 * cos - x2 * sin, x1 * sin + x2 * cos], axis=-1)
        Bs, Ts, C = X.shape
        H, Hkv = (NUM_HEAD, NUM_KV_HEAD)
        dh = C // H
        G = H // Hkv
        Q = apply_rope((X @ Wq).reshape(Bs, Ts, H, dh))
        K = apply_rope((X @ Wk).reshape(Bs, Ts, Hkv, dh))
        V = (X @ Wv).reshape(Bs, Ts, Hkv, dh)
        Qh = Q.transpose(0, 2, 1, 3).reshape(Bs, Hkv, G, Ts, dh)
        Kh = K.transpose(0, 2, 1, 3)
        Vh = V.transpose(0, 2, 1, 3)
        scores = jnp.einsum('bkgtd,bksd->bkgts', Qh, Kh) / jnp.sqrt(jnp.float32(dh))
        causal = jnp.tril(jnp.ones((Ts, Ts), dtype=bool))
        scores = jnp.where(causal[None, None, None], scores, -jnp.inf)
        attn = jax.nn.softmax(scores, axis=-1)
        out = jnp.einsum('bkgts,bksd->bkgtd', attn, Vh)
        out = out.reshape(Bs, H, Ts, dh).transpose(0, 2, 1, 3).reshape(Bs, Ts, C)
        return out @ Wo

    def _L1_ffn_ref(x, up, down, perm):
        import jax, jax.numpy as jnp
        import numpy as np
        B, L, H, Dh, M = (4, 512, 16, 64, 256)
        D = H * Dh
        b, l, Dm = x.shape
        h, d = (up.shape[0], up.shape[1])
        unperm = jnp.argsort(perm)
        t = x.reshape(b * l, Dm)
        t = t[:, perm]
        t = t.reshape(b * l, h, d)
        t = jnp.einsum('bhd,hdm->bhm', t, up)
        t = jax.nn.gelu(t, approximate=False)
        t = jnp.einsum('bhm,hmd->bhd', t, down)
        t = t.reshape(b * l, h * d)
        t = t[:, unperm]
        out = t.reshape(b, l, Dm)
        return out
    x = x + _L0_xattn_ref(_layernorm(x, axis=-1), ctx_4096, L0_xattn_x1_scale, L0_xattn_x1_zp, L0_xattn_x2_scale, L0_xattn_x2_zp)
    x = x + _L0_attn_ref(_layernorm(x, axis=-1), L0_attn_W_in, L0_attn_conv_w, L0_attn_conv_b, L0_attn_Wx, L0_attn_dt_ln_w, L0_attn_b_ln_w, L0_attn_c_ln_w, L0_attn_Wdt, L0_attn_dt_bias, L0_attn_A, L0_attn_D_param, L0_attn_W_out)
    x = x + _L0_ffn_ref(_layernorm(x, axis=-1), L0_ffn_W_base, L0_ffn_b_base, L0_ffn_W_router, L0_ffn_A, L0_ffn_B)
    x = x + _L1_xattn_ref(_layernorm(x, axis=-1), ctx_4096, L1_xattn_Wq, L1_xattn_bq, L1_xattn_Wk, L1_xattn_bk)
    x = x + _L1_attn_ref(_layernorm(x, axis=-1), L1_attn_Wq, L1_attn_Wk, L1_attn_Wv, L1_attn_Wo)
    x = x + _L1_ffn_ref(_layernorm(x, axis=-1), L1_ffn_up, L1_ffn_down, L1_ffn_perm)
    return x

_drawn_inputs = setup_inputs


def setup_inputs(seed=0):
    import zlib

    import numpy as np

    out = dict(_drawn_inputs(seed))
    spreads = {'L0_attn_dt_ln_w': (1.0, 0.6),
     'L0_attn_b_ln_w': (1.0, 0.6),
     'L0_attn_c_ln_w': (1.0, 0.6),
     'L0_attn_D_param': (1.0, 0.6),
     'L1_xattn_bq': (0.0, 2.0),
     'L1_xattn_bk': (0.0, 2.0)}
    factors = {'L0_attn_W_in': 8.0,
     'L0_attn_conv_w': 8.0,
     'L0_attn_conv_b': 8.0,
     'L0_attn_Wx': 8.0,
     'L0_attn_Wdt': 8.0,
     'L0_attn_dt_bias': 8.0,
     'L0_attn_A': 8.0,
     'L0_attn_W_out': 8.0,
     'L0_ffn_b_base': 200.0,
     'L0_ffn_W_router': 8.0,
     'L0_ffn_A': 8.0,
     'L0_ffn_B': 8.0,
     'L1_xattn_Wq': 199.61,
     'L1_xattn_Wk': 184.862,
     'L1_attn_Wq': 8.0,
     'L1_attn_Wk': 8.0,
     'L1_attn_Wv': 8.0,
     'L1_attn_Wo': 8.0,
     'L0_ffn_W_base': 7.01}
    for name, (base, spread) in spreads.items():
        noise = np.random.default_rng([zlib.crc32(name.encode()), seed]).standard_normal(out[name].shape)
        drawn = base * np.exp(spread * noise) if base else spread * noise
        out[name] = jnp.asarray(drawn.astype(out[name].dtype))
    for name, factor in factors.items():
        out[name] = (out[name] * factor).astype(out[name].dtype)
    return out
```

```python
from contextlib import ExitStack

import concourse.bass as bass
from concourse import mybir

ALU = mybir.AluOpType
ACT = mybir.ActivationFunctionType
AX = mybir.AxisListType.X
F32 = mybir.dt.float32
BF16 = mybir.dt.bfloat16
I32 = mybir.dt.int32

P = 128
B, L = 2, 64
D = 1024
KT = D // P
UK = 4
UN = 512
UNIT = UK * UN
SLOTS = 8
LN_EPS = 1e-5

DI = 2048
DT = DI // P
NS = 16
R = 64
CK = 4
NB = 2 * DI // UN
SSM = R + 2 * NS
RMS_EPS = 1e-6
GD = UN // P
NG = DT // GD
HN = NS // 2
STEPS = 2 * DT
SIG_MIN = -40.0

NE, RANK = 8, 16
LORA_SCALE = 2.0

XSCALE = 1.0 / 32.0
H, HKV, DH = 32, 8, 32
GQ = H // HKV
ASCALE = float(DH) ** -0.5
MH, MD, MM = 16, 64, 256

ROUND = 1.5 * 2.0 ** 23
QMAX = 255.0
QMID = 128.0


def unit_list():
    units = [("ctx", i) for i in range(8)]
    units += [("w_in", i) for i in range(16)]
    units += [("w_out", i) for i in range(8)]
    units += [("w_base", i) for i in range(4)]
    units += [("x_wq", i) for i in range(4)]
    units += [("x_wk", i) for i in range(4)]
    units += [("ctx_t", i) for i in range(8)]
    units += [("ctx", i) for i in range(8)]
    units += [("a_wkv", i) for i in range(2)]
    units += [("a_wq", i) for i in range(4)]
    units += [("a_wo", i) for i in range(4)]
    units += [("mlp_up", 0), ("mlp_down", 0)]
    return units


def perceiver(nc, dram, out):
    units = unit_list()
    first = {}
    for n, (name, i) in enumerate(units):
        if name == "ctx" and n >= 8:
            name = "ctx_again"
        first.setdefault(name, n)

    with ExitStack() as stack:
        def sb(name, shape, dtype=F32):
            return stack.enter_context(nc.sbuf_tensor(name, shape, dtype))

        def sem(name):
            return stack.enter_context(nc.semaphore(name))

        ring = sb("ring", [P, SLOTS, UNIT])
        x = sb("x", [P, D])
        h = sb("h", [P, D])
        hT = sb("hT", [P, KT, P])
        ident = sb("ident", [P, P])
        small = sb("small", [P, 640])
        arena = sb("arena", [P, 32640])
        psum = stack.enter_context(nc.psum_tensor("psum", [P, 8, 512], F32))

        def carve(tile, start, *dims):
            size = 1
            for d in dims:
                size *= d
            ap = tile[:, start:start + size]
            if len(dims) == 2:
                ap = ap.rearrange("p (a b) -> p a b", a=dims[0])
            if len(dims) == 3:
                ap = ap.rearrange("p (a b c) -> p a b c", a=dims[0], b=dims[1])
            return ap

        quant = carve(small, 0, 4)
        qrec = carve(small, 4, 2)
        qneg = carve(small, 6, 2)
        zrest = carve(small, 8, 2)
        zpart = small[:, 10:12].bitcast(BF16)
        q_sum = carve(small, 12, 1)
        q_row = carve(small, 13, 1)
        q_s12 = carve(small, 14, 1)
        var_eps = carve(small, 15, 1)
        rstd = carve(small, 16, 1)
        minus_half = carve(small, 17, 4)
        stats = carve(small, 24, 2, 6)
        mv = carve(small, 36, 2)
        rms_sum = carve(small, 40, 3)
        rms_var = carve(small, 43, 3)
        rms_inv = carve(small, 46, 3)
        top = carve(small, 50, 1)
        den = carve(small, 51, 1)
        den_inv = carve(small, 52, 1)
        logit = carve(small, 56, NE)
        rank = carve(small, 64, NE)
        gate = carve(small, 72, NE)
        qbias = carve(small, 80, 1)
        smax2 = carve(small, 81, 2)
        smax = carve(small, 83, 1)
        sbias = carve(small, 84, 1)
        ssum2 = carve(small, 85, 2)
        ssum = carve(small, 87, 1)
        sinv = carve(small, 88, 1)
        hmax = carve(small, 96, GQ, HKV)
        oinv = carve(small, 128, 4, HKV)
        cosf = carve(small, 160, DH)
        sinf = carve(small, 192, DH)
        mask = carve(small, 224, L)
        row_no = carve(small, 288, KT)
        perm_col = carve(small, 296, KT)
        perm_coli = small[:, 304:304 + KT].bitcast(I32)
        conv_w = carve(small, 320, DT, CK)
        conv_b = carve(small, 384, DT)
        dt_b = carve(small, 400, DT)
        d_par = carve(small, 416, DT)
        rms_w = carve(small, 432, SSM)
        tri = carve(small, 528, NE, NE)

        q2 = arena[:, 0:8192].bitcast(BF16).rearrange("p (u n) -> p u n", u=8)
        q1T = arena[:, 8192:8704].bitcast(BF16).rearrange("p (k t) -> p k t", k=KT)
        zneg = arena[:, 8704:8800].bitcast(BF16).rearrange("p (j t) -> p j t", j=3)
        ones64 = arena[:, 8800:8832].bitcast(BF16)
        uT = arena[:, 0:DT * B * (L + 3)].rearrange("p (k b t) -> p k b t", k=DT, b=B)
        uc = carve(arena, 2144, DT, P)
        delta = carve(arena, 4192, DT, P)
        duT = carve(arena, 6240, DI)
        sg = carve(arena, 8288, DT, P)
        bdiag = carve(arena, 10336, NS, P)
        cwide = carve(arena, 12384, NS * P)
        dA = carve(arena, 14432, 3, HN * P)
        cdiag = carve(arena, 14432, NS, P)
        state = carve(arena, 17504, 3, HN * P)
        pairs = carve(arena, 20576, 3, HN * P // 2)
        proj = carve(arena, 22112, 4, UN)
        sig = carve(arena, 24160, 2, UN)
        zbuf = carve(arena, 30464, NG, UN)
        wxT = carve(arena, 26208, DT, SSM)
        wdtT = carve(arena, 27744, DI)
        a_par = carve(arena, 29792, DT, NS)
        ssm = carve(arena, 30048, SSM)
        rms_junk = carve(arena, 30144, R)
        dtT = carve(arena, 30208, P)
        ones = carve(arena, 30336, P)
        b_base = carve(arena, 10336, D)
        bq = carve(arena, 11360, D)
        bk = carve(arena, 12384, D)
        w_ar = carve(arena, 13408, KT, NE * RANK + NE)
        lora_b = carve(arena, 14496, D)
        lora_g = carve(arena, 15520, NE, RANK)
        lora_gT = carve(arena, 15648, P)
        above = carve(arena, 15776, NE, NE)
        ties = carve(arena, 15840, NE, NE)
        xq = carve(arena, 0, D)
        xqT = carve(arena, 1024, KT, P)
        xk = carve(arena, 2048, D)
        xkT = carve(arena, 3072, KT, P)
        prob = carve(arena, 4096, D)
        probT = carve(arena, 5120, KT, P)
        junk = carve(arena, 6144, D)
        rope_c = carve(arena, 0, D)
        rope_s = carve(arena, 1024, D)
        qrot = carve(arena, 2048, D)
        krot = carve(arena, 3072, HKV * DH)
        krep = carve(arena, 3328, HKV, GQ, DH)
        aqT = carve(arena, 4352, KT, P)
        akT = carve(arena, 5376, KT, P)
        vdup = carve(arena, 6400, B, HKV * (DH + 1))
        aprob = carve(arena, 6928, GQ, HKV, L)
        aprobT = carve(arena, 8976 - 8976, 2 * KT, P)
        attn = carve(arena, 2048, D)
        attnT = carve(arena, 3072, KT, P)
        permi = arena[:, 9312:10336].bitcast(I32)
        perm_row = carve(arena, 9312, D)
        iota = carve(arena, 15904 - 5568, D)
        pick = carve(arena, 16256, KT, D)
        place = carve(arena, 24448, KT, D)
        gT = carve(arena, 0, KT, P)
        hidden = carve(arena, 1024, MH, 2, P)
        oT = carve(arena, 5120, KT, P)
        y_out = carve(arena, 6144, D)

        unit_in = [sem(f"unit_in{s}") for s in range(SLOTS)]
        x_in = sem("x_in")
        quant_in = sem("quant_in")
        tables_in = sem("tables_in")
        tri_in = sem("tri_in")
        mamba_in = sem("mamba_in")
        mix_in = sem("mix_in")
        perm_in = sem("perm_in")
        vdup_in = sem("vdup_in")
        out_done = sem("out_done")
        ctx_coded = sem("ctx_coded")
        unit_used = sem("unit_used")
        const_zero = sem("const_zero")
        const_ready = sem("const_ready")
        var_ready = sem("var_ready")
        rstd_ready = sem("rstd_ready")
        h_ready = sem("h_ready")
        hT_psum = sem("hT_psum")
        hT_lo = sem("hT_lo")
        hT_hi = sem("hT_hi")
        x_ready = sem("x_ready")
        dve_step = sem("dve_step")
        act_step = sem("act_step")
        scales_ready = sem("scales_ready")
        ctx_scaled = sem("ctx_scaled")
        q1_ready = sem("q1_ready")
        q1_psum = sem("q1_psum")
        q1T_ready = sem("q1T_ready")
        z_ready = sem("z_ready")
        q_done = sem("q_done")
        edge_zero = sem("edge_zero")
        proj_psum = sem("proj_psum")
        proj_sb = sem("proj_sb")
        projT_psum = sem("projT_psum")
        projT_read = sem("projT_read")
        sig_in = sem("sig_in")
        sig_out = sem("sig_out")
        gated = sem("gated")
        ssm_psum = sem("ssm_psum")
        ssm_sum = sem("ssm_sum")
        ssm_inv = sem("ssm_inv")
        dt_normed = sem("dt_normed")
        bc_ready = sem("bc_ready")
        dtT_psum = sem("dtT_psum")
        dtT_ready = sem("dtT_ready")
        z_psum = sem("z_psum")
        z_read = sem("z_read")
        z_abs = sem("z_abs")
        softlog = sem("softlog")
        delta_ready = sem("delta_ready")
        du_ready = sem("du_ready")
        duT_psum = sem("duT_psum")
        duT_ready = sem("duT_ready")
        bdiag_ready = sem("bdiag_ready")
        cdiag_ready = sem("cdiag_ready")
        c_psum = sem("c_psum")
        c_ready = sem("c_ready")
        dbu_ready = sem("dbu_ready")
        dA_ready = sem("dA_ready")
        scan_done = sem("scan_done")
        prod_ready = sem("prod_ready")
        pairs_ready = sem("pairs_ready")
        reduced = sem("reduced")
        yg_ready = sem("yg_ready")
        y_psum = sem("y_psum")
        ar_psum = sem("ar_psum")
        top_ready = sem("top_ready")
        exp_ready = sem("exp_ready")
        g_ready = sem("g_ready")
        gT_psum = sem("gT_psum")
        gT_ready = sem("gT_ready")
        biased = sem("biased")
        base_psum = sem("base_psum")
        xq_psum = sem("xq_psum")
        xq_ready = sem("xq_ready")
        xqT_psum = sem("xqT_psum")
        xqT_lo = sem("xqT_lo")
        xqT_hi = sem("xqT_hi")
        xk_psum = sem("xk_psum")
        xk_lo = sem("xk_lo")
        xk_hi = sem("xk_hi")
        xkT_psum = sem("xkT_psum")
        xkT_lo = sem("xkT_lo")
        xkT_hi = sem("xkT_hi")
        score_psum = sem("score_psum")
        sbias_ready = sem("sbias_ready")
        prob_ready = sem("prob_ready")
        probT_psum = sem("probT_psum")
        probT_lo = sem("probT_lo")
        probT_hi = sem("probT_hi")
        xatt_psum = sem("xatt_psum")
        kv_psum = sem("kv_psum")
        aq_psum = sem("aq_psum")
        krot_ready = sem("krot_ready")
        krep_ready = sem("krep_ready")
        v_ready = sem("v_ready")
        akT_psum = sem("akT_psum")
        akT_ready = sem("akT_ready")
        qrot_ready = sem("qrot_ready")
        aqT_psum = sem("aqT_psum")
        aqT_ready = sem("aqT_ready")
        as_psum = sem("as_psum")
        as_ready = sem("as_ready")
        ap_ready = sem("ap_ready")
        apT_psum = sem("apT_psum")
        apT_ready = sem("apT_ready")
        pv_psum = sem("pv_psum")
        attn_ready = sem("attn_ready")
        attnT_psum = sem("attnT_psum")
        attnT_ready = sem("attnT_ready")
        ao_psum = sem("ao_psum")
        perm_f = sem("perm_f")
        iota_ready = sem("iota_ready")
        pick_ready = sem("pick_ready")
        place_ready = sem("place_ready")
        g_psum = sem("g_psum")
        g_sb = sem("g_sb")
        up_psum = sem("up_psum")
        hidden_ready = sem("hidden_ready")
        down_psum = sem("down_psum")
        oT_ready = sem("oT_ready")
        placed = sem("placed")

        last_use = [(ctx_coded, n + 1) for n in range(8)]
        middle = 0

        def uses(*signals):
            nonlocal middle
            for signal in signals:
                if signal is None:
                    middle += 1
                    last_use.append((unit_used, middle))
                else:
                    last_use.append(signal)

        for j in range(NB):
            uses(None, (proj_psum, j + 1))
        for nh in range(2):
            uses(None, None, None, (y_psum, nh + 1))
        uses(None, None, None, None)
        for signal in (xq_psum, xk_psum):
            uses(None, (signal, 1), None, (signal, 2))
        for signal in (score_psum, xatt_psum):
            for nh in range(2):
                uses(None)
                last_use.append(last_use[-1])
                uses((signal, nh + 1), (signal, nh + 1))
        uses(None, (kv_psum, 1))
        for signal in (aq_psum, ao_psum):
            uses(None, (signal, 1), None, (signal, 2))

        def slot(n):
            return ring[:, n % SLOTS, :].rearrange("p (k n) -> p k n", k=UK)

        def arrived(eng, n):
            eng.wait_ge(unit_in[n % SLOTS], 16 * (n // SLOTS + 1))

        def wide(ap, count):
            n = ap.shape[1]
            return ap.rearrange("p (u n) -> p u n", u=1).to_broadcast([P, count, n])

        def along(ap, count):
            n = ap.shape[1]
            return ap.rearrange("p (n u) -> p n u", u=1).to_broadcast([P, n, count])

        block = stack.enter_context(nc.Block())

        @block.sync
        def _(sp):
            sp.dma_start(x[:, :], dram["x"]).then_inc(x_in, 16)
            for n, (name, i) in enumerate(units):
                if n >= SLOTS:
                    sp.wait_ge(*last_use[n - SLOTS])
                sp.dma_start(ring[:, n % SLOTS, :], dram[name][i]).then_inc(unit_in[n % SLOTS], 16)
            for nh in range(2):
                sp.wait_ge(x_ready, 12 + nh - 1)
                cols = slice(nh * UN, nh * UN + UN)
                sp.dma_start(out[:, cols], y_out[:, cols]).then_inc(out_done, 16)
            sp.wait_ge(out_done, 32)

        @block.gpsimd
        def _(pool):
            pool.dma_start(quant, dram["quant"].to_broadcast([P, 4])).then_inc(quant_in, 16)
            pool.dma_start(small[:, 160:304], dram["tables"]).then_inc(tables_in, 16)
            pool.memset(ident[:, :], 0.0).then_inc(const_zero, 1)
            pool.memset(minus_half, -0.5).then_inc(const_ready, 1)
            pool.memset(ones64, 1.0).then_inc(const_ready, 1)
            pool.wait_ge(const_zero, 1)
            pool.affine_select(out=ident[:, :], in_=ident[:, :], compare_op=ALU.not_equal, fill=1.0, base=0,
                               pattern=[[-1, P]], channel_multiplier=1).then_inc(const_ready, 1)

            def rstd_of(n):
                pool.wait_ge(var_ready, n + 1)
                pool.tensor_tensor(rstd, var_eps, minus_half[:, 0:1], ALU.pow).then_inc(rstd_ready, 1)

            pool.wait_ge(const_ready, 3)
            rstd_of(0)
            pool.dma_start(wxT, dram["wx"]).then_inc(mamba_in, 16)
            pool.dma_start(wdtT[0:R, :], dram["wdt"]).then_inc(mamba_in, 16)
            pool.dma_start(a_par, dram["a_par"]).then_inc(mamba_in, 16)
            pool.dma_start(small[:, 320:432], dram["chan"]).then_inc(mamba_in, 16)
            pool.dma_start(rms_w, dram["rms_w"].to_broadcast([P, SSM])).then_inc(mamba_in, 16)
            pool.memset(ones, 1.0).then_inc(const_ready, 1)
            rstd_of(1)
            pool.wait_ge(q_done, 2)
            pool.memset(uT[:, :, :, 0:CK - 1], 0.0).then_inc(edge_zero, 1)

            pool.wait_ge(ssm_sum, 1)
            pool.tensor_tensor(rms_inv, rms_var, minus_half[:, 0:3], ALU.pow).then_inc(ssm_inv, 1)
            pool.wait_ge(bc_ready, 2)
            pool.tensor_tensor(bdiag, wide(ident[:, :], NS), along(ssm[:, R:R + NS], P), ALU.mult).then_inc(bdiag_ready, 1)
            pool.tensor_tensor(cdiag, wide(ident[:, :], NS), along(ssm[:, R + NS:SSM], P), ALU.mult).then_inc(cdiag_ready, 1)
            pool.wait_ge(c_psum, 4)
            pool.memset(dA.rearrange("p s (n t) -> p (s n) t", t=L)[:, :, 0:1], 0.0).then_inc(edge_zero, 1)
            for s in range(STEPS):
                pool.wait_ge(prod_ready, s + 1)
                if s >= 3:
                    pool.wait_ge(reduced, s - 2)
                prod = state[:, s % 3, :]
                half = HN * P // 2
                pool.tensor_tensor(pairs[:, s % 3, :], prod[:, 0:half], prod[:, half:], ALU.add).then_inc(pairs_ready, 1)

            pool.wait_ge(reduced, STEPS)
            pool.dma_start(b_base, dram["b_base"].to_broadcast([P, D])).then_inc(mix_in, 16)
            pool.dma_start(w_ar, dram["w_ar"]).then_inc(mix_in, 16)
            pool.dma_start(lora_b, dram["lora_b"]).then_inc(mix_in, 16)
            pool.dma_start(bq, dram["bq"].to_broadcast([P, D])).then_inc(mix_in, 16)
            pool.dma_start(bk, dram["bk"].to_broadcast([P, D])).then_inc(mix_in, 16)
            rstd_of(2)
            pool.wait_ge(mix_in, 80)
            pool.wait_ge(h_ready, 6)
            pool.tensor_tensor(x[:, :], x[:, :], b_base, ALU.add).then_inc(biased, 1)
            rstd_of(3)
            pool.wait_ge(y_psum, 2)
            pool.dma_start(permi, dram["perm_row"].to_broadcast([P, D])).then_inc(perm_in, 16)
            pool.dma_start(perm_coli, dram["perm_col"]).then_inc(perm_in, 16)
            pool.iota(iota, pattern=[[1, D]], base=0, channel_multiplier=0,
                      allow_small_or_imprecise_dtypes=True).then_inc(iota_ready, 1)
            pool.wait_ge(perm_in, 32)
            pool.tensor_copy(perm_row, permi).then_inc(perm_f, 1)
            pool.tensor_copy(perm_col, perm_coli).then_inc(perm_f, 1)
            pool.wait_ge(perm_f, 2)
            pool.wait_ge(tables_in, 16)
            for k in range(KT):
                pool.tensor_scalar(pick[:, k, :], perm_row, row_no[:, k:k + 1], None, ALU.is_equal).then_inc(pick_ready, 1)
                if k == 3:
                    rstd_of(4)
            pool.wait_ge(iota_ready, 1)
            for k in range(KT):
                pool.tensor_scalar(place[:, k, :], iota, perm_col[:, k:k + 1], None, ALU.is_equal).then_inc(place_ready, 1)
            rstd_of(5)

        @block.scalar
        def _(act):
            steps = [0]

            def step(ins):
                steps[0] += 1
                ins.then_inc(act_step, 1)
                act.wait_ge(act_step, steps[0])

            act.dma_start(tri, dram["tri"]).then_inc(tri_in, 16)

            act.wait_ge(scales_ready, 1)
            for n in range(8):
                arrived(act, n)
                act.activation(ring[:, n % SLOTS, :], ring[:, n % SLOTS, :], ACT.Identity,
                               bias=quant[:, 3:4], scale=qrec[:, 1:2]).then_inc(ctx_scaled, 1)

            def evacuate_hT(n):
                act.wait_ge(hT_psum, 2 * n - 1)
                act.activation(hT[:, 0:4, :], psum[:, 6, :], ACT.Copy).then_inc(hT_lo, 1)

            evacuate_hT(1)

            def proj_copy(j):
                act.wait_ge(proj_psum, j + 1)
                if j >= 4:
                    act.wait_ge(projT_psum, j - 3)
                act.activation(proj[:, j % 4, :], psum[:, j % 3, :], ACT.Copy).then_inc(proj_sb, 1)

            def sigmoid(g):
                act.wait_ge(sig_in, g + 1)
                v = sig[:, g % 2, :]
                step(act.activation(v, v, ACT.Exp, scale=-1.0))
                step(act.activation(v, v, ACT.Ln, bias=1.0))
                act.activation(v, v, ACT.Exp, scale=-1.0).then_inc(sig_out, 1)

            def softplus_log(g):
                act.wait_ge(z_abs, g + 1)
                v = delta[:, GD * g:GD * g + GD, :]
                step(act.activation(v, v, ACT.Exp, scale=-1.0))
                act.activation(v, v, ACT.Ln, bias=1.0).then_inc(softlog, 1)

            def duT_copy(g):
                act.wait_ge(duT_psum, g + 1)
                act.activation(duT[:, UN * g:UN * g + UN], psum[:, 2 + 3 * (g % 2), :], ACT.Copy).then_inc(duT_ready, 1)

            def c_copy(c):
                act.wait_ge(c_psum, c + 1)
                act.activation(cwide[:, UN * c:UN * c + UN], psum[:, 6 + c % 2, :], ACT.Copy).then_inc(c_ready, 1)

            proj_copy(0)
            proj_copy(1)
            proj_copy(2)
            sigmoid(0)
            proj_copy(3)
            sigmoid(1)
            proj_copy(4)
            sigmoid(2)
            proj_copy(5)
            sigmoid(3)
            sigmoid(4)
            act.wait_ge(dtT_psum, 1)
            act.activation(dtT[0:R, :], psum[0:R, 5, 128:256], ACT.Copy).then_inc(dtT_ready, 1)
            proj_copy(6)
            for g in range(NG):
                softplus_log(g)
            sigmoid(5)
            proj_copy(7)
            c_copy(0)
            c_copy(1)
            for g in range(NG):
                duT_copy(g)
            sigmoid(6)
            c_copy(2)
            c_copy(3)
            act.wait_ge(edge_zero, 2)
            act.wait_ge(delta_ready, NG)
            for s in range(STEPS):
                if s >= 3:
                    act.wait_ge(scan_done, s - 2)
                if s == 2:
                    sigmoid(7)
                k = s // 2
                for n in range(HN):
                    to = dA[:, s % 3, n * P:n * P + P].rearrange("p (b t) -> p b t", b=B)[:, :, 1:]
                    of = delta[:, k, :].rearrange("p (b t) -> p b t", b=B)[:, :, 1:]
                    state_no = HN * (s % 2) + n
                    last = act.activation(to, of, ACT.Exp, scale=a_par[:, k, state_no:state_no + 1])
                last.then_inc(dA_ready, 1)

            evacuate_hT(2)
            act.wait_ge(top_ready, 1)
            act.activation(gate, logit, ACT.Exp, bias=top).then_inc(exp_ready, 1)
            act.wait_ge(gT_psum, 1)
            act.activation(lora_gT, psum[:, 3, 0:P], ACT.Copy).then_inc(gT_ready, 1)

            evacuate_hT(3)
            act.wait_ge(xqT_psum, 1)
            act.activation(xqT[:, 0:4, :], psum[:, 4, :], ACT.Copy).then_inc(xqT_lo, 1)
            act.wait_ge(xk_psum, 1)
            act.activation(xk[:, 0:UN], psum[:, 2, :], ACT.Copy).then_inc(xk_lo, 1)
            act.wait_ge(xkT_psum, 1)
            act.activation(xkT[:, 0:4, :], psum[:, 6, :], ACT.Copy).then_inc(xkT_lo, 1)
            act.wait_ge(sbias_ready, 1)
            for nh in range(2):
                act.activation(prob[:, nh * UN:nh * UN + UN], psum[:, nh, :], ACT.Exp, bias=sbias, scale=XSCALE,
                               accum_out=ssum2[:, nh:nh + 1]).then_inc(prob_ready, 1)
            act.wait_ge(probT_psum, 1)
            act.activation(probT[:, 0:4, :], psum[:, 4, :], ACT.Copy).then_inc(probT_lo, 1)

            evacuate_hT(4)
            act.wait_ge(krot_ready, 1)
            for r in range(GQ):
                last = act.activation(krep[:, :, r, :], krot.rearrange("p (g d) -> p g d", g=HKV), ACT.Copy)
            last.then_inc(krep_ready, 1)
            for b in range(B):
                rows = slice(L * b, L * b + L)
                to = vdup[rows, b, :].rearrange("p (h d) -> p h d", h=HKV)
                act.activation(to[:, :, 0:DH], psum[rows, 0, 256:512].rearrange("p (h d) -> p h d", h=HKV),
                               ACT.Copy).then_inc(v_ready, 1)
            act.wait_ge(v_ready, 3)
            act.dma_start(vdup[L:P, 0, :], vdup[0:L, 0, :]).then_inc(vdup_in, 16)
            act.dma_start(vdup[0:L, 1, :], vdup[L:P, 1, :]).then_inc(vdup_in, 16)
            for n in range(2):
                act.wait_ge(akT_psum, n + 1)
                act.activation(akT[:, 4 * n:4 * n + 4, :], psum[:, 4 + n, :], ACT.Copy).then_inc(akT_ready, 1)
            for n in range(2):
                act.wait_ge(aqT_psum, n + 1)
                act.activation(aqT[:, 4 * n:4 * n + 4, :], psum[:, 6 + n, :], ACT.Copy).then_inc(aqT_ready, 1)
            for r in range(GQ):
                act.wait_ge(as_ready, r + 1)
                act.activation(aprob[:, r, :, :], aprob[:, r, :, :], ACT.Exp).then_inc(ap_ready, 1)
            for r in (0, 2):
                act.wait_ge(apT_psum, r + 1)
                act.activation(aprobT[:, 4 * r:4 * r + 4, :], psum[:, 4 + r, :], ACT.Copy).then_inc(apT_ready, 1)
            act.wait_ge(attnT_psum, 1)
            act.activation(attnT[:, 0:4, :], psum[:, 6, :], ACT.Copy).then_inc(attnT_ready, 1)

            evacuate_hT(5)
            act.wait_ge(g_psum, 1)
            act.activation(gT[:, 0:4, :], psum[:, 4, :], ACT.Copy).then_inc(g_sb, 1)
            for q in range(4):
                for r in range(2):
                    act.wait_ge(up_psum, q + 1)
                    to = hidden[:, 4 * q + r:4 * q + r + 3:2, :, :]
                    act.activation(to, psum[:, 4 * r + q, :].rearrange("p (h m t) -> p h m t", h=2, m=2),
                                   ACT.Gelu).then_inc(hidden_ready, 1)
            act.wait_ge(down_psum, 1)
            act.activation(oT[:, 0:4, :], psum[:, 0, :], ACT.Copy).then_inc(oT_ready, 1)

        @block.tensor
        def _(pe):
            def transpose4(bank, tile, first_col, signal):
                for k in range(4):
                    c = first_col + P * k
                    last = pe.transpose(psum[:, bank, P * k:P * k + P], tile[:, c:c + P], ident[:, :])
                last.then_inc(signal, 1)

            def products(bank, left, u, k0, start, stop, signal=unit_used):
                arrived(pe, u)
                for k in range(UK):
                    last = pe.matmul(psum[:, bank, :], left[:, k0 + k, :], slot(u)[:, k, :],
                                     start=(start and k == 0), stop=(stop and k == UK - 1))
                last.then_inc(signal, 1)

            pe.wait_ge(const_ready, 3)
            for half in range(2):
                pe.wait_ge(q1_ready, 1)
                transpose4(6 + half, h, UN * half, q1_psum)
            pe.wait_ge(q1T_ready, 2)
            pe.wait_ge(z_ready, 1)
            for nh in range(2):
                for kh in range(2):
                    u = 4 * nh + 2 * kh
                    pe.wait_ge(ctx_coded, u + 2)
                    for k in range(UK):
                        for part in range(4):
                            for b in range(B):
                                left = q1T[:, UK * kh + k, L * b:L * b + L] if part == 0 else zneg[:, part - 1, :]
                                last = pe.matmul(psum[L * b:L * b + L, nh, :], left, q2[:, u + b, UN * k:UN * k + UN],
                                                 start=(kh == 0 and k == 0 and part == 0),
                                                 stop=(kh == 1 and k == UK - 1 and part == 3))
                last.then_inc(q_done, 1)

            def transpose_h(n):
                for half in range(2):
                    pe.wait_ge(h_ready, 2 * n + half + 1)
                    transpose4(6 + half, h, UN * half, hT_psum)

            transpose_h(1)

            def turn(j):
                pe.wait_ge(proj_sb, j + 1)
                if j >= 2:
                    pe.wait_ge(projT_read, j - 1)
                transpose4(3 + j % 2, proj[:, j % 4, :], 0, projT_psum)

            w_in = first["w_in"]
            for j in range(NB):
                if j >= 3:
                    pe.wait_ge(proj_sb, j - 2)
                pe.wait_ge(hT_lo, 1)
                products(j % 3, hT, w_in + 2 * j, 0, True, False)
                if j >= 1:
                    turn(j - 1)
                if j == 6:
                    pe.wait_ge(dt_normed, 1)
                    pe.transpose(psum[0:R, 5, 128:256], ssm[:, 0:R], ident[:, :]).then_inc(dtT_psum, 1)
                if j == 7:
                    pe.wait_ge(cdiag_ready, 1)
                    for c in range(2):
                        pe.wait_ge(z_read, 3 + c)
                        pe.matmul(psum[:, 6 + c, :], ones, cdiag[:, 4 * c:4 * c + 4, :], start=True, stop=True).then_inc(c_psum, 1)
                pe.wait_ge(hT_hi, 1)
                products(j % 3, hT, w_in + 2 * j + 1, 4, False, True, proj_psum)
                if j == 5:
                    pe.wait_ge(gated, 4)
                    pe.wait_ge(mamba_in, 80)
                    for k in range(DT):
                        last = pe.matmul(psum[:, 5, 0:SSM], uc[:, k, :], wxT[:, k, :], start=(k == 0), stop=(k == DT - 1))
                    last.then_inc(ssm_psum, 1)
                if j == 6:
                    pe.wait_ge(dtT_ready, 1)
                    for k in range(DT):
                        g = k // GD
                        if k % GD == 0 and g >= 2:
                            pe.wait_ge(z_read, g - 1)
                        last = pe.matmul(psum[:, 6 + g % 2, P * (k % GD):P * (k % GD) + P], wdtT[0:R, P * k:P * k + P],
                                         dtT[0:R, :], start=True, stop=True)
                        if k % GD == GD - 1:
                            last.then_inc(z_psum, 1)
            for g in range(NG):
                pe.wait_ge(du_ready, g + 1)
                if g >= 2:
                    pe.wait_ge(duT_ready, g - 1)
                transpose4(2 + 3 * (g % 2), zbuf[:, g, :], 0, duT_psum)
            for c in range(2, 4):
                pe.wait_ge(c_ready, c - 1)
                pe.matmul(psum[:, 4 + c, :], ones, cdiag[:, 4 * c:4 * c + 4, :], start=True, stop=True).then_inc(c_psum, 1)
            pe.wait_ge(proj_sb, 8)
            pe.wait_ge(projT_read, 6)
            transpose4(4, proj[:, 7 % 4, :], 0, projT_psum)

            def scan_input(s):
                if s >= 3:
                    pe.wait_ge(scan_done, s - 2)
                for c in range(2):
                    last = pe.matmul(psum[:, 2 * (s % 3) + c, :], duT[:, P * (s // 2):P * (s // 2) + P],
                                     bdiag[:, HN * (s % 2) + 4 * c:HN * (s % 2) + 4 * c + 4, :], start=True, stop=True)
                last.then_inc(dbu_ready, 1)

            def state_sum(s):
                pe.wait_ge(pairs_ready, s + 1)
                k = s // 2
                g = k // GD
                if g >= 2:
                    pe.wait_ge(yg_ready, g - 1)
                cols = slice(P * (k % GD), P * (k % GD) + P)
                for n in range(HN // 2):
                    last = pe.matmul(psum[:, 6 + g % 2, cols], ident[:, :], pairs[:, s % 3, P * n:P * n + P],
                                     start=(s % 2 == 0 and n == 0), stop=(s % 2 == 1 and n == HN // 2 - 1))
                last.then_inc(reduced, 1)

            pe.wait_ge(bdiag_ready, 1)
            pe.wait_ge(duT_ready, 4)
            pe.wait_ge(c_ready, 4)
            pe.wait_ge(projT_read, 8)
            for s in range(STEPS):
                scan_input(s)
                if s >= 2:
                    state_sum(s - 2)
            state_sum(STEPS - 2)
            state_sum(STEPS - 1)
            for nh in range(2):
                for g in range(NG):
                    pe.wait_ge(yg_ready, g + 1)
                    products(nh, sg, first["w_out"] + NG * nh + g, GD * g, g == 0, g == NG - 1,
                             y_psum if g == NG - 1 else unit_used)

            transpose_h(2)
            pe.wait_ge(mix_in, 80)
            pe.wait_ge(hT_lo, 2)
            pe.wait_ge(hT_hi, 2)
            for k in range(KT):
                last = pe.matmul(psum[:, 2, 0:NE * RANK + NE], hT[:, k, :], w_ar[:, k, :], start=(k == 0), stop=(k == KT - 1))
            last.then_inc(ar_psum, 1)
            for nh in range(2):
                for kh in range(2):
                    products(nh, hT, first["w_base"] + 2 * nh + kh, UK * kh, kh == 0, False)
                if nh == 0:
                    pe.wait_ge(g_ready, 1)
                    pe.transpose(psum[:, 3, 0:P], lora_g.rearrange("p e r -> p (e r)"), ident[:, :]).then_inc(gT_psum, 1)
                    pe.wait_ge(gT_ready, 1)
                pe.matmul(psum[:, nh, :], lora_gT, lora_b[:, UN * nh:UN * nh + UN], start=False, stop=True).then_inc(base_psum, 1)

            transpose_h(3)
            xwq, xwk = first["x_wq"], first["x_wk"]
            pe.wait_ge(hT_lo, 3)
            products(0, hT, xwq, 0, True, False)
            pe.wait_ge(hT_hi, 3)
            products(0, hT, xwq + 1, 4, False, True, xq_psum)
            products(1, hT, xwq + 2, 0, True, False)
            pe.wait_ge(xq_ready, 1)
            transpose4(4, xq, 0, xqT_psum)
            products(1, hT, xwq + 3, 4, False, True, xq_psum)
            pe.wait_ge(xqT_lo, 1)
            products(2, xqT, xwk, 0, True, False)
            pe.wait_ge(xq_ready, 2)
            transpose4(5, xq, UN, xqT_psum)
            pe.wait_ge(xqT_hi, 1)
            products(2, xqT, xwk + 1, 4, False, True, xk_psum)
            products(3, xqT, xwk + 2, 0, True, False)
            pe.wait_ge(xk_lo, 1)
            transpose4(6, xk, 0, xkT_psum)
            products(3, xqT, xwk + 3, 4, False, True, xk_psum)
            pe.wait_ge(xk_hi, 1)
            transpose4(7, xk, UN, xkT_psum)

            def batched(bank, left, u0, kh, signal):
                arrived(pe, u0)
                arrived(pe, u0 + 1)
                for k in range(UK):
                    for b in range(B):
                        last = pe.matmul(psum[L * b:L * b + L, bank, :], left[:, UK * kh + k, L * b:L * b + L],
                                         slot(u0 + b)[:, k, :], start=(kh == 0 and k == 0), stop=(kh == 1 and k == UK - 1))
                last.then_inc(signal if kh else unit_used, 1)

            pe.wait_ge(xkT_lo, 1)
            for nh in range(2):
                for kh in range(2):
                    if nh == 0 and kh == 1:
                        pe.wait_ge(xkT_hi, 1)
                    batched(nh, xkT, first["ctx_t"] + 4 * nh + 2 * kh, kh, score_psum)
            for half in range(2):
                pe.wait_ge(prob_ready, half + 1)
                transpose4(4 + half, prob, UN * half, probT_psum)
            pe.wait_ge(probT_lo, 1)
            for nh in range(2):
                for kh in range(2):
                    if nh == 0 and kh == 1:
                        pe.wait_ge(probT_hi, 1)
                    batched(2 + nh, probT, first["ctx_again"] + 4 * nh + 2 * kh, kh, xatt_psum)

            transpose_h(4)
            pe.wait_ge(hT_lo, 4)
            products(0, hT, first["a_wkv"], 0, True, False)
            pe.wait_ge(hT_hi, 4)
            products(0, hT, first["a_wkv"] + 1, 4, False, True, kv_psum)
            awq = first["a_wq"]
            products(1, hT, awq, 0, True, False)
            products(1, hT, awq + 1, 4, False, True, aq_psum)
            pe.wait_ge(krep_ready, 1)
            transpose4(4, krep.rearrange("p g r d -> p (g r d)"), 0, akT_psum)
            transpose4(5, krep.rearrange("p g r d -> p (g r d)"), UN, akT_psum)
            products(2, hT, awq + 2, 0, True, False)
            pe.wait_ge(qrot_ready, 1)
            transpose4(6, qrot, 0, aqT_psum)
            products(2, hT, awq + 3, 4, False, True, aq_psum)
            pe.wait_ge(qrot_ready, 2)
            transpose4(7, qrot, UN, aqT_psum)
            pe.wait_ge(akT_ready, 2)
            for j in range(KT):
                pe.wait_ge(aqT_ready, j // 4 + 1)
                for r in range(GQ):
                    for b in range(B):
                        rows = slice(DH * r, DH * r + DH)
                        cols = slice(L * b, L * b + L)
                        last = pe.matmul(psum[cols, r, L * j:L * j + L], aqT[rows, j, cols], akT[rows, j, cols],
                                         start=True, stop=True, tile_position=(DH * r, L * b))
            last.then_inc(as_psum, 1)
            flat = aprob.rearrange("p r j s -> p r (j s)")
            for r in range(GQ):
                pe.wait_ge(ap_ready, r + 1)
                transpose4(4 + r, flat[:, r, :], 0, apT_psum)
            pe.wait_ge(apT_ready, 4)
            pe.wait_ge(vdup_in, 32)
            for r in range(GQ):
                for j in range(HKV):
                    odd = j % 2
                    rows = slice(L * odd, L * odd + L)
                    at = (DH + 1) * (4 * (r % 2) + j // 2)
                    for b in range(B):
                        last = pe.matmul(psum[L * b:L * b + L, 2 * odd + r // 2, at:at + DH + 1],
                                         aprobT[rows, 4 * r + j // 2, L * b:L * b + L],
                                         vdup[rows, b, (DH + 1) * j:(DH + 1) * (j + 1)],
                                         start=True, stop=True, tile_position=(L * odd, L * b))
            last.then_inc(pv_psum, 1)
            pe.wait_ge(attn_ready, 1)
            transpose4(6, attn, 0, attnT_psum)
            transpose4(7, attn, UN, attnT_psum)
            pe.wait_ge(attnT_ready, 2)
            for nh in range(2):
                for kh in range(2):
                    products(nh, attnT, first["a_wo"] + 2 * nh + kh, UK * kh, kh == 0, kh == 1,
                             ao_psum if kh else unit_used)

            transpose_h(5)
            pe.wait_ge(hT_lo, 5)
            pe.wait_ge(hT_hi, 5)
            pe.wait_ge(pick_ready, KT)
            for i in range(KT):
                for k in range(KT):
                    last = pe.matmul(psum[:, 4 + i // 4, P * (i % 4):P * (i % 4) + P], pick[:, k, P * i:P * i + P], hT[:, k, :],
                                     start=(k == 0), stop=(k == KT - 1))
                if i % 4 == 3:
                    last.then_inc(g_psum, 1)
            up = ring[:, first["mlp_up"] % SLOTS, :].rearrange("p (a m) -> p a m", a=MH // 2)
            down = ring[:, first["mlp_down"] % SLOTS, :].rearrange("p (m h d) -> p m h d", m=2, h=MH)
            arrived(pe, first["mlp_up"])
            arrived(pe, first["mlp_down"])
            pe.wait_ge(g_sb, 2)
            for a in range(MH // 2):
                for m in range(2):
                    for r in range(2):
                        rows = slice(MD * r, MD * r + MD)
                        at = 256 * (a % 2) + P * m
                        last = pe.matmul(psum[:, 4 * r + a // 2, at:at + P], up[rows, a, P * m:P * m + P], gT[rows, a, :],
                                         start=True, stop=True)
                if a % 2:
                    last.then_inc(up_psum, 1)
            for a in range(MH // 2):
                pe.wait_ge(hidden_ready, 8)
                for m in range(2):
                    for r in range(2):
                        last = pe.matmul(psum[MD * r:MD * r + MD, a // 4, P * (a % 4):P * (a % 4) + P], down[:, m, 2 * a + r, :],
                                         hidden[:, 2 * a + r, m, :], start=(m == 0), stop=(m == 1))
                if a % 4 == 3:
                    last.then_inc(down_psum, 1)
            pe.wait_ge(oT_ready, 2)
            pe.wait_ge(place_ready, KT)
            for nh in range(2):
                for k in range(KT):
                    last = pe.matmul(psum[:, 2 + nh, :], oT[:, k, :], place[:, k, UN * nh:UN * nh + UN], start=(k == 0), stop=(k == KT - 1))
                last.then_inc(placed, 1)

        @block.vector
        def _(dve):
            steps = [0]

            def step(ins):
                steps[0] += 1
                ins.then_inc(dve_step, 1)
                dve.wait_ge(dve_step, steps[0])

            def halves(nh):
                return slice(UN * nh, UN * nh + UN)

            def norm(n):
                for nh in range(2):
                    if n:
                        dve.wait_ge(x_ready, 2 * n - 1 + nh)
                    step(dve.bn_stats(stats[:, nh, :], x[:, halves(nh)]))
                step(dve.bn_aggr(mv, stats.rearrange("p a b -> p (a b)")))
                dve.tensor_scalar(var_eps, mv[:, 1:2], LN_EPS, None, ALU.add).then_inc(var_ready, 1)
                dve.wait_ge(rstd_ready, n + 1)
                for nh in range(2):
                    dve.tensor_scalar(h[:, halves(nh)], x[:, halves(nh)], mv[:, 0:1], rstd, ALU.subtract,
                                      ALU.mult).then_inc(h_ready, 1)

            def finish_hT(n):
                dve.wait_ge(hT_psum, 2 * n)
                dve.tensor_copy(hT[:, 4:8, :], psum[:, 7, :]).then_inc(hT_hi, 1)

            def add_to_x(nh, bank, to=None):
                to = x if to is None else to
                dve.tensor_tensor(to[:, halves(nh)], x[:, halves(nh)], psum[:, bank, :], ALU.add).then_inc(x_ready, 1)

            dve.wait_ge(quant_in, 16)
            dve.reciprocal(qrec, quant[:, 0:2]).then_inc(scales_ready, 1)
            dve.wait_ge(x_in, 16)
            norm(0)
            dve.wait_ge(h_ready, 2)
            step(dve.tensor_scalar(h[:, :], h[:, :], qrec[:, 0:1], quant[:, 2:3], ALU.mult, ALU.add))
            step(dve.tensor_scalar(h[:, :], h[:, :], ROUND, ROUND, ALU.add, ALU.max))
            dve.tensor_scalar(h[:, :], h[:, :], ROUND + QMAX, ROUND + QMID, ALU.min, ALU.subtract).then_inc(q1_ready, 1)
            step(dve.tensor_scalar(qneg, quant[:, 2:4], -1.0, QMID, ALU.mult, ALU.add))
            dve.wait_ge(const_ready, 3)
            step(dve.tensor_copy(zrest[:, 0:1], qneg[:, 0:1]))
            for j in range(3):
                step(dve.tensor_copy(zpart[:, j:j + 1], zrest[:, 0:1]))
                if j < 2:
                    step(dve.tensor_tensor(zrest[:, 0:1], zrest[:, 0:1], zpart[:, j:j + 1], ALU.subtract))
            for j in range(3):
                last = dve.tensor_scalar(zneg[:, j, :], ones64, zpart[:, j:j + 1], None, ALU.mult)
            last.then_inc(z_ready, 1)
            for half in range(2):
                dve.wait_ge(q1_psum, half + 1)
                dve.tensor_copy(q1T[:, 4 * half:4 * half + 4, :], psum[:, 6 + half, :]).then_inc(q1T_ready, 1)

            def code(n):
                dve.wait_ge(ctx_scaled, n + 1)
                v = ring[:, n % SLOTS, :]
                step(dve.tensor_scalar(v, v, ROUND, ROUND, ALU.add, ALU.max))
                dve.tensor_scalar(q2[:, n, :], v, ROUND + QMAX, ROUND + QMID, ALU.min, ALU.subtract).then_inc(ctx_coded, 1)

            code(0)
            code(1)
            dve.wait_ge(q1_ready, 1)
            step(dve.tensor_reduce(q_sum, h[:, :], AX, ALU.add))
            step(dve.tensor_scalar(q_row, qneg[:, 0:1], float(D), q_sum, ALU.mult, ALU.add))
            step(dve.tensor_scalar(q_s12, quant[:, 0:1], quant[:, 1:2], None, ALU.mult))
            step(dve.tensor_scalar(q_row, q_row, qneg[:, 1:2], q_s12, ALU.mult, ALU.mult))
            step(dve.tensor_scalar(x[:, :], x[:, :], q_row, None, ALU.add))
            for n in range(2, 8):
                code(n)
            for nh in range(2):
                dve.wait_ge(q_done, nh + 1)
                dve.scalar_tensor_tensor(out=x[:, halves(nh)], in0=psum[:, nh, :], scalar=q_s12, in1=x[:, halves(nh)],
                                         op0=ALU.mult, op1=ALU.add).then_inc(x_ready, 1)

            norm(1)
            finish_hT(1)
            dve.wait_ge(mamba_in, 80)
            dve.wait_ge(edge_zero, 1)

            def conv(g):
                dve.wait_ge(projT_psum, g + 1)
                tiles = range(GD * g, GD * g + GD)
                dve.tensor_copy(uT[:, GD * g:GD * g + GD, :, CK - 1:],
                                psum[:, 3 + g % 2, :].rearrange("p (k b t) -> p k b t", k=GD, b=B)).then_inc(projT_read, 1)
                dve.wait_ge(projT_read, g + 1)
                for j in range(CK):
                    for k in tiles:
                        to = uc[:, k, :].rearrange("p (b t) -> p b t", b=B)
                        tap = uT[:, k, :, j:j + L]
                        if j == 0:
                            last = dve.tensor_scalar(to, tap, conv_w[:, k, 0:1], conv_b[:, k:k + 1], ALU.mult, ALU.add)
                        else:
                            last = dve.scalar_tensor_tensor(out=to, in0=tap, scalar=conv_w[:, k, j:j + 1], in1=to,
                                                            op0=ALU.mult, op1=ALU.add)
                    step(last)
                if g >= 2:
                    dve.wait_ge(gated, g - 1)
                dve.tensor_scalar(sig[:, g % 2, :], uc[:, GD * g:GD * g + GD, :].rearrange("p k t -> p (k t)"),
                                  SIG_MIN, None, ALU.max).then_inc(sig_in, 1)

            def times_sigmoid(n):
                dve.wait_ge(sig_out, n + 1)
                v = (uc if n < NG else sg)[:, GD * (n % NG):GD * (n % NG) + GD, :].rearrange("p k t -> p (k t)")
                dve.tensor_tensor(v, v, sig[:, n % 2, :], ALU.mult).then_inc(gated, 1)

            def gate_copy(g):
                n = NG + g
                bank = 3 + n % 2
                dve.wait_ge(projT_psum, n + 1)
                v = sg[:, GD * g:GD * g + GD, :].rearrange("p k t -> p (k t)")
                dve.tensor_copy(v, psum[:, bank, :]).then_inc(projT_read, 1)
                dve.wait_ge(projT_read, n + 1)
                dve.wait_ge(gated, n - 1)
                dve.tensor_scalar(sig[:, n % 2, :], v, SIG_MIN, None, ALU.max).then_inc(sig_in, 1)

            conv(0)
            conv(1)
            times_sigmoid(0)
            conv(2)
            times_sigmoid(1)
            conv(3)
            times_sigmoid(2)
            times_sigmoid(3)
            gate_copy(0)
            dve.wait_ge(ssm_psum, 1)
            step(dve.tensor_copy(ssm, psum[:, 5, 0:SSM]))
            parts = [(0, R), (R, R + NS), (R + NS, SSM)]
            for i, (a, c) in enumerate(parts):
                step(dve.tensor_tensor_reduce(out=rms_junk[:, 0:c - a], in0=ssm[:, a:c], in1=ssm[:, a:c], scale=1.0, scalar=0.0,
                                              op0=ALU.mult, op1=ALU.add, accum_out=rms_sum[:, i:i + 1]))
            for i, (a, c) in enumerate(parts):
                last = dve.tensor_scalar(rms_var[:, i:i + 1], rms_sum[:, i:i + 1], 1.0 / (c - a), RMS_EPS, ALU.mult, ALU.add)
            last.then_inc(ssm_sum, 1)
            dve.wait_ge(ssm_inv, 1)
            for i, (a, c) in enumerate(parts):
                dve.scalar_tensor_tensor(out=ssm[:, a:c], in0=ssm[:, a:c], scalar=rms_inv[:, i:i + 1], in1=rms_w[:, a:c],
                                         op0=ALU.mult, op1=ALU.mult).then_inc(dt_normed if i == 0 else bc_ready, 1)
            times_sigmoid(4)
            gate_copy(1)

            def softplus_in(g):
                dve.wait_ge(z_psum, g + 1)
                z = zbuf[:, g, :].rearrange("p (k t) -> p k t", k=GD)
                dve.tensor_tensor(z, psum[:, 6 + g % 2, :].rearrange("p (k t) -> p k t", k=GD),
                                  along(dt_b[:, GD * g:GD * g + GD], P), ALU.add).then_inc(z_read, 1)
                dve.wait_ge(z_read, g + 1)
                dve.scalar_tensor_tensor(out=delta[:, GD * g:GD * g + GD, :], in0=z, scalar=-1.0, in1=z, op0=ALU.mult,
                                         op1=ALU.max).then_inc(z_abs, 1)

            def softplus_out(g):
                dve.wait_ge(softlog, g + 1)
                z = zbuf[:, g, :].rearrange("p (k t) -> p k t", k=GD)
                v = delta[:, GD * g:GD * g + GD, :]
                dve.scalar_tensor_tensor(out=v, in0=z, scalar=0.0, in1=v, op0=ALU.max, op1=ALU.add).then_inc(delta_ready, 1)
                dve.wait_ge(delta_ready, g + 1)
                dve.tensor_tensor(z, v, uc[:, GD * g:GD * g + GD, :], ALU.mult).then_inc(du_ready, 1)

            softplus_in(0)
            softplus_in(1)
            softplus_out(0)
            softplus_out(1)
            softplus_in(2)
            softplus_in(3)
            softplus_out(2)
            softplus_out(3)
            times_sigmoid(5)
            gate_copy(2)
            times_sigmoid(6)
            gate_copy(3)

            def scan(s):
                dve.wait_ge(dA_ready, s + 1)
                dve.wait_ge(dbu_ready, s + 1)
                if s >= 3:
                    dve.wait_ge(pairs_ready, s - 2)
                p = 2 * (s % 3)
                dve.tensor_tensor_scan(state[:, s % 3, :], dA[:, s % 3, :], psum[:, p:p + 2, :].rearrange("p a b -> p (a b)"),
                                       0.0, ALU.mult, ALU.add).then_inc(scan_done, 1)

            def times_c(s):
                dve.wait_ge(scan_done, s + 1)
                c = cwide[:, HN * P * (s % 2):HN * P * (s % 2) + HN * P]
                dve.tensor_tensor(state[:, s % 3, :], state[:, s % 3, :], c, ALU.mult).then_inc(prod_ready, 1)

            def gate_y(g):
                dve.wait_ge(reduced, 2 * GD * (g + 1))
                for k in range(GD * g, GD * g + GD):
                    cols = slice(P * (k % GD), P * (k % GD) + P)
                    last = dve.scalar_tensor_tensor(out=uc[:, k, :], in0=uc[:, k, :], scalar=d_par[:, k:k + 1],
                                                    in1=psum[:, 6 + g % 2, cols], op0=ALU.mult, op1=ALU.add)
                step(last)
                v = slice(GD * g, GD * g + GD)
                dve.tensor_tensor(sg[:, v, :], sg[:, v, :], uc[:, v, :], ALU.mult).then_inc(yg_ready, 1)

            for s in range(STEPS):
                scan(s)
                if s == 1:
                    dve.wait_ge(c_ready, 4)
                if s >= 1:
                    times_c(s - 1)
                if s == 4:
                    times_sigmoid(7)
                if s >= 12 and (s - 12) % 8 == 0:
                    gate_y((s - 12) // 8)
            times_c(STEPS - 1)
            gate_y(NG - 1)
            for nh in range(2):
                dve.wait_ge(y_psum, nh + 1)
                add_to_x(nh, nh)

            norm(2)
            finish_hT(2)
            dve.wait_ge(tri_in, 16)
            dve.wait_ge(ar_psum, 1)
            ranks = NE * RANK
            step(dve.tensor_copy(logit, psum[:, 2, ranks:ranks + NE]))
            step(dve.tensor_reduce(top, logit, AX, ALU.max))
            dve.tensor_scalar(top, top, -1.0, None, ALU.mult).then_inc(top_ready, 1)
            step(dve.tensor_tensor(above, wide(logit, NE), along(logit, NE), ALU.is_gt))
            step(dve.tensor_tensor(ties, wide(logit, NE), along(logit, NE), ALU.is_equal))
            step(dve.tensor_tensor(ties, ties, tri, ALU.mult))
            step(dve.tensor_tensor(above, above, ties, ALU.add))
            step(dve.tensor_reduce(rank, above, AX, ALU.add))
            dve.wait_ge(exp_ready, 1)
            step(dve.scalar_tensor_tensor(out=gate, in0=rank, scalar=1.5, in1=gate, op0=ALU.is_lt, op1=ALU.mult))
            step(dve.tensor_reduce(den, gate, AX, ALU.add))
            step(dve.reciprocal(den_inv, den))
            step(dve.tensor_scalar(gate, gate, den_inv, LORA_SCALE, ALU.mult, ALU.mult))
            dve.tensor_tensor(lora_g, psum[:, 2, 0:ranks].rearrange("p (e r) -> p e r", e=NE), along(gate, RANK),
                              ALU.mult).then_inc(g_ready, 1)
            dve.wait_ge(biased, 1)
            for nh in range(2):
                dve.wait_ge(base_psum, nh + 1)
                add_to_x(nh, nh)

            norm(3)
            finish_hT(3)
            for nh in range(2):
                dve.wait_ge(xq_psum, nh + 1)
                dve.tensor_tensor(xq[:, halves(nh)], psum[:, nh, :], bq[:, halves(nh)], ALU.add).then_inc(xq_ready, 1)
            dve.wait_ge(xqT_psum, 2)
            dve.tensor_copy(xqT[:, 4:8, :], psum[:, 5, :]).then_inc(xqT_hi, 1)
            step(dve.tensor_tensor_reduce(out=junk, in0=xq, in1=bk, scale=1.0, scalar=0.0, op0=ALU.mult, op1=ALU.add,
                                          accum_out=qbias))
            dve.wait_ge(xk_psum, 2)
            dve.tensor_copy(xk[:, halves(1)], psum[:, 3, :]).then_inc(xk_hi, 1)
            dve.wait_ge(xkT_psum, 2)
            dve.tensor_copy(xkT[:, 4:8, :], psum[:, 7, :]).then_inc(xkT_hi, 1)
            for nh in range(2):
                dve.wait_ge(score_psum, nh + 1)
                step(dve.tensor_reduce(smax2[:, nh:nh + 1], psum[:, nh, :], AX, ALU.max))
            step(dve.tensor_reduce(smax, smax2, AX, ALU.max))
            step(dve.tensor_scalar(smax, smax, qbias, -XSCALE, ALU.add, ALU.mult))
            dve.scalar_tensor_tensor(out=sbias, in0=qbias, scalar=XSCALE, in1=smax, op0=ALU.mult, op1=ALU.add).then_inc(sbias_ready, 1)
            dve.wait_ge(probT_psum, 2)
            dve.tensor_copy(probT[:, 4:8, :], psum[:, 5, :]).then_inc(probT_hi, 1)
            step(dve.tensor_reduce(ssum, ssum2, AX, ALU.add))
            step(dve.reciprocal(sinv, ssum))
            for nh in range(2):
                dve.wait_ge(xatt_psum, nh + 1)
                dve.scalar_tensor_tensor(out=x[:, halves(nh)], in0=psum[:, 2 + nh, :], scalar=sinv, in1=x[:, halves(nh)],
                                         op0=ALU.mult, op1=ALU.add).then_inc(x_ready, 1)

            norm(4)
            finish_hT(4)
            step(dve.memset(vdup.rearrange("p b (h d) -> p (b h) d", d=DH + 1)[:, :, DH:], 1.0))
            dve.tensor_copy(hmax.rearrange("p a b -> p (a b)")[:, 0:1], sinv).then_inc(v_ready, 1)

            def rotate(source, heads, to, signal):
                v = source.rearrange("p (h d) -> p h d", h=heads)
                c = rope_c[:, 0:heads * DH].rearrange("p (h d) -> p h d", h=heads)
                s = rope_s[:, 0:heads * DH].rearrange("p (h d) -> p h d", h=heads)
                hd = DH // 2
                dve.tensor_tensor(c, v, wide(cosf, heads), ALU.mult)
                dve.tensor_tensor(s[:, :, 0:hd], v[:, :, hd:], wide(sinf[:, 0:hd], heads), ALU.mult)
                step(dve.tensor_tensor(s[:, :, hd:], v[:, :, 0:hd], wide(sinf[:, hd:], heads), ALU.mult))
                dve.tensor_tensor(to.rearrange("p (h d) -> p h d", h=heads), c, s, ALU.add).then_inc(signal, 1)

            dve.wait_ge(tables_in, 16)
            dve.wait_ge(kv_psum, 1)
            rotate(psum[:, 0, 0:HKV * DH], HKV, krot, krot_ready)
            dve.wait_ge(krot_ready, 1)
            for n in range(2):
                dve.wait_ge(aq_psum, n + 1)
                if n:
                    dve.wait_ge(qrot_ready, 1)
                rotate(psum[:, 1 + n, :], H // 2, qrot[:, halves(n)], qrot_ready)
            dve.wait_ge(as_psum, 1)
            for r in range(GQ):
                v = aprob[:, r, :, :]
                step(dve.scalar_tensor_tensor(out=v, in0=psum[:, r, :].rearrange("p (j s) -> p j s", j=HKV), scalar=ASCALE,
                                              in1=wide(mask, HKV), op0=ALU.mult, op1=ALU.add))
                step(dve.tensor_reduce(hmax[:, r, :], v, AX, ALU.max))
                dve.tensor_tensor(v, v, along(hmax[:, r, :], L), ALU.subtract).then_inc(as_ready, 1)
            for r in (1, 3):
                dve.wait_ge(apT_psum, r + 1)
                dve.tensor_copy(aprobT[:, 4 * r:4 * r + 4, :], psum[:, 4 + r, :]).then_inc(apT_ready, 1)
            dve.wait_ge(pv_psum, 1)
            for q in range(4):
                odd, hi = q // 2, q % 2
                o = psum[:, q, 0:HKV * (DH + 1)].rearrange("p (n d) -> p n d", n=HKV)
                inv = oinv[:, q, :]
                step(dve.reciprocal(inv.rearrange("p (n u) -> p n u", u=1), o[:, :, DH:]))
                for a in range(2):
                    to = attn.rearrange("p (j r d) -> p j r d", j=HKV, r=GQ)[:, odd::2, 2 * hi + a, :]
                    last = dve.tensor_tensor(to, o[:, 4 * a:4 * a + 4, 0:DH], along(inv[:, 4 * a:4 * a + 4], DH), ALU.mult)
            last.then_inc(attn_ready, 1)
            dve.wait_ge(attnT_psum, 2)
            dve.tensor_copy(attnT[:, 4:8, :], psum[:, 7, :]).then_inc(attnT_ready, 1)
            for nh in range(2):
                dve.wait_ge(ao_psum, nh + 1)
                add_to_x(nh, nh)

            norm(5)
            finish_hT(5)
            dve.wait_ge(g_psum, 2)
            dve.tensor_copy(gT[:, 4:8, :], psum[:, 5, :]).then_inc(g_sb, 1)
            dve.wait_ge(down_psum, 2)
            dve.tensor_copy(oT[:, 4:8, :], psum[:, 1, :]).then_inc(oT_ready, 1)
            for nh in range(2):
                dve.wait_ge(placed, nh + 1)
                add_to_x(nh, 2 + nh, y_out)


def kernel(**inputs):
    import numpy as np
    import concourse.bacc as bacc
    from concourse.bass_utils import run_bass_kernel_spmd

    f = {name: np.asarray(a) for name, a in inputs.items()}

    def blocks(w):
        k, n = w.shape
        w = w.reshape(k // (UK * P), UK, P, n // UN, UN).transpose(3, 0, 2, 1, 4)
        return w.reshape(-1, P, UNIT)

    def tiles(w):
        return w.reshape(w.shape[0] // P, P, -1).transpose(1, 0, 2)

    def both(w0, w1):
        return np.stack([blocks(w0), blocks(w1)], 1).reshape(-1, P, UNIT)

    ctx = f["ctx_4096"]
    half = DH // 2
    freq = (1.0 / np.float32(10000.0) ** (np.arange(half, dtype=np.float32) / np.float32(half))).astype(np.float32)
    angle = np.arange(L, dtype=np.float32)[:, None] * freq[None, :]
    cos, sin = np.cos(angle).astype(np.float32), np.sin(angle).astype(np.float32)
    cos = np.concatenate([cos, cos], 1)
    sin = np.concatenate([-sin, sin], 1)
    mask = np.where(np.tril(np.ones((L, L), bool)), 0.0, -1e30).astype(np.float32)
    rows = (np.arange(P)[:, None] + P * np.arange(KT)[None, :]).astype(np.float32)
    pad = np.zeros((P, 8), np.float32)
    tables = np.concatenate([np.concatenate([cos, cos]), np.concatenate([sin, sin]), np.concatenate([mask, mask]), rows, pad], 1)
    tri = np.broadcast_to(np.tril(np.ones((NE, NE), np.float32), -1).reshape(1, -1), (P, NE * NE))

    perm = f["L1_ffn_perm"].astype(np.int32) if f["L1_ffn_perm"].dtype != np.int32 else f["L1_ffn_perm"]
    arrays = {
        "x": f["x"].reshape(P, D),
        "quant": np.stack([f["L0_xattn_x1_scale"], f["L0_xattn_x2_scale"], f["L0_xattn_x1_zp"], f["L0_xattn_x2_zp"]], 1),
        "tables": tables,
        "tri": tri,
        "ctx": both(ctx[0], ctx[1]),
        "ctx_t": both(ctx[0].T, ctx[1].T),
        "w_in": blocks(f["L0_attn_W_in"].T),
        "wx": tiles(f["L0_attn_Wx"].T),
        "wdt": f["L0_attn_Wdt"].T,
        "a_par": tiles(f["L0_attn_A"]),
        "chan": np.concatenate([tiles(f["L0_attn_conv_w"]).reshape(P, -1), tiles(f["L0_attn_conv_b"]).reshape(P, -1),
                                tiles(f["L0_attn_dt_bias"]).reshape(P, -1), tiles(f["L0_attn_D_param"]).reshape(P, -1)], 1),
        "rms_w": np.concatenate([f["L0_attn_dt_ln_w"], f["L0_attn_b_ln_w"], f["L0_attn_c_ln_w"]])[None],
        "w_out": blocks(f["L0_attn_W_out"].T),
        "w_base": blocks(f["L0_ffn_W_base"].T),
        "b_base": f["L0_ffn_b_base"][None],
        "w_ar": tiles(np.concatenate([f["L0_ffn_A"].reshape(NE * RANK, D), f["L0_ffn_W_router"]]).T),
        "lora_b": f["L0_ffn_B"].transpose(0, 2, 1).reshape(NE * RANK, D),
        "x_wq": blocks(f["L1_xattn_Wq"].T),
        "x_wk": blocks(f["L1_xattn_Wk"]),
        "bq": f["L1_xattn_bq"][None],
        "bk": f["L1_xattn_bk"][None],
        "a_wkv": blocks(np.concatenate([f["L1_attn_Wk"], f["L1_attn_Wv"]], 1)),
        "a_wq": blocks(f["L1_attn_Wq"]),
        "a_wo": blocks(f["L1_attn_Wo"]),
        "mlp_up": f["L1_ffn_up"].reshape(MH // 2, P, MM).transpose(1, 0, 2).reshape(1, P, UNIT),
        "mlp_down": f["L1_ffn_down"].reshape(MH, 2, P, MD).transpose(2, 1, 0, 3).reshape(1, P, UNIT),
        "perm_row": perm[None],
        "perm_col": perm.reshape(KT, P).T,
    }
    arrays = {name: np.ascontiguousarray(a) for name, a in arrays.items()}
    nc = bacc.Bacc("TRN2", target_bir_lowering=False, num_devices=1)
    dram = {name: nc.dram_tensor(f"in_{name}", a.shape, mybir.dt.from_np(a.dtype), kind="ExternalInput").ap()
            for name, a in arrays.items()}
    out = nc.dram_tensor("out", (P, D), F32, kind="ExternalOutput").ap()
    perceiver(nc, dram, out)
    result = run_bass_kernel_spmd(nc, [{f"in_{name}": a for name, a in arrays.items()}], core_ids=[0])
    return result.results[0]["out"].reshape(B, L, D)
```

```python
from contextlib import ExitStack

import concourse.bass as bass
from concourse import mybir

ALU = mybir.AluOpType
ACT = mybir.ActivationFunctionType
AX = mybir.AxisListType.X
F32 = mybir.dt.float32
BF16 = mybir.dt.bfloat16
F32R = mybir.dt.float32r
I32 = mybir.dt.int32

P = 128
B, L = 2, 64
D = 1024
KT = D // P
UK = 4
UN = 512
UNIT = UK * UN
SLOTS = 7
LN_EPS = 1e-5

DI = 2048
DT = DI // P
NS = 16
R = 64
CK = 4
NB = 2 * DI // UN
SSM = R + 2 * NS
RMS_EPS = 1e-6
GD = UN // P
NG = DT // GD
HN = NS // 2
OWN = 6 * P
STEPS = 2 * DT

NE, RANK = 8, 16
LORA_SCALE = 2.0

XSCALE = 1.0 / 32.0
H, HKV, DH = 32, 8, 32
GQ = H // HKV
ASCALE = float(DH) ** -0.5
MH, MD, MM = 16, 64, 256

ROUND = 1.5 * 2.0 ** 23
QMAX = 255.0
QMID = 128.0


def unit_list():
    units = [("ctx", i) for i in range(8)]
    units += [("w_in", i) for i in range(16)]
    units += [("w_out", i) for i in range(8)]
    units += [("w_base", i) for i in range(4)]
    units += [("x_wq", i) for i in range(4)]
    units += [("x_wk", i) for i in (0, 2, 1, 3)]
    units += [("ctx_t", i) for i in (0, 1, 4, 5, 2, 3, 6, 7)]
    units += [("ctx", i) for i in (0, 1, 4, 5, 2, 3, 6, 7)]
    units += [("a_wkv", i) for i in range(2)]
    units += [("a_wq", i) for i in range(4)]
    units += [("a_wo", i) for i in range(4)]
    units += [("mlp_up", 0), ("mlp_down", 0)]
    return units


def perceiver(nc, dram, out):
    units = unit_list()
    first = {}
    for n, (name, i) in enumerate(units):
        if name == "ctx" and n >= 8:
            name = "ctx_again"
        first.setdefault(name, n)

    with ExitStack() as stack:
        def sb(name, shape, dtype=F32):
            return stack.enter_context(nc.sbuf_tensor(name, shape, dtype))

        def sem(name):
            return stack.enter_context(nc.semaphore(name))

        ring = sb("ring", [P, SLOTS, UNIT])
        x = sb("x", [P, D])
        h = sb("h", [P, D])
        hT = sb("hT", [P, KT, P])
        ident = sb("ident", [P, P])
        small = sb("small", [P, 640])
        arena = sb("arena", [P, 24576])
        rounded = sb("rounded", [P, 4 * DI], F32R)
        split = sb("split", [P, 2, KT, P], F32R)
        b_high = sb("b_high", [P, NS], F32R)
        psum = stack.enter_context(nc.psum_tensor("psum", [P, 8, 512], F32))

        def carve(tile, start, *dims):
            size = 1
            for d in dims:
                size *= d
            ap = tile[:, start:start + size]
            if len(dims) == 2:
                ap = ap.rearrange("p (a b) -> p a b", a=dims[0])
            if len(dims) == 3:
                ap = ap.rearrange("p (a b c) -> p a b c", a=dims[0], b=dims[1])
            return ap

        quant = carve(small, 0, 4)
        qrec = carve(small, 4, 2)
        qneg = carve(small, 6, 2)
        q_col = carve(small, 8, 1)
        b_low = carve(small, 592, NS)
        q_sum = carve(small, 12, 1)
        q_row = carve(small, 13, 1)
        q_s12 = carve(small, 14, 1)
        var_eps = carve(small, 15, 1)
        rstd = carve(small, 16, 1)
        minus_half = carve(small, 17, 4)
        stats = carve(small, 24, 2, 6)
        mv = carve(small, 36, 2)
        const_warm = carve(small, 21, 1)
        rms_sum = carve(small, 40, 3)
        rms_var = carve(small, 43, 3)
        rms_inv = carve(small, 46, 3)
        top = carve(small, 50, 1)
        den = carve(small, 51, 1)
        den_inv = carve(small, 52, 1)
        logit = carve(small, 56, NE)
        rank = carve(small, 64, NE)
        gate = carve(small, 72, NE)
        qbias = carve(small, 80, 1)
        smax2 = carve(small, 81, 2)
        smax = carve(small, 83, 1)
        sbias = carve(small, 84, 1)
        ssum2 = carve(small, 85, 2)
        ssum = carve(small, 87, 1)
        sinv = carve(small, 88, 1)
        hmax = carve(small, 96, GQ, HKV)
        oinv = carve(small, 128, 4, HKV)
        cosf = carve(small, 160, DH)
        sinf = carve(small, 192, DH)
        mask = carve(small, 224, L)
        row_no = carve(small, 288, KT)
        perm_col = carve(small, 296, KT)
        perm_coli = small[:, 304:304 + KT].bitcast(I32)
        conv_w = carve(small, 320, DT, CK)
        conv_b = carve(small, 384, DT)
        dt_b = carve(small, 400, DT)
        d_par = carve(small, 416, DT)
        rms_w = carve(small, 432, SSM)
        tri = carve(small, 528, NE, NE)

        q2 = arena[:, 0:8192].bitcast(BF16).rearrange("p (u n) -> p u n", u=8)
        q1T = arena[:, 8192:8704].bitcast(BF16).rearrange("p (k t) -> p k t", k=KT)
        ones64 = arena[:, 8704:8736].bitcast(BF16)
        codes_junk = carve(arena, 9216, D)
        uT = arena[:, 0:DT * B * (L + 3)].rearrange("p (k b t) -> p k b t", k=DT, b=B)
        zbuf = carve(arena, 0, NG, UN)
        uc = carve(arena, 2144, DT, P)
        delta = carve(arena, 4192, DT, P)
        sg = carve(arena, 6240, DT, P)
        cwide = carve(arena, 8288, NS * P)
        dA = carve(arena, 10336, 3, HN * P)
        state = carve(arena, 13408, 3, HN * P)
        cdiag = carve(arena, 14432, NS, P)
        pairs = carve(arena, 16480, 3, HN * P // 2)
        proj = carve(arena, 16480, 3, UN)
        tanh = carve(arena, 18016, 2, UN)
        wxT = carve(arena, 19040, DT, SSM)
        wdtT = carve(arena, 20576, DI)
        a_par = carve(arena, 22624, DT, NS)
        ssm = carve(arena, 22880, SSM)
        rms_junk = carve(arena, 22976, R)
        dtT = carve(arena, 23040, P)
        ones = carve(arena, 23168, P)
        bd_high = rounded[:, 0:DI].rearrange("p (n t) -> p n t", n=NS)
        bd_low = rounded[:, DI:2 * DI].rearrange("p (n t) -> p n t", n=NS)
        du_high = rounded[:, 2 * DI:3 * DI]
        du_low = rounded[:, 3 * DI:4 * DI]
        lora_b = carve(arena, 0, D)
        w_ar = carve(arena, 1024, KT, NE * RANK + NE)
        bk = carve(arena, 19040, D)
        b_base = carve(arena, 20576, D)
        bq = carve(arena, 21600, D)
        lora_g = carve(arena, 23296, NE, RANK)
        lora_gT = carve(arena, 23424, P)
        above = carve(arena, 23552, NE, NE)
        ties = carve(arena, 23616, NE, NE)
        xq = carve(arena, 0, D)
        xqT = carve(arena, 1024, KT, P)
        xk = carve(arena, 2048, D)
        xkT = carve(arena, 3072, KT, P)
        prob = carve(arena, 4096, D)
        probT = carve(arena, 5120, KT, P)
        junk = carve(arena, 6144, D)
        rope_c = carve(arena, 0, D)
        rope_s = carve(arena, 1024, D)
        qrot = carve(arena, 2048, D)
        krot = carve(arena, 3072, HKV * DH)
        krep = carve(arena, 3328, HKV, GQ, DH)
        aqT = carve(arena, 4352, KT, P)
        akT = carve(arena, 5376, KT, P)
        vdup = carve(arena, 6400, B, HKV * (DH + 1))
        aprob = carve(arena, 6928, GQ, HKV, L)
        aprobT = carve(arena, 0, 2 * KT, P)
        attn = carve(arena, 2048, D)
        attnT = carve(arena, 3072, KT, P)
        permi = arena[:, 9312:10336].bitcast(I32)
        perm_row = carve(arena, 9312, D)
        iota = carve(arena, 10336, D)
        onehot = rounded[:, :].rearrange("p (k n) -> p k n", k=KT)
        gT = carve(arena, 0, KT, P)
        hidden = carve(arena, 1024, MH, 2, P)
        picked = carve(arena, 5120, D)
        y_out = carve(arena, 6144, D)

        unit_in = [sem(f"unit_in{s}") for s in range(SLOTS)]
        x_in = sem("x_in")
        quant_in = sem("quant_in")
        tables_in = sem("tables_in")
        tri_in = sem("tri_in")
        mamba_in = sem("mamba_in")
        rank_in = sem("rank_in")
        bias_in = sem("bias_in")
        perm_in = sem("perm_in")
        vdup_in = sem("vdup_in")
        out_done = sem("out_done")
        ctx_coded = sem("ctx_coded")
        unit_used = sem("unit_used")
        const_zero = sem("const_zero")
        const_ready = sem("const_ready")
        stats_ready = sem("stats_ready")
        var_ready = sem("var_ready")
        rstd_ready = sem("rstd_ready")
        h_ready = sem("h_ready")
        hT_psum = sem("hT_psum")
        hT_lo = sem("hT_lo")
        hT_hi = sem("hT_hi")
        x_ready = sem("x_ready")
        dve_step = sem("dve_step")
        act_step = sem("act_step")
        scales_ready = sem("scales_ready")
        ctx_scaled = sem("ctx_scaled")
        q1_ready = sem("q1_ready")
        qneg_ready = sem("qneg_ready")
        q_step = sem("q_step")
        q_summed = sem("q_summed")
        x_offset = sem("x_offset")
        q1_psum = sem("q1_psum")
        q1T_ready = sem("q1T_ready")
        q_done = sem("q_done")
        edge_zero = sem("edge_zero")
        proj_psum = sem("proj_psum")
        proj_sb = sem("proj_sb")
        projT_psum = sem("projT_psum")
        projT_read = sem("projT_read")
        conv_half = sem("conv_half")
        tanh_ready = sem("tanh_ready")
        gated = sem("gated")
        ssm_psum = sem("ssm_psum")
        ssm_sum = sem("ssm_sum")
        ssm_inv = sem("ssm_inv")
        dt_normed = sem("dt_normed")
        bc_ready = sem("bc_ready")
        dtT_psum = sem("dtT_psum")
        dtT_ready = sem("dtT_ready")
        z_psum = sem("z_psum")
        z_read = sem("z_read")
        z_abs = sem("z_abs")
        z_exp = sem("z_exp")
        softlog = sem("softlog")
        delta_ready = sem("delta_ready")
        du_ready = sem("du_ready")
        duT_psum = sem("duT_psum")
        du_high_ready = sem("du_high_ready")
        du_low_ready = sem("du_low_ready")
        b_split = sem("b_split")
        bd_high_ready = sem("bd_high_ready")
        bd_low_ready = sem("bd_low_ready")
        cdiag_ready = sem("cdiag_ready")
        c_psum = sem("c_psum")
        c_ready = sem("c_ready")
        dbu_ready = sem("dbu_ready")
        dA_ready = sem("dA_ready")
        scan_done = sem("scan_done")
        prod_ready = sem("prod_ready")
        prod_rest = sem("prod_rest")
        pairs_ready = sem("pairs_ready")
        reduced = sem("reduced")
        yg_ready = sem("yg_ready")
        y_psum = sem("y_psum")
        ar_psum = sem("ar_psum")
        top_ready = sem("top_ready")
        exp_ready = sem("exp_ready")
        g_ready = sem("g_ready")
        gT_psum = sem("gT_psum")
        gT_ready = sem("gT_ready")
        biased = sem("biased")
        base_psum = sem("base_psum")
        xq_psum = sem("xq_psum")
        xq_ready = sem("xq_ready")
        xqT_psum = sem("xqT_psum")
        xqT_lo = sem("xqT_lo")
        xqT_hi = sem("xqT_hi")
        xk_psum = sem("xk_psum")
        xk_lo = sem("xk_lo")
        xk_hi = sem("xk_hi")
        xkT_psum = sem("xkT_psum")
        xkT_lo = sem("xkT_lo")
        xkT_hi = sem("xkT_hi")
        score_psum = sem("score_psum")
        sbias_ready = sem("sbias_ready")
        prob_ready = sem("prob_ready")
        probT_psum = sem("probT_psum")
        probT_lo = sem("probT_lo")
        probT_hi = sem("probT_hi")
        xatt_psum = sem("xatt_psum")
        kv_psum = sem("kv_psum")
        aq_psum = sem("aq_psum")
        krot_ready = sem("krot_ready")
        krep_ready = sem("krep_ready")
        v_ready = sem("v_ready")
        akT_psum = sem("akT_psum")
        akT_ready = sem("akT_ready")
        qrot_ready = sem("qrot_ready")
        aqT_psum = sem("aqT_psum")
        aqT_ready = sem("aqT_ready")
        as_psum = sem("as_psum")
        hmax_ready = sem("hmax_ready")
        as_ready = sem("as_ready")
        ap_ready = sem("ap_ready")
        apT_psum = sem("apT_psum")
        apT_even = sem("apT_even")
        apT_odd = sem("apT_odd")
        pv_psum = sem("pv_psum")
        attn_ready = sem("attn_ready")
        attnT_psum = sem("attnT_psum")
        attnT_ready = sem("attnT_ready")
        ao_psum = sem("ao_psum")
        perm_f = sem("perm_f")
        iota_ready = sem("iota_ready")
        pick_ready = sem("pick_ready")
        place_ready = sem("place_ready")
        hs_high = sem("hs_high")
        hs_low = sem("hs_low")
        g_psum = sem("g_psum")
        picked_lo = sem("picked_lo")
        picked_hi = sem("picked_hi")
        gT_turned = sem("gT_turned")
        g_lo = sem("g_lo")
        g_hi = sem("g_hi")
        up_psum = sem("up_psum")
        hidden_ready = sem("hidden_ready")
        down_psum = sem("down_psum")
        o_high = sem("o_high")
        o_low = sem("o_low")
        placed = sem("placed")
        y_ready = sem("y_ready")

        last_use = [(ctx_coded, n + 1) for n in range(8)]
        middle = 0

        def uses(*signals):
            nonlocal middle
            for signal in signals:
                if signal is None:
                    middle += 1
                    last_use.append((unit_used, middle))
                else:
                    last_use.append(signal)

        for j in range(NB):
            uses(None, (proj_psum, j + 1))
        for nh in range(2):
            uses(None, None, None, (y_psum, nh + 1))
        uses(None, None, None, None)
        uses(None, (xq_psum, 1), None, (xq_psum, 2))
        uses(None, None, (xk_psum, 1), (xk_psum, 2))
        for signal in (score_psum, xatt_psum):
            for pair in range(2):
                uses(None)
                last_use.append(last_use[-1])
            uses((signal, 1), (signal, 1), (signal, 2), (signal, 2))
        uses(None, (kv_psum, 1))
        for signal in (aq_psum, ao_psum):
            uses(None, (signal, 1), None, (signal, 2))

        def slot(n):
            return ring[:, n % SLOTS, :].rearrange("p (k n) -> p k n", k=UK)

        def arrived(eng, n):
            eng.wait_ge(unit_in[n % SLOTS], 16 * (n // SLOTS + 1))

        def turn_bank(j):
            return 0 if j == NB - 1 else 3 + j % 2

        def du_bank(g):
            return 6 if g == 0 else 7

        def wide(ap, count):
            n = ap.shape[1]
            return ap.rearrange("p (u n) -> p u n", u=1).to_broadcast([P, count, n])

        def along(ap, count):
            n = ap.shape[1]
            return ap.rearrange("p (n u) -> p n u", u=1).to_broadcast([P, n, count])

        block = stack.enter_context(nc.Block())

        @block.sync
        def _(sp):
            sp.dma_start(x[:, :], dram["x"]).then_inc(x_in, 16)
            for n, (name, i) in enumerate(units):
                if n == 8:
                    sp.dma_start(small[:, 320:432], dram["chan"]).then_inc(mamba_in, 16)
                    sp.dma_start(rms_w, dram["rms_w"].to_broadcast([P, SSM])).then_inc(mamba_in, 16)
                    sp.dma_start(wxT, dram["wx"]).then_inc(mamba_in, 16)
                    sp.dma_start(wdtT[0:R, :], dram["wdt"]).then_inc(mamba_in, 16)
                    sp.dma_start(a_par, dram["a_par"]).then_inc(mamba_in, 16)
                if n >= SLOTS:
                    sp.wait_ge(*last_use[n - SLOTS])
                sp.dma_start(ring[:, n % SLOTS, :], dram[name][i]).then_inc(unit_in[n % SLOTS], 16)
            for nh in range(2):
                sp.wait_ge(y_ready, nh + 1)
                cols = slice(nh * UN, nh * UN + UN)
                sp.dma_start(out[:, cols], y_out[:, cols]).then_inc(out_done, 16)
            sp.wait_ge(out_done, 32)

        @block.gpsimd
        def _(pool):
            pool.dma_start(small[:, 160:304], dram["tables"]).then_inc(tables_in, 16)
            pool.memset(ident[:, :], 0.0).then_inc(const_zero, 1)
            pool.memset(minus_half, -0.5).then_inc(const_zero, 1)
            pool.memset(const_warm, 0.0).then_inc(const_ready, 1)
            pool.memset(ones64, 1.0).then_inc(const_ready, 1)
            pool.wait_ge(const_zero, 2)
            pool.affine_select(out=ident[:, :], in_=ident[:, :], compare_op=ALU.not_equal, fill=1.0, base=0,
                               pattern=[[-1, P]], channel_multiplier=1).then_inc(const_ready, 1)

            def rstd_of(n):
                pool.wait_ge(var_ready, n + 1)
                pool.tensor_tensor(rstd, var_eps, minus_half[:, 0:1], ALU.pow).then_inc(rstd_ready, 1)

            pool.wait_ge(const_ready, 3)
            rstd_of(0)
            pool.memset(ones, 1.0).then_inc(const_ready, 1)

            q_steps = [0]

            def q(ins):
                q_steps[0] += 1
                ins.then_inc(q_step, 1)
                pool.wait_ge(q_step, q_steps[0])

            pool.wait_ge(qneg_ready, 1)
            q(pool.tensor_scalar(q_s12, quant[:, 0:1], quant[:, 1:2], None, ALU.mult))
            q(pool.tensor_scalar(q_col, qneg[:, 0:1], q_s12, None, ALU.mult))
            pool.wait_ge(q_summed, 1)
            q(pool.tensor_scalar(q_row, qneg[:, 0:1], float(D), q_sum, ALU.mult, ALU.add))
            q(pool.tensor_scalar(q_row, q_row, qneg[:, 1:2], q_s12, ALU.mult, ALU.mult))
            pool.tensor_scalar(x[:, :], x[:, :], q_row, None, ALU.add).then_inc(x_offset, 1)

            rstd_of(1)
            pool.wait_ge(q_done, 2)
            pool.memset(uT[:, :, :, 0:CK - 1], 0.0).then_inc(edge_zero, 1)
            pool.memset(dA.rearrange("p s (n t) -> p (s n) t", t=L)[:, :, 0:1], 0.0).then_inc(edge_zero, 1)

            pool.wait_ge(ssm_sum, 1)
            pool.tensor_tensor(rms_inv, rms_var, minus_half[:, 0:3], ALU.pow).then_inc(ssm_inv, 1)
            pool.wait_ge(bc_ready, 2)
            pool.tensor_tensor(cdiag, wide(ident[:, :], NS), along(ssm[:, R + NS:SSM], P), ALU.mult).then_inc(cdiag_ready, 1)
            pool.wait_ge(b_split, 1)
            pool.tensor_tensor(bd_low, wide(ident[:, :], NS), along(b_low, P), ALU.mult).then_inc(bd_low_ready, 1)
            pool.wait_ge(projT_psum, 8)
            half = HN * P // 2
            for s in range(STEPS):
                pool.wait_ge(scan_done, s + 1)
                pool.wait_ge(c_ready, 4)
                prod = state[:, s % 3, :]
                c = cwide[:, HN * P * (s % 2):HN * P * (s % 2) + HN * P]
                pool.tensor_tensor(prod[:, OWN:], prod[:, OWN:], c[:, OWN:], ALU.mult).then_inc(prod_rest, 1)
                pool.wait_ge(prod_rest, s + 1)
                pool.wait_ge(prod_ready, s + 1)
                if s >= 3:
                    pool.wait_ge(reduced, s - 2)
                pool.tensor_tensor(pairs[:, s % 3, :], prod[:, 0:half], prod[:, half:], ALU.add).then_inc(pairs_ready, 1)

            rstd_of(2)
            pool.wait_ge(bias_in, 48)
            pool.wait_ge(h_ready, 6)
            pool.tensor_tensor(x[:, :], x[:, :], b_base, ALU.add).then_inc(biased, 1)
            rstd_of(3)
            pool.wait_ge(y_psum, 2)
            pool.dma_start(permi, dram["perm_row"].to_broadcast([P, D])).then_inc(perm_in, 16)
            pool.dma_start(perm_coli, dram["perm_col"]).then_inc(perm_in, 16)
            pool.iota(iota, pattern=[[1, D]], base=0, channel_multiplier=0,
                      allow_small_or_imprecise_dtypes=True).then_inc(iota_ready, 1)
            pool.wait_ge(perm_in, 32)
            pool.tensor_copy(perm_row, permi).then_inc(perm_f, 1)
            pool.tensor_copy(perm_col, perm_coli).then_inc(perm_f, 1)
            pool.wait_ge(perm_f, 2)
            pool.wait_ge(tables_in, 16)
            for k in range(KT):
                pool.tensor_scalar(onehot[:, k, :], perm_row, row_no[:, k:k + 1], None, ALU.is_equal).then_inc(pick_ready, 1)
            rstd_of(4)
            for r in range(GQ):
                pool.wait_ge(hmax_ready, r + 1)
                v = aprob[:, r, :, :]
                pool.tensor_tensor(v, v, along(hmax[:, r, :], L), ALU.subtract).then_inc(as_ready, 1)
            rstd_of(5)

        @block.scalar
        def _(act):
            steps = [0]

            def step(ins):
                steps[0] += 1
                ins.then_inc(act_step, 1)
                act.wait_ge(act_step, steps[0])

            act.dma_start(quant, dram["quant"].to_broadcast([P, 4])).then_inc(quant_in, 16)
            act.dma_start(tri, dram["tri"]).then_inc(tri_in, 16)

            act.wait_ge(const_ready, 3)
            step(act.activation(const_warm, const_warm, ACT.Identity))
            act.wait_ge(scales_ready, 1)
            for n in range(8):
                if n == 2:
                    act.wait_ge(q1_ready, 1)
                    act.activation(codes_junk, h[:, :], ACT.Copy, accum_out=q_sum).then_inc(q_summed, 1)
                arrived(act, n)
                act.activation(ring[:, n % SLOTS, :], ring[:, n % SLOTS, :], ACT.Identity,
                               bias=quant[:, 3:4], scale=qrec[:, 1:2]).then_inc(ctx_scaled, 1)

            def evacuate_hT(n):
                act.wait_ge(hT_psum, 2 * n - 1)
                act.activation(hT[:, 0:4, :], psum[:, 6, :], ACT.Copy).then_inc(hT_lo, 1)

            evacuate_hT(1)

            def proj_copy(j):
                act.wait_ge(proj_psum, j + 1)
                if j >= 3:
                    act.wait_ge(projT_psum, j - 2)
                act.activation(proj[:, j % 3, :], psum[:, j % 3, :], ACT.Copy).then_inc(proj_sb, 1)

            def half_tanh(n):
                if n < NG:
                    act.wait_ge(conv_half, n + 1)
                else:
                    act.wait_ge(projT_read, n + 1)
                if n >= 2:
                    act.wait_ge(gated, n - 1)
                v = (uc if n < NG else sg)[:, GD * (n % NG):GD * (n % NG) + GD, :].rearrange("p k t -> p (k t)")
                act.activation(tanh[:, n % 2, :], v, ACT.Tanh).then_inc(tanh_ready, 1)

            def softplus_exp(g):
                act.wait_ge(z_abs, g + 1)
                v = delta[:, GD * g:GD * g + GD, :]
                act.activation(v, v, ACT.Exp, scale=-1.0).then_inc(z_exp, 1)

            def softplus_log(g):
                act.wait_ge(z_exp, g + 1)
                v = delta[:, GD * g:GD * g + GD, :]
                act.activation(v, v, ACT.Ln, bias=1.0).then_inc(softlog, 1)

            def du_copy(g):
                act.wait_ge(duT_psum, g + 1)
                act.activation(du_high[:, UN * g:UN * g + UN], psum[:, du_bank(g), :], ACT.Copy).then_inc(du_high_ready, 1)

            def c_copy(c):
                act.wait_ge(c_psum, c + 1)
                act.activation(cwide[:, UN * c:UN * c + UN], psum[:, 7 - 2 * (c % 2), :], ACT.Copy).then_inc(c_ready, 1)

            proj_copy(0)
            proj_copy(1)
            half_tanh(0)
            proj_copy(2)
            half_tanh(1)
            proj_copy(3)
            half_tanh(2)
            half_tanh(3)
            proj_copy(4)
            act.wait_ge(dtT_psum, 1)
            act.activation(dtT[0:R, :], psum[0:R, 5, 128:256], ACT.Copy).then_inc(dtT_ready, 1)
            softplus_exp(0)
            softplus_exp(1)
            softplus_exp(2)
            softplus_exp(3)
            proj_copy(5)
            half_tanh(4)
            for g in range(NG):
                softplus_log(g)
            for c in range(4):
                c_copy(c)
            act.wait_ge(edge_zero, 2)

            def decay(s):
                k = s // 2
                act.wait_ge(delta_ready, k // GD + 1)
                if s >= 3:
                    act.wait_ge(scan_done, s - 2)
                for n in range(HN):
                    to = dA[:, s % 3, n * P:n * P + P].rearrange("p (b t) -> p b t", b=B)[:, :, 1:]
                    of = delta[:, k, :].rearrange("p (b t) -> p b t", b=B)[:, :, 1:]
                    state_no = HN * (s % 2) + n
                    last = act.activation(to, of, ACT.Exp, scale=a_par[:, k, state_no:state_no + 1])
                last.then_inc(dA_ready, 1)

            decay(0)
            proj_copy(6)
            du_copy(0)
            decay(1)
            decay(2)
            proj_copy(7)
            for s in range(3, STEPS):
                decay(s)
                if s in (3, 6, 9):
                    du_copy(s // 3)
                if s in (4, 7, 10):
                    half_tanh(5 + s // 3 - 1)
                if s == 12:
                    act.wait_ge(du_low_ready, NG)
                    act.dma_start(lora_b, dram["lora_b"]).then_inc(rank_in, 16)
                    act.dma_start(w_ar, dram["w_ar"]).then_inc(rank_in, 16)
                    act.dma_start(b_base, dram["b_base"].to_broadcast([P, D])).then_inc(bias_in, 16)
                    act.dma_start(bq, dram["bq"].to_broadcast([P, D])).then_inc(bias_in, 16)
                    act.dma_start(bk, dram["bk"].to_broadcast([P, D])).then_inc(bias_in, 16)

            evacuate_hT(2)
            act.wait_ge(top_ready, 1)
            act.activation(gate, logit, ACT.Exp, bias=top).then_inc(exp_ready, 1)
            act.wait_ge(gT_psum, 1)
            act.activation(lora_gT, psum[:, 3, 0:P], ACT.Copy).then_inc(gT_ready, 1)

            evacuate_hT(3)
            act.wait_ge(xqT_psum, 1)
            act.activation(xqT[:, 0:4, :], psum[:, 4, :], ACT.Copy).then_inc(xqT_lo, 1)
            act.wait_ge(xk_psum, 1)
            act.activation(xk[:, 0:UN], psum[:, 2, :], ACT.Copy).then_inc(xk_lo, 1)
            act.wait_ge(xkT_psum, 1)
            act.activation(xkT[:, 0:4, :], psum[:, 6, :], ACT.Copy).then_inc(xkT_lo, 1)
            act.wait_ge(sbias_ready, 1)
            for nh in range(2):
                act.activation(prob[:, nh * UN:nh * UN + UN], psum[:, nh, :], ACT.Exp, bias=sbias, scale=XSCALE,
                               accum_out=ssum2[:, nh:nh + 1]).then_inc(prob_ready, 1)
            act.wait_ge(probT_psum, 1)
            act.activation(probT[:, 0:4, :], psum[:, 4, :], ACT.Copy).then_inc(probT_lo, 1)

            evacuate_hT(4)
            act.wait_ge(krot_ready, 1)
            for r in range(GQ):
                last = act.activation(krep[:, :, r, :], krot.rearrange("p (g d) -> p g d", g=HKV), ACT.Copy)
            last.then_inc(krep_ready, 1)
            for b in range(B):
                rows = slice(L * b, L * b + L)
                to = vdup[rows, b, :].rearrange("p (h d) -> p h d", h=HKV)
                act.activation(to[:, :, 0:DH], psum[rows, 0, 256:512].rearrange("p (h d) -> p h d", h=HKV),
                               ACT.Copy).then_inc(v_ready, 1)
            act.wait_ge(v_ready, 3)
            act.dma_start(vdup[L:P, 0, :], vdup[0:L, 0, :]).then_inc(vdup_in, 16)
            act.dma_start(vdup[0:L, 1, :], vdup[L:P, 1, :]).then_inc(vdup_in, 16)
            for n in range(2):
                act.wait_ge(akT_psum, n + 1)
                act.activation(akT[:, 4 * n:4 * n + 4, :], psum[:, 4 + n, :], ACT.Copy).then_inc(akT_ready, 1)
            for n in range(2):
                act.wait_ge(aqT_psum, n + 1)
                act.activation(aqT[:, 4 * n:4 * n + 4, :], psum[:, 6 - 2 * n, :], ACT.Copy).then_inc(aqT_ready, 1)
            for r in range(GQ):
                act.wait_ge(as_ready, r + 1)
                act.activation(aprob[:, r, :, :], aprob[:, r, :, :], ACT.Exp).then_inc(ap_ready, 1)
                if r % 2:
                    act.wait_ge(apT_psum, r)
                    act.activation(aprobT[:, 4 * r - 4:4 * r, :], psum[:, 3 + r, :], ACT.Copy).then_inc(apT_even, 1)
            act.wait_ge(attnT_psum, 1)
            act.activation(attnT[:, 0:4, :], psum[:, 6, :], ACT.Copy).then_inc(attnT_ready, 1)

            act.wait_ge(hT_psum, 9)
            act.activation(split[:, 0, 0:4, :], psum[:, 6, :], ACT.Copy).then_inc(hs_high, 1)
            act.wait_ge(g_psum, 1)
            act.activation(picked[:, 0:UN], psum[:, 4, :], ACT.Copy).then_inc(picked_lo, 1)
            act.wait_ge(gT_turned, 1)
            act.activation(gT[:, 0:4, :], psum[:, 6, :], ACT.Copy).then_inc(g_lo, 1)
            for q in range(4):
                for r in range(2):
                    act.wait_ge(up_psum, q + 1)
                    to = hidden[:, 4 * q + r:4 * q + r + 3:2, :, :]
                    act.activation(to, psum[:, 4 * r + q, :].rearrange("p (h m t) -> p h m t", h=2, m=2),
                                   ACT.Gelu).then_inc(hidden_ready, 1)
            act.wait_ge(down_psum, 1)
            act.activation(split[:, 0, 0:4, :], psum[:, 0, :], ACT.Copy).then_inc(o_high, 1)

        @block.tensor
        def _(pe):
            def transpose4(bank, tile, first_col, signal):
                for k in range(4):
                    c = first_col + P * k
                    last = pe.transpose(psum[:, bank, P * k:P * k + P], tile[:, c:c + P], ident[:, :])
                last.then_inc(signal, 1)

            def products(bank, left, u, k0, start, stop, signal=unit_used):
                arrived(pe, u)
                for k in range(UK):
                    last = pe.matmul(psum[:, bank, :], left[:, k0 + k, :], slot(u)[:, k, :],
                                     start=(start and k == 0), stop=(stop and k == UK - 1))
                last.then_inc(signal, 1)

            pe.wait_ge(const_ready, 3)
            for half in range(2):
                pe.wait_ge(q1_ready, 1)
                transpose4(6 + half, h, UN * half, q1_psum)
            pe.wait_ge(q1T_ready, 2)
            for nh in range(2):
                for kh in range(2):
                    for b in range(B):
                        u = 4 * nh + 2 * kh + b
                        pe.wait_ge(ctx_coded, u + 1)
                        rows = slice(L * b, L * b + L)
                        for k in range(UK):
                            right = q2[:, u, UN * k:UN * k + UN]
                            at = dict(start=(kh == 0 and k == 0), stop=(kh == 1 and k == UK - 1))
                            pe.matmul(psum[rows, nh, :], q1T[:, UK * kh + k, rows], right, **at)
                            last = pe.matmul(psum[rows, 2 + nh, :], ones64, right, **at)
                last.then_inc(q_done, 1)

            def transpose_h(n):
                for half in range(2):
                    pe.wait_ge(h_ready, 2 * n + half + 1)
                    transpose4(6 + half, h, UN * half, hT_psum)

            transpose_h(1)

            def turn(j):
                pe.wait_ge(proj_sb, j + 1)
                if j >= 2:
                    pe.wait_ge(projT_read, j - 1)
                transpose4(turn_bank(j), proj[:, j % 3, :], 0, projT_psum)

            def small_projection(g):
                if g == 0:
                    pe.wait_ge(mamba_in, 80)
                pe.wait_ge(gated, g + 1)
                for k in range(GD * g, GD * g + GD):
                    last = pe.matmul(psum[:, 5, 0:SSM], uc[:, k, :], wxT[:, k, :], start=(k == 0), stop=(k == DT - 1))
                if g == NG - 1:
                    last.then_inc(ssm_psum, 1)

            def time_steps(g):
                if g == 0:
                    pe.wait_ge(dtT_ready, 1)
                if g >= 2:
                    pe.wait_ge(z_read, g - 1)
                for k in range(GD * g, GD * g + GD):
                    last = pe.matmul(psum[:, 6 + g % 2, P * (k % GD):P * (k % GD) + P], wdtT[0:R, P * k:P * k + P],
                                     dtT[0:R, :], start=True, stop=True)
                last.then_inc(z_psum, 1)

            def turn_dt():
                pe.wait_ge(dt_normed, 1)
                pe.transpose(psum[0:R, 5, 128:256], ssm[:, 0:R], ident[:, :]).then_inc(dtT_psum, 1)

            def spread_c(c):
                if c == 0:
                    pe.wait_ge(cdiag_ready, 1)
                    pe.wait_ge(z_read, 4)
                if c >= 2:
                    pe.wait_ge(c_ready, c - 1)
                pe.matmul(psum[:, 7 - 2 * (c % 2), :], ones, cdiag[:, 4 * c:4 * c + 4, :], start=True,
                          stop=True).then_inc(c_psum, 1)

            def turn_du(g):
                pe.wait_ge(du_ready, g + 1)
                if g == 0:
                    pe.wait_ge(z_read, 3)
                elif g == 1:
                    pe.wait_ge(c_ready, 4)
                else:
                    pe.wait_ge(du_low_ready, g)
                transpose4(du_bank(g), zbuf[:, g, :], 0, duT_psum)

            def scan_input(s):
                if s % (2 * GD) == 0:
                    pe.wait_ge(du_low_ready, s // (2 * GD) + 1)
                if s == 0:
                    pe.wait_ge(bd_high_ready, 1)
                    pe.wait_ge(bd_low_ready, 1)
                if s == 0:
                    pe.wait_ge(projT_read, 7)
                if s == 1:
                    pe.wait_ge(c_ready, 4)
                if s == 2:
                    pe.wait_ge(projT_read, 8)
                if s >= 3:
                    pe.wait_ge(scan_done, s - 2)
                k = s // 2
                left = slice(P * k, P * k + P)
                for c in range(2):
                    right = slice(HN * (s % 2) + 4 * c, HN * (s % 2) + 4 * c + 4)
                    to = psum[:, 2 * ((s + 1) % 3) + c, :]
                    pe.matmul(to, du_high[:, left], bd_high[:, right, :], start=True, stop=False)
                    pe.matmul(to, du_high[:, left], bd_low[:, right, :], start=False, stop=False)
                    last = pe.matmul(to, du_low[:, left], bd_high[:, right, :], start=False, stop=True)
                last.then_inc(dbu_ready, 1)

            between = {}
            for j in range(NG - 1):
                between[KT * (j + 1) + 2] = [(turn, j)]
            gates = KT * NG
            between[gates + 2] = [(turn, 3)]
            between[gates + 4] = [(small_projection, g) for g in range(3)]
            between[gates + 7] = [(small_projection, 3)]
            between[gates + 9] = [(turn, 4)]
            between[gates + 10] = [(turn_dt,)]
            between[gates + 11] = [(time_steps, 0), (time_steps, 1)]
            between[gates + 13] = [(time_steps, 2)]
            between[gates + 14] = [(time_steps, 3)]
            between[gates + 17] = [(spread_c, 0), (spread_c, 1)]
            between[gates + 19] = [(turn, 5)]
            between[gates + 21] = [(spread_c, 2), (spread_c, 3)]
            between[gates + 23] = [(turn_du, 0)]
            between[gates + 27] = [(turn, 6)]
            between[gates + 29] = [(scan_input, 0)]
            between[gates + 31] = [(scan_input, 1)]
            w_in = first["w_in"]
            for j in range(NB):
                if j >= 3:
                    pe.wait_ge(proj_sb, j - 2)
                for k in range(KT):
                    if j == 0 and k % UK == 0:
                        pe.wait_ge(*((hT_hi if k else hT_lo), 1))
                    for hook, *which in between.get(KT * j + k, []):
                        hook(*which)
                    u = w_in + 2 * j + k // UK
                    if k % UK == 0:
                        arrived(pe, u)
                    last = pe.matmul(psum[:, j % 3, :], hT[:, k, :], slot(u)[:, k % UK, :], start=(k == 0), stop=(k == KT - 1))
                    if k % UK == UK - 1:
                        last.then_inc(proj_psum if k == KT - 1 else unit_used, 1)

            def state_sum(s):
                pe.wait_ge(pairs_ready, s + 1)
                k = s // 2
                g = k // GD
                if s == 2 * GD:
                    pe.wait_ge(du_low_ready, NG)
                if g >= 2:
                    pe.wait_ge(yg_ready, g - 1)
                cols = slice(P * (k % GD), P * (k % GD) + P)
                for n in range(HN // 2):
                    last = pe.matmul(psum[:, 6 + g % 2, cols], ident[:, :], pairs[:, s % 3, P * n:P * n + P],
                                     start=(s % 2 == 0 and n == 0), stop=(s % 2 == 1 and n == HN // 2 - 1))
                last.then_inc(reduced, 1)

            turn(7)
            for s in range(STEPS):
                if s >= 2:
                    scan_input(s)
                if s in (1, 5, 8):
                    turn_du({1: 1, 5: 2, 8: 3}[s])
                if s >= 3:
                    state_sum(s - 3)

            def output(nh, g, k):
                if k % GD == 0:
                    pe.wait_ge(yg_ready, g + 1)
                    arrived(pe, first["w_out"] + NG * nh + g)
                last = pe.matmul(psum[:, nh, :], sg[:, GD * g + k, :], slot(first["w_out"] + NG * nh + g)[:, k, :],
                                 start=(g == 0 and k == 0), stop=(g == NG - 1 and k == GD - 1))
                if k == GD - 1:
                    last.then_inc(y_psum if g == NG - 1 else unit_used, 1)

            pe.wait_ge(scan_done, STEPS - 2)
            state_sum(STEPS - 3)
            output(0, 0, 0)
            output(0, 0, 1)
            state_sum(STEPS - 2)
            output(0, 0, 2)
            output(0, 0, 3)
            state_sum(STEPS - 1)
            for nh in range(2):
                for g in range(NG):
                    if (nh, g) != (0, 0):
                        for k in range(GD):
                            output(nh, g, k)

            transpose_h(2)
            for nh in range(2):
                for kh in range(2):
                    pe.wait_ge(*((hT_hi if kh else hT_lo), 2))
                    products(nh, hT, first["w_base"] + 2 * nh + kh, UK * kh, kh == 0, False)
                    if nh == 0 and kh == 0:
                        pe.wait_ge(rank_in, 32)
                        pe.wait_ge(hT_hi, 2)
                        for k in range(KT):
                            last = pe.matmul(psum[:, 2, 0:NE * RANK + NE], hT[:, k, :], w_ar[:, k, :], start=(k == 0),
                                             stop=(k == KT - 1))
                        last.then_inc(ar_psum, 1)
                if nh == 0:
                    pe.wait_ge(g_ready, 1)
                    pe.transpose(psum[:, 3, 0:P], lora_g.rearrange("p e r -> p (e r)"), ident[:, :]).then_inc(gT_psum, 1)
                    pe.wait_ge(gT_ready, 1)
                pe.matmul(psum[:, nh, :], lora_gT, lora_b[:, UN * nh:UN * nh + UN], start=False, stop=True).then_inc(base_psum, 1)

            transpose_h(3)
            xwq, xwk = first["x_wq"], first["x_wk"]
            pe.wait_ge(hT_lo, 3)
            products(0, hT, xwq, 0, True, False)
            pe.wait_ge(hT_hi, 3)
            products(0, hT, xwq + 1, 4, False, True, xq_psum)
            products(1, hT, xwq + 2, 0, True, False)
            pe.wait_ge(xq_ready, 1)
            transpose4(4, xq, 0, xqT_psum)
            products(1, hT, xwq + 3, 4, False, True, xq_psum)
            pe.wait_ge(xqT_lo, 1)
            products(2, xqT, xwk, 0, True, False)
            pe.wait_ge(xq_ready, 2)
            transpose4(5, xq, UN, xqT_psum)
            products(3, xqT, xwk + 1, 0, True, False)
            pe.wait_ge(xqT_hi, 1)
            products(2, xqT, xwk + 2, 4, False, True, xk_psum)
            products(3, xqT, xwk + 3, 4, False, True, xk_psum)
            pe.wait_ge(xk_lo, 1)
            transpose4(6, xk, 0, xkT_psum)
            pe.wait_ge(xk_hi, 1)
            transpose4(7, xk, UN, xkT_psum)

            def batched(bank, left, u0, kh, signal):
                arrived(pe, u0)
                arrived(pe, u0 + 1)
                for k in range(UK):
                    for b in range(B):
                        last = pe.matmul(psum[L * b:L * b + L, bank, :], left[:, UK * kh + k, L * b:L * b + L],
                                         slot(u0 + b)[:, k, :], start=(kh == 0 and k == 0), stop=(kh == 1 and k == UK - 1))
                last.then_inc(signal if kh else unit_used, 1)

            pe.wait_ge(xkT_lo, 1)
            for kh in range(2):
                if kh:
                    pe.wait_ge(xkT_hi, 1)
                for nh in range(2):
                    batched(nh, xkT, first["ctx_t"] + 4 * kh + 2 * nh, kh, score_psum)
            for half in range(2):
                pe.wait_ge(prob_ready, half + 1)
                transpose4(4 + half, prob, UN * half, probT_psum)
            pe.wait_ge(probT_lo, 1)
            for kh in range(2):
                if kh:
                    pe.wait_ge(probT_hi, 1)
                for nh in range(2):
                    batched(2 + nh, probT, first["ctx_again"] + 4 * kh + 2 * nh, kh, xatt_psum)

            transpose_h(4)
            pe.wait_ge(hT_lo, 4)
            products(0, hT, first["a_wkv"], 0, True, False)
            pe.wait_ge(hT_hi, 4)
            products(0, hT, first["a_wkv"] + 1, 4, False, True, kv_psum)
            awq = first["a_wq"]
            products(1, hT, awq, 0, True, False)
            products(1, hT, awq + 1, 4, False, True, aq_psum)
            pe.wait_ge(krep_ready, 1)
            transpose4(4, krep.rearrange("p g r d -> p (g r d)"), 0, akT_psum)
            transpose4(5, krep.rearrange("p g r d -> p (g r d)"), UN, akT_psum)
            products(7, hT, awq + 2, 0, True, False)
            pe.wait_ge(qrot_ready, 1)
            transpose4(6, qrot, 0, aqT_psum)
            products(7, hT, awq + 3, 4, False, True, aq_psum)
            pe.wait_ge(akT_ready, 2)
            pe.wait_ge(v_ready, 3)
            def scores(r, half):
                for j in range(4 * half, 4 * half + 4):
                    for b in range(B):
                        rows = slice(DH * r, DH * r + DH)
                        cols = slice(L * b, L * b + L)
                        last = pe.matmul(psum[cols, r, L * j:L * j + L], aqT[rows, j, cols], akT[rows, j, cols],
                                         start=True, stop=True, tile_position=(DH * r, L * b))
                if half:
                    last.then_inc(as_psum, 1)

            pe.wait_ge(aqT_ready, 1)
            for r in range(GQ):
                scores(r, 0)
            pe.wait_ge(qrot_ready, 2)
            transpose4(4, qrot, UN, aqT_psum)
            pe.wait_ge(aqT_ready, 2)
            for r in range(GQ):
                scores(r, 1)
            flat = aprob.rearrange("p r j s -> p r (j s)")

            def turn_prob(r):
                pe.wait_ge(ap_ready, r + 1)
                transpose4(4 + r, flat[:, r, :], 0, apT_psum)

            def weighted_values(r):
                pe.wait_ge(*((apT_odd if r % 2 else apT_even), r // 2 + 1))
                if r % 2 == 0:
                    pe.wait_ge(hmax_ready, 3 + r // 2)
                for j in range(HKV):
                    odd = j % 2
                    rows = slice(L * odd, L * odd + L)
                    at = (DH + 1) * (4 * (r % 2) + j // 2)
                    for b in range(B):
                        last = pe.matmul(psum[L * b:L * b + L, 2 * odd + r // 2, at:at + DH + 1],
                                         aprobT[rows, 4 * r + j // 2, L * b:L * b + L],
                                         vdup[rows, b, (DH + 1) * j:(DH + 1) * (j + 1)],
                                         start=True, stop=True, tile_position=(L * odd, L * b))
                if r % 2:
                    last.then_inc(pv_psum, 1)

            turn_prob(0)
            turn_prob(1)
            pe.wait_ge(vdup_in, 32)
            weighted_values(0)
            turn_prob(2)
            weighted_values(1)
            turn_prob(3)
            weighted_values(2)
            weighted_values(3)
            pe.wait_ge(attn_ready, 1)
            transpose4(6, attn, 0, attnT_psum)
            transpose4(7, attn, UN, attnT_psum)
            pe.wait_ge(attnT_ready, 2)
            for nh in range(2):
                for kh in range(2):
                    products(nh, attnT, first["a_wo"] + 2 * nh + kh, UK * kh, kh == 0, kh == 1,
                             ao_psum if kh else unit_used)

            transpose_h(5)
            pe.wait_ge(pick_ready, KT)
            for nh in range(2):
                for part, signal in enumerate((hs_high, hs_low)):
                    for k in range(KT):
                        if nh == 0 and k % 4 == 0:
                            pe.wait_ge(signal, k // 4 + 1)
                        last = pe.matmul(psum[:, 4 + nh, :], split[:, part, k, :], onehot[:, k, UN * nh:UN * nh + UN],
                                         start=(part == 0 and k == 0), stop=(part == 1 and k == KT - 1))
                last.then_inc(g_psum, 1)
            for half in range(2):
                pe.wait_ge(picked_hi if half else picked_lo, 1)
                transpose4(6 + half, picked, UN * half, gT_turned)
            up = ring[:, first["mlp_up"] % SLOTS, :].rearrange("p (a m) -> p a m", a=MH // 2)
            down = ring[:, first["mlp_down"] % SLOTS, :].rearrange("p (m h d) -> p m h d", m=2, h=MH)
            arrived(pe, first["mlp_up"])
            arrived(pe, first["mlp_down"])
            for a in range(MH // 2):
                pe.wait_ge(g_hi if a >= 4 else g_lo, 1)
                for m in range(2):
                    for r in range(2):
                        rows = slice(MD * r, MD * r + MD)
                        at = 256 * (a % 2) + P * m
                        last = pe.matmul(psum[:, 4 * r + a // 2, at:at + P], up[rows, a, P * m:P * m + P], gT[rows, a, :],
                                         start=True, stop=True)
                if a % 2:
                    last.then_inc(up_psum, 1)
            for a in range(MH // 2):
                pe.wait_ge(hidden_ready, 2 * (a // 2 + 1))
                for m in range(2):
                    for r in range(2):
                        last = pe.matmul(psum[MD * r:MD * r + MD, a // 4, P * (a % 4):P * (a % 4) + P], down[:, m, 2 * a + r, :],
                                         hidden[:, 2 * a + r, m, :], start=(m == 0), stop=(m == 1))
                if a % 4 == 3:
                    last.then_inc(down_psum, 1)
            for nh in range(2):
                for part, signal in enumerate((o_high, o_low)):
                    for k in range(KT):
                        if nh == 0 and k % 4 == 0:
                            pe.wait_ge(signal, k // 4 + 1)
                        if nh == 0 and part == 0:
                            pe.wait_ge(place_ready, k + 1)
                        last = pe.matmul(psum[:, 2 + nh, :], split[:, part, k, :], onehot[:, k, UN * nh:UN * nh + UN],
                                         start=(part == 0 and k == 0), stop=(part == 1 and k == KT - 1))
                last.then_inc(placed, 1)

        @block.vector
        def _(dve):
            steps = [0]

            def step(ins):
                steps[0] += 1
                ins.then_inc(dve_step, 1)
                dve.wait_ge(dve_step, steps[0])

            def halves(nh):
                return slice(UN * nh, UN * nh + UN)

            def statistics(nh):
                dve.bn_stats(stats[:, nh, :], x[:, halves(nh)]).then_inc(stats_ready, 1)

            def norm(n):
                dve.wait_ge(stats_ready, 2 * n + 2)
                step(dve.bn_aggr(mv, stats.rearrange("p a b -> p (a b)")))
                dve.tensor_scalar(var_eps, mv[:, 1:2], LN_EPS, None, ALU.add).then_inc(var_ready, 1)
                dve.wait_ge(rstd_ready, n + 1)
                for nh in range(2):
                    dve.tensor_scalar(h[:, halves(nh)], x[:, halves(nh)], mv[:, 0:1], rstd, ALU.subtract,
                                      ALU.mult).then_inc(h_ready, 1)

            def finish_hT(n):
                dve.wait_ge(hT_psum, 2 * n)
                dve.tensor_copy(hT[:, 4:8, :], psum[:, 7, :]).then_inc(hT_hi, 1)

            updates = [0]

            def x_updated(ins):
                ins.then_inc(x_ready, 1)
                updates[0] += 1
                dve.wait_ge(x_ready, updates[0])
                statistics((updates[0] - 1) % 2)

            def add_to_x(nh, bank):
                x_updated(dve.tensor_tensor(x[:, halves(nh)], x[:, halves(nh)], psum[:, bank, :], ALU.add))

            dve.wait_ge(quant_in, 16)
            dve.reciprocal(qrec, quant[:, 0:2]).then_inc(scales_ready, 1)
            dve.wait_ge(x_in, 16)
            statistics(0)
            statistics(1)
            norm(0)
            dve.wait_ge(h_ready, 2)
            step(dve.tensor_scalar(h[:, :], h[:, :], qrec[:, 0:1], quant[:, 2:3], ALU.mult, ALU.add))
            step(dve.tensor_scalar(h[:, :], h[:, :], ROUND, ROUND, ALU.add, ALU.max))
            dve.tensor_scalar(h[:, :], h[:, :], ROUND + QMAX, ROUND + QMID, ALU.min, ALU.subtract).then_inc(q1_ready, 1)
            dve.tensor_scalar(qneg, quant[:, 2:4], -1.0, QMID, ALU.mult, ALU.add).then_inc(qneg_ready, 1)

            def code(n):
                dve.wait_ge(ctx_scaled, n + 1)
                v = ring[:, n % SLOTS, :]
                step(dve.tensor_scalar(v, v, ROUND, ROUND, ALU.add, ALU.max))
                dve.tensor_scalar(q2[:, n, :], v, ROUND + QMAX, ROUND + QMID, ALU.min, ALU.subtract).then_inc(ctx_coded, 1)

            code(0)
            for half in range(2):
                dve.wait_ge(q1_psum, half + 1)
                dve.tensor_copy(q1T[:, 4 * half:4 * half + 4, :], psum[:, 6 + half, :]).then_inc(q1T_ready, 1)
            code(1)
            for n in range(2, 8):
                code(n)
            for nh in range(2):
                if nh == 0:
                    dve.wait_ge(x_offset, 1)
                dve.wait_ge(q_done, nh + 1)
                step(dve.scalar_tensor_tensor(out=x[:, halves(nh)], in0=psum[:, 2 + nh, :], scalar=q_col, in1=x[:, halves(nh)],
                                              op0=ALU.mult, op1=ALU.add))
                x_updated(dve.scalar_tensor_tensor(out=x[:, halves(nh)], in0=psum[:, nh, :], scalar=q_s12,
                                                   in1=x[:, halves(nh)], op0=ALU.mult, op1=ALU.add))

            norm(1)
            finish_hT(1)
            dve.wait_ge(mamba_in, 80)
            dve.wait_ge(edge_zero, 1)

            def conv(g):
                dve.wait_ge(projT_psum, g + 1)
                tiles = range(GD * g, GD * g + GD)
                dve.tensor_copy(uT[:, GD * g:GD * g + GD, :, CK - 1:],
                                psum[:, turn_bank(g), :].rearrange("p (k b t) -> p k b t", k=GD, b=B)).then_inc(projT_read, 1)
                dve.wait_ge(projT_read, g + 1)
                for j in range(CK):
                    for k in tiles:
                        to = uc[:, k, :].rearrange("p (b t) -> p b t", b=B)
                        tap = uT[:, k, :, j:j + L]
                        if j == 0:
                            last = dve.tensor_scalar(to, tap, conv_w[:, k, 0:1], conv_b[:, k:k + 1], ALU.mult, ALU.add)
                        else:
                            last = dve.scalar_tensor_tensor(out=to, in0=tap, scalar=conv_w[:, k, j:j + 1], in1=to,
                                                            op0=ALU.mult, op1=ALU.add)
                    if j < CK - 1:
                        step(last)
                last.then_inc(conv_half, 1)

            def silu(n):
                dve.wait_ge(tanh_ready, n + 1)
                v = (uc if n < NG else sg)[:, GD * (n % NG):GD * (n % NG) + GD, :].rearrange("p k t -> p (k t)")
                dve.scalar_tensor_tensor(out=v, in0=tanh[:, n % 2, :], scalar=1.0, in1=v, op0=ALU.add,
                                         op1=ALU.mult).then_inc(gated, 1)

            def gate_copy(g):
                n = NG + g
                dve.wait_ge(projT_psum, n + 1)
                v = sg[:, GD * g:GD * g + GD, :].rearrange("p k t -> p (k t)")
                dve.tensor_scalar(v, psum[:, turn_bank(n), :], 0.5, None, ALU.mult).then_inc(projT_read, 1)

            step(dve.tensor_scalar(small[:, 320:400], small[:, 320:400], 0.5, None, ALU.mult))
            conv(0)
            conv(1)
            silu(0)
            conv(2)
            silu(1)
            silu(2)
            conv(3)
            silu(3)
            dve.wait_ge(ssm_psum, 1)
            step(dve.tensor_copy(ssm, psum[:, 5, 0:SSM]))
            parts = [(0, R), (R, R + NS), (R + NS, SSM)]
            for i, (a, c) in enumerate(parts):
                step(dve.tensor_tensor_reduce(out=rms_junk[:, 0:c - a], in0=ssm[:, a:c], in1=ssm[:, a:c], scale=1.0, scalar=0.0,
                                              op0=ALU.mult, op1=ALU.add, accum_out=rms_sum[:, i:i + 1]))
            for i, (a, c) in enumerate(parts):
                last = dve.tensor_scalar(rms_var[:, i:i + 1], rms_sum[:, i:i + 1], 1.0 / (c - a), RMS_EPS, ALU.mult, ALU.add)
            last.then_inc(ssm_sum, 1)
            dve.wait_ge(ssm_inv, 1)
            for i, (a, c) in enumerate(parts):
                dve.scalar_tensor_tensor(out=ssm[:, a:c], in0=ssm[:, a:c], scalar=rms_inv[:, i:i + 1], in1=rms_w[:, a:c],
                                         op0=ALU.mult, op1=ALU.mult).then_inc(dt_normed if i == 0 else bc_ready, 1)
            dve.wait_ge(bc_ready, 2)
            step(dve.tensor_copy(b_high[:, :], ssm[:, R:R + NS]))
            dve.tensor_tensor(b_low, ssm[:, R:R + NS], b_high[:, :].bitcast(F32), ALU.subtract).then_inc(b_split, 1)
            dve.tensor_tensor(bd_high, wide(ident[:, :], NS), along(ssm[:, R:R + NS], P), ALU.mult).then_inc(bd_high_ready, 1)

            def softplus_in(g):
                dve.wait_ge(z_psum, g + 1)
                z = zbuf[:, g, :].rearrange("p (k t) -> p k t", k=GD)
                dve.tensor_tensor(z, psum[:, 6 + g % 2, :].rearrange("p (k t) -> p k t", k=GD),
                                  along(dt_b[:, GD * g:GD * g + GD], P), ALU.add).then_inc(z_read, 1)
                dve.wait_ge(z_read, g + 1)
                dve.scalar_tensor_tensor(out=delta[:, GD * g:GD * g + GD, :], in0=z, scalar=-1.0, in1=z, op0=ALU.mult,
                                         op1=ALU.max).then_inc(z_abs, 1)

            def softplus_out(g):
                dve.wait_ge(softlog, g + 1)
                z = zbuf[:, g, :].rearrange("p (k t) -> p k t", k=GD)
                v = delta[:, GD * g:GD * g + GD, :]
                dve.scalar_tensor_tensor(out=v, in0=z, scalar=0.0, in1=v, op0=ALU.max, op1=ALU.add).then_inc(delta_ready, 1)
                dve.wait_ge(delta_ready, g + 1)
                dve.tensor_tensor(z, v, uc[:, GD * g:GD * g + GD, :], ALU.mult).then_inc(du_ready, 1)

            def du_rest(g):
                dve.wait_ge(du_high_ready, g + 1)
                cols = slice(UN * g, UN * g + UN)
                dve.tensor_tensor(du_low[:, cols], psum[:, du_bank(g), :], du_high[:, cols].bitcast(F32),
                                  ALU.subtract).then_inc(du_low_ready, 1)

            for g in range(NG):
                softplus_in(g)
            gate_copy(0)
            silu(4)
            gate_copy(1)
            softplus_out(0)
            softplus_out(1)
            softplus_out(2)
            softplus_out(3)
            du_rest(0)
            gate_copy(2)

            def scan(s):
                dve.wait_ge(dA_ready, s + 1)
                dve.wait_ge(dbu_ready, s + 1)
                if s >= 3:
                    dve.wait_ge(pairs_ready, s - 2)
                p = 2 * ((s + 1) % 3)
                dve.tensor_tensor_scan(state[:, s % 3, :], dA[:, s % 3, :], psum[:, p:p + 2, :].rearrange("p a b -> p (a b)"),
                                       0.0, ALU.mult, ALU.add).then_inc(scan_done, 1)

            def times_c(s):
                dve.wait_ge(scan_done, s + 1)
                c = cwide[:, HN * P * (s % 2):HN * P * (s % 2) + OWN]
                v = state[:, s % 3, 0:OWN]
                dve.tensor_tensor(v, v, c, ALU.mult).then_inc(prod_ready, 1)

            def gate_y(g):
                dve.wait_ge(reduced, 2 * GD * (g + 1))
                for k in range(GD * g, GD * g + GD):
                    cols = slice(P * (k % GD), P * (k % GD) + P)
                    last = dve.scalar_tensor_tensor(out=uc[:, k, :], in0=uc[:, k, :], scalar=d_par[:, k:k + 1],
                                                    in1=psum[:, 6 + g % 2, cols], op0=ALU.mult, op1=ALU.add)
                step(last)
                v = slice(GD * g, GD * g + GD)
                dve.tensor_tensor(sg[:, v, :], sg[:, v, :], uc[:, v, :], ALU.mult).then_inc(yg_ready, 1)

            for s in range(STEPS):
                scan(s)
                if s == 1:
                    dve.wait_ge(c_ready, 4)
                if s >= 1:
                    times_c(s - 1)
                if s == 1:
                    gate_copy(3)
                if s in (3, 6, 9):
                    du_rest(s // 3)
                if s in (5, 8, 11):
                    silu(5 + s // 3 - 1)
                if s >= 12 and (s - 12) % 8 == 0:
                    gate_y((s - 12) // 8)
            times_c(STEPS - 1)
            gate_y(NG - 1)
            for nh in range(2):
                dve.wait_ge(y_psum, nh + 1)
                add_to_x(nh, nh)

            norm(2)
            finish_hT(2)
            dve.wait_ge(tri_in, 16)
            dve.wait_ge(ar_psum, 1)
            ranks = NE * RANK
            step(dve.tensor_copy(logit, psum[:, 2, ranks:ranks + NE]))
            step(dve.tensor_reduce(top, logit, AX, ALU.max))
            dve.tensor_scalar(top, top, -1.0, None, ALU.mult).then_inc(top_ready, 1)
            step(dve.tensor_tensor(above, wide(logit, NE), along(logit, NE), ALU.is_gt))
            step(dve.tensor_tensor(ties, wide(logit, NE), along(logit, NE), ALU.is_equal))
            step(dve.tensor_tensor(ties, ties, tri, ALU.mult))
            step(dve.tensor_tensor(above, above, ties, ALU.add))
            step(dve.tensor_reduce(rank, above, AX, ALU.add))
            dve.wait_ge(exp_ready, 1)
            step(dve.scalar_tensor_tensor(out=gate, in0=rank, scalar=1.5, in1=gate, op0=ALU.is_lt, op1=ALU.mult))
            step(dve.tensor_reduce(den, gate, AX, ALU.add))
            step(dve.reciprocal(den_inv, den))
            step(dve.tensor_scalar(gate, gate, den_inv, LORA_SCALE, ALU.mult, ALU.mult))
            dve.tensor_tensor(lora_g, psum[:, 2, 0:ranks].rearrange("p (e r) -> p e r", e=NE), along(gate, RANK),
                              ALU.mult).then_inc(g_ready, 1)
            dve.wait_ge(biased, 1)
            for nh in range(2):
                dve.wait_ge(base_psum, nh + 1)
                add_to_x(nh, nh)

            norm(3)
            finish_hT(3)
            for nh in range(2):
                dve.wait_ge(xq_psum, nh + 1)
                dve.tensor_tensor(xq[:, halves(nh)], psum[:, nh, :], bq[:, halves(nh)], ALU.add).then_inc(xq_ready, 1)
            dve.wait_ge(xqT_psum, 2)
            dve.tensor_copy(xqT[:, 4:8, :], psum[:, 5, :]).then_inc(xqT_hi, 1)
            step(dve.tensor_tensor_reduce(out=junk, in0=xq, in1=bk, scale=1.0, scalar=0.0, op0=ALU.mult, op1=ALU.add,
                                          accum_out=qbias))
            dve.wait_ge(xk_psum, 2)
            dve.tensor_copy(xk[:, halves(1)], psum[:, 3, :]).then_inc(xk_hi, 1)
            dve.wait_ge(xkT_psum, 2)
            dve.tensor_copy(xkT[:, 4:8, :], psum[:, 7, :]).then_inc(xkT_hi, 1)
            for nh in range(2):
                dve.wait_ge(score_psum, nh + 1)
                step(dve.tensor_reduce(smax2[:, nh:nh + 1], psum[:, nh, :], AX, ALU.max))
            step(dve.tensor_reduce(smax, smax2, AX, ALU.max))
            step(dve.tensor_scalar(smax, smax, qbias, -XSCALE, ALU.add, ALU.mult))
            dve.scalar_tensor_tensor(out=sbias, in0=qbias, scalar=XSCALE, in1=smax, op0=ALU.mult, op1=ALU.add).then_inc(sbias_ready, 1)
            dve.wait_ge(probT_psum, 2)
            dve.tensor_copy(probT[:, 4:8, :], psum[:, 5, :]).then_inc(probT_hi, 1)
            step(dve.tensor_reduce(ssum, ssum2, AX, ALU.add))
            step(dve.reciprocal(sinv, ssum))
            for nh in range(2):
                dve.wait_ge(xatt_psum, nh + 1)
                x_updated(dve.scalar_tensor_tensor(out=x[:, halves(nh)], in0=psum[:, 2 + nh, :], scalar=sinv,
                                                   in1=x[:, halves(nh)], op0=ALU.mult, op1=ALU.add))

            norm(4)
            finish_hT(4)
            step(dve.memset(vdup.rearrange("p b (h d) -> p (b h) d", d=DH + 1)[:, :, DH:], 1.0))
            dve.tensor_copy(hmax.rearrange("p a b -> p (a b)")[:, 0:1], sinv).then_inc(v_ready, 1)

            def rotate(source, heads, to, signal):
                v = source.rearrange("p (h d) -> p h d", h=heads)
                c = rope_c[:, 0:heads * DH].rearrange("p (h d) -> p h d", h=heads)
                s = rope_s[:, 0:heads * DH].rearrange("p (h d) -> p h d", h=heads)
                hd = DH // 2
                dve.tensor_tensor(c, v, wide(cosf, heads), ALU.mult)
                dve.tensor_tensor(s[:, :, 0:hd], v[:, :, hd:], wide(sinf[:, 0:hd], heads), ALU.mult)
                step(dve.tensor_tensor(s[:, :, hd:], v[:, :, 0:hd], wide(sinf[:, hd:], heads), ALU.mult))
                dve.tensor_tensor(to.rearrange("p (h d) -> p h d", h=heads), c, s, ALU.add).then_inc(signal, 1)

            dve.wait_ge(tables_in, 16)
            dve.wait_ge(kv_psum, 1)
            rotate(psum[:, 0, 0:HKV * DH], HKV, krot, krot_ready)
            dve.wait_ge(krot_ready, 1)
            for n in range(2):
                dve.wait_ge(aq_psum, n + 1)
                if n:
                    dve.wait_ge(qrot_ready, 1)
                rotate(psum[:, 7 if n else 1, :], H // 2, qrot[:, halves(n)], qrot_ready)
            for r in range(GQ):
                dve.wait_ge(as_psum, r + 1)
                v = aprob[:, r, :, :]
                step(dve.scalar_tensor_tensor(out=v, in0=psum[:, r, :].rearrange("p (j s) -> p j s", j=HKV), scalar=ASCALE,
                                              in1=wide(mask, HKV), op0=ALU.mult, op1=ALU.add))
                dve.tensor_reduce(hmax[:, r, :], v, AX, ALU.max).then_inc(hmax_ready, 1)
            for r in (1, 3):
                dve.wait_ge(apT_psum, r + 1)
                dve.tensor_copy(aprobT[:, 4 * r:4 * r + 4, :], psum[:, 4 + r, :]).then_inc(apT_odd, 1)
            for q in (0, 2, 1, 3):
                odd, hi = q // 2, q % 2
                dve.wait_ge(pv_psum, hi + 1)
                o = psum[:, q, 0:HKV * (DH + 1)].rearrange("p (n d) -> p n d", n=HKV)
                inv = oinv[:, q, :]
                step(dve.reciprocal(inv.rearrange("p (n u) -> p n u", u=1), o[:, :, DH:]))
                for a in range(2):
                    to = attn.rearrange("p (j r d) -> p j r d", j=HKV, r=GQ)[:, odd::2, 2 * hi + a, :]
                    last = dve.tensor_tensor(to, o[:, 4 * a:4 * a + 4, 0:DH], along(inv[:, 4 * a:4 * a + 4], DH), ALU.mult)
            last.then_inc(attn_ready, 1)
            dve.wait_ge(attnT_psum, 2)
            dve.tensor_copy(attnT[:, 4:8, :], psum[:, 7, :]).then_inc(attnT_ready, 1)
            for nh in range(2):
                dve.wait_ge(ao_psum, nh + 1)
                add_to_x(nh, nh)

            norm(5)

            def split_half(half, bank, high, low):
                v = slice(4 * half, 4 * half + 4)
                if half:
                    dve.tensor_copy(split[:, 0, v, :], psum[:, bank, :]).then_inc(high, 1)
                dve.wait_ge(high, half + 1)
                dve.tensor_tensor(split[:, 1, v, :], psum[:, bank, :].rearrange("p (k t) -> p k t", k=4),
                                  split[:, 0, v, :].bitcast(F32), ALU.subtract).then_inc(low, 1)

            dve.wait_ge(hs_high, 1)
            split_half(0, 6, hs_high, hs_low)
            dve.wait_ge(hT_psum, 10)
            split_half(1, 7, hs_high, hs_low)
            dve.wait_ge(g_psum, 2)
            dve.tensor_copy(picked[:, halves(1)], psum[:, 5, :]).then_inc(picked_hi, 1)
            dve.wait_ge(gT_turned, 2)
            dve.tensor_copy(gT[:, 4:8, :], psum[:, 7, :]).then_inc(g_hi, 1)
            dve.wait_ge(iota_ready, 1)
            for k in range(KT):
                dve.tensor_scalar(onehot[:, k, :], iota, perm_col[:, k:k + 1], None, ALU.is_equal).then_inc(place_ready, 1)
            dve.wait_ge(o_high, 1)
            split_half(0, 0, o_high, o_low)
            dve.wait_ge(down_psum, 2)
            split_half(1, 1, o_high, o_low)
            for nh in range(2):
                dve.wait_ge(placed, nh + 1)
                dve.tensor_tensor(y_out[:, halves(nh)], x[:, halves(nh)], psum[:, 2 + nh, :], ALU.add).then_inc(y_ready, 1)


def kernel(**inputs):
    import numpy as np
    import concourse.bacc as bacc
    from concourse.bass_utils import run_bass_kernel_spmd

    f = {name: np.asarray(a) for name, a in inputs.items()}

    def blocks(w):
        k, n = w.shape
        w = w.reshape(k // (UK * P), UK, P, n // UN, UN).transpose(3, 0, 2, 1, 4)
        return w.reshape(-1, P, UNIT)

    def tiles(w):
        return w.reshape(w.shape[0] // P, P, -1).transpose(1, 0, 2)

    def both(w0, w1):
        return np.stack([blocks(w0), blocks(w1)], 1).reshape(-1, P, UNIT)

    ctx = f["ctx_4096"]
    half = DH // 2
    freq = (1.0 / np.float32(10000.0) ** (np.arange(half, dtype=np.float32) / np.float32(half))).astype(np.float32)
    angle = np.arange(L, dtype=np.float32)[:, None] * freq[None, :]
    cos, sin = np.cos(angle).astype(np.float32), np.sin(angle).astype(np.float32)
    cos = np.concatenate([cos, cos], 1)
    sin = np.concatenate([-sin, sin], 1)
    mask = np.where(np.tril(np.ones((L, L), bool)), 0.0, -1e30).astype(np.float32)
    rows = (np.arange(P)[:, None] + P * np.arange(KT)[None, :]).astype(np.float32)
    pad = np.zeros((P, 8), np.float32)
    tables = np.concatenate([np.concatenate([cos, cos]), np.concatenate([sin, sin]), np.concatenate([mask, mask]), rows, pad], 1)
    tri = np.broadcast_to(np.tril(np.ones((NE, NE), np.float32), -1).reshape(1, -1), (P, NE * NE))

    perm = f["L1_ffn_perm"].astype(np.int32) if f["L1_ffn_perm"].dtype != np.int32 else f["L1_ffn_perm"]
    arrays = {
        "x": f["x"].reshape(P, D),
        "quant": np.stack([f["L0_xattn_x1_scale"], f["L0_xattn_x2_scale"], f["L0_xattn_x1_zp"], f["L0_xattn_x2_zp"]], 1),
        "tables": tables,
        "tri": tri,
        "ctx": both(ctx[0], ctx[1]),
        "ctx_t": both(ctx[0].T, ctx[1].T),
        "w_in": blocks(f["L0_attn_W_in"].T),
        "wx": tiles(f["L0_attn_Wx"].T),
        "wdt": f["L0_attn_Wdt"].T,
        "a_par": tiles(f["L0_attn_A"]),
        "chan": np.concatenate([tiles(f["L0_attn_conv_w"]).reshape(P, -1), tiles(f["L0_attn_conv_b"]).reshape(P, -1),
                                tiles(f["L0_attn_dt_bias"]).reshape(P, -1), tiles(f["L0_attn_D_param"]).reshape(P, -1)], 1),
        "rms_w": np.concatenate([f["L0_attn_dt_ln_w"], f["L0_attn_b_ln_w"], f["L0_attn_c_ln_w"]])[None],
        "w_out": blocks(f["L0_attn_W_out"].T),
        "w_base": blocks(f["L0_ffn_W_base"].T),
        "b_base": f["L0_ffn_b_base"][None],
        "w_ar": tiles(np.concatenate([f["L0_ffn_A"].reshape(NE * RANK, D), f["L0_ffn_W_router"]]).T),
        "lora_b": f["L0_ffn_B"].transpose(0, 2, 1).reshape(NE * RANK, D),
        "x_wq": blocks(f["L1_xattn_Wq"].T),
        "x_wk": blocks(f["L1_xattn_Wk"]),
        "bq": f["L1_xattn_bq"][None],
        "bk": f["L1_xattn_bk"][None],
        "a_wkv": blocks(np.concatenate([f["L1_attn_Wk"], f["L1_attn_Wv"]], 1)),
        "a_wq": blocks(f["L1_attn_Wq"]),
        "a_wo": blocks(f["L1_attn_Wo"]),
        "mlp_up": f["L1_ffn_up"].reshape(MH // 2, P, MM).transpose(1, 0, 2).reshape(1, P, UNIT),
        "mlp_down": f["L1_ffn_down"].reshape(MH, 2, P, MD).transpose(2, 1, 0, 3).reshape(1, P, UNIT),
        "perm_row": perm[None],
        "perm_col": perm.reshape(KT, P).T,
    }
    arrays = {name: np.ascontiguousarray(a) for name, a in arrays.items()}
    nc = bacc.Bacc("TRN2", target_bir_lowering=False, num_devices=1)
    dram = {name: nc.dram_tensor(f"in_{name}", a.shape, mybir.dt.from_np(a.dtype), kind="ExternalInput").ap()
            for name, a in arrays.items()}
    out = nc.dram_tensor("out", (P, D), F32, kind="ExternalOutput").ap()
    perceiver(nc, dram, out)
    result = run_bass_kernel_spmd(nc, [{f"in_{name}": a for name, a in arrays.items()}], core_ids=[0])
    return result.results[0]["out"].reshape(B, L, D)
```

```python
from contextlib import ExitStack

import concourse.bass as bass
from concourse import mybir

ALU = mybir.AluOpType
ACT = mybir.ActivationFunctionType
AX = mybir.AxisListType.X
F32 = mybir.dt.float32
BF16 = mybir.dt.bfloat16
F32R = mybir.dt.float32r
I32 = mybir.dt.int32

P = 128
B, L = 2, 64
D = 1024
KT = D // P
UK = 4
UN = 512
UNIT = UK * UN
SLOTS = 7
LN_EPS = 1e-5

DI = 2048
DT = DI // P
NS = 16
R = 64
CK = 4
NB = 2 * DI // UN
SSM = R + 2 * NS
RMS_EPS = 1e-6
GD = UN // P
NG = DT // GD
HN = NS // 2
OWN = 6 * P
DIRECT = 2
STEPS = 2 * DT

NE, RANK = 8, 16
LORA_SCALE = 2.0

XSCALE = 1.0 / 32.0
H, HKV, DH = 32, 8, 32
GQ = H // HKV
ASCALE = float(DH) ** -0.5
MH, MD, MM = 16, 64, 256

ROUND = 1.5 * 2.0 ** 23
QMAX = 255.0
QMID = 128.0


def unit_list():
    units = [("ctx", i) for i in range(8)]
    units += [("w_in", i) for i in range(16)]
    units += [("w_out", i) for i in (0, 4, 1, 2, 3, 5, 6, 7)]
    units += [("w_base", i) for i in range(4)]
    units += [("x_wq", i) for i in range(4)]
    units += [("x_wk", i) for i in (0, 2, 1, 3)]
    units += [("ctx_t", i) for i in (0, 1, 4, 5, 2, 3, 6, 7)]
    units += [("ctx", i) for i in (0, 1, 4, 5, 2, 3, 6, 7)]
    units += [("a_wkv", i) for i in range(2)]
    units += [("a_wq", i) for i in range(4)]
    units += [("a_wo", i) for i in range(4)]
    units += [("mlp_up", 0), ("mlp_down", 0)]
    return units


def perceiver(nc, dram, out):
    units = unit_list()
    first = {}
    for n, (name, i) in enumerate(units):
        if name == "ctx" and n >= 8:
            name = "ctx_again"
        first.setdefault(name, n)

    with ExitStack() as stack:
        def sb(name, shape, dtype=F32):
            return stack.enter_context(nc.sbuf_tensor(name, shape, dtype))

        def sem(name):
            return stack.enter_context(nc.semaphore(name))

        ring = sb("ring", [P, SLOTS, UNIT])
        x = sb("x", [P, D])
        h = sb("h", [P, D])
        hT = sb("hT", [P, KT, P])
        ident = sb("ident", [P, P])
        small = sb("small", [P, 640])
        with nc.sbuf_tensor("arena_halves", [P, 24576], F32R) as arena_r:
            pass
        arena = sb("arena", [P, 24576])
        rounded = sb("rounded", [P, 4 * DI], F32R)
        split = sb("split", [P, 2, KT, P], F32R)
        b_high = sb("b_high", [P, NS], F32R)
        psum = stack.enter_context(nc.psum_tensor("psum", [P, 8, 512], F32))

        def carve(tile, start, *dims):
            size = 1
            for d in dims:
                size *= d
            ap = tile[:, start:start + size]
            if len(dims) == 2:
                ap = ap.rearrange("p (a b) -> p a b", a=dims[0])
            if len(dims) == 3:
                ap = ap.rearrange("p (a b c) -> p a b c", a=dims[0], b=dims[1])
            return ap

        quant = carve(small, 0, 4)
        qrec = carve(small, 4, 2)
        qneg = carve(small, 6, 2)
        q_col = carve(small, 8, 1)
        b_low = carve(small, 592, NS)
        q_sum = carve(small, 12, 1)
        q_row = carve(small, 13, 1)
        q_s12 = carve(small, 14, 1)
        var_eps = carve(small, 15, 1)
        rstd = carve(small, 16, 1)
        minus_half = carve(small, 17, 4)
        stats = carve(small, 24, 2, 6)
        mv = carve(small, 36, 2)
        const_warm = carve(small, 21, 1)
        rms_sum = carve(small, 40, 3)
        rms_var = carve(small, 43, 3)
        rms_inv = carve(small, 46, 3)
        top = carve(small, 50, 1)
        den = carve(small, 51, 1)
        den_inv = carve(small, 52, 1)
        logit = carve(small, 56, NE)
        rank = carve(small, 64, NE)
        gate = carve(small, 72, NE)
        qbias = carve(small, 80, 1)
        smax2 = carve(small, 81, 2)
        smax = carve(small, 83, 1)
        sbias = carve(small, 84, 1)
        ssum2 = carve(small, 85, 2)
        ssum = carve(small, 87, 1)
        sinv = carve(small, 88, 1)
        hmax = carve(small, 96, GQ, HKV)
        oinv = carve(small, 128, 4, HKV)
        cosf = carve(small, 160, DH)
        sinf = carve(small, 192, DH)
        mask = carve(small, 224, L)
        row_no = carve(small, 288, KT)
        perm_col = carve(small, 296, KT)
        perm_coli = small[:, 304:304 + KT].bitcast(I32)
        conv_w = carve(small, 320, DT, CK)
        conv_b = carve(small, 384, DT)
        dt_b = carve(small, 400, DT)
        d_par = carve(small, 416, DT)
        rms_w = carve(small, 432, SSM)
        tri = carve(small, 528, NE, NE)

        q2 = arena[:, 0:8192].bitcast(BF16).rearrange("p (u n) -> p u n", u=8)
        q1T = arena[:, 8192:8704].bitcast(BF16).rearrange("p (k t) -> p k t", k=KT)
        ones64 = arena[:, 8704:8736].bitcast(BF16)
        codes_junk = carve(arena, 9216, D)
        uT = arena[:, 0:DT * B * (L + 3)].rearrange("p (k b t) -> p k b t", k=DT, b=B)
        zbuf = carve(arena, 0, NG, UN)
        uc = carve(arena, 2144, DT, P)
        delta = carve(arena, 4192, DT, P)
        sg = carve(arena, 6240, DT, P)
        cwide = carve(arena, 8288, NS * P)
        dA = carve(arena, 10336, 3, HN * P)
        state = carve(arena, 13408, 3, HN * P)
        cdiag = carve(arena, 14432, NS, P)
        pairs = carve(arena, 16480, 3, HN * P // 2)
        proj = carve(arena, 16480, 3, UN)
        tanh = carve(arena, 18016, 2, UN)
        wxT = carve(arena, 19040, DT, SSM)
        wdtT = carve(arena, 20576, DI)
        a_par = carve(arena, 22624, DT, NS)
        ssm = carve(arena, 22880, SSM)
        rms_junk = carve(arena, 22976, R)
        dtT = carve(arena, 23040, P)
        ones = carve(arena, 23168, P)
        bd_high = rounded[:, 0:DI].rearrange("p (n t) -> p n t", n=NS)
        bd_low = rounded[:, DI:2 * DI].rearrange("p (n t) -> p n t", n=NS)
        du_high = rounded[:, 2 * DI:3 * DI]
        du_low = rounded[:, 3 * DI:4 * DI]
        sg_high = carve(arena_r, 4192 - UN, DT, P)
        sg_low = carve(arena_r, 6240, DT, P)
        unit_halves = [ap.rearrange("p (a k n) -> p a k n", a=2, k=UK) for ap in (
            rounded[:, 0:2 * UNIT], rounded[:, 2 * UNIT:4 * UNIT], arena_r[:, 11392:11392 + 2 * UNIT])]
        w_ar = carve(arena, 0, KT, NE * RANK + NE)
        lora_b = carve(arena, 1088, D)
        bk = carve(arena, 19040, D)
        b_base = carve(arena, 20576, D)
        bq = carve(arena, 21600, D)
        lora_g = carve(arena, 23296, NE, RANK)
        lora_gT = carve(arena, 23424, P)
        above = carve(arena, 23552, NE, NE)
        ties = carve(arena, 23616, NE, NE)
        ring_more = carve(arena, 7168, UNIT)
        xq = carve(arena, 0, D)
        xq_split = carve(arena_r, 4096, 2, KT * P).rearrange("p a (k t) -> p a k t", k=KT)
        xk = carve(arena, 2048, D)
        xkT = carve(arena, 3072, KT, P)
        prob = carve(arena, 4096, D)
        probT = carve(arena, 5120, KT, P)
        junk = carve(arena, 1024, D)
        rope_c = carve(arena, 0, D)
        rope_s = carve(arena, 1024, D)
        qrot = carve(arena, 2048, D)
        krot = carve(arena, 3072, HKV * DH)
        krep = carve(arena, 3328, HKV, GQ, DH)
        aqT = carve(arena, 4352, KT, P)
        akT = carve(arena, 5376, KT, P)
        vdup = carve(arena, 6400, B, HKV * (DH + 1))
        aprob = carve(arena, 2048, GQ, HKV, L)
        aprobT = carve(arena, 0, 2 * KT, P)
        attn = carve(arena, 4352, D)
        permi = arena[:, 18016:19040].bitcast(I32)
        perm_row = carve(arena, 9312, D)
        iota = carve(arena, 10336, D)
        onehot = carve(arena_r, 15488, KT, D)
        gT = carve(arena, 0, KT, P)
        hidden = carve(arena, 1024, MH, 2, P)
        picked = carve(arena, 5120, D)
        y_out = carve(arena, 6144, D)

        unit_in = [sem(f"unit_in{s}") for s in range(SLOTS + 1)]
        x_in = sem("x_in")
        quant_in = sem("quant_in")
        tables_in = sem("tables_in")
        tri_in = sem("tri_in")
        mamba_in = sem("mamba_in")
        rank_in = sem("rank_in")
        bias_in = sem("bias_in")
        perm_in = sem("perm_in")
        vdup_in = sem("vdup_in")
        out_done = sem("out_done")
        ctx_coded = sem("ctx_coded")
        unit_used = sem("unit_used")
        unit_high = sem("unit_high")
        unit_low = sem("unit_low")
        const_zero = sem("const_zero")
        const_ready = sem("const_ready")
        stats_ready = sem("stats_ready")
        var_ready = sem("var_ready")
        rstd_ready = sem("rstd_ready")
        h_ready = sem("h_ready")
        hT_psum = sem("hT_psum")
        hT_lo = sem("hT_lo")
        hT_hi = sem("hT_hi")
        hs_high = sem("hs_high")
        hs_low = sem("hs_low")
        hT_sum = sem("hT_sum")
        x_ready = sem("x_ready")
        dve_step = sem("dve_step")
        act_step = sem("act_step")
        scales_ready = sem("scales_ready")
        ctx_scaled = sem("ctx_scaled")
        q1_ready = sem("q1_ready")
        qneg_ready = sem("qneg_ready")
        q_step = sem("q_step")
        q_summed = sem("q_summed")
        x_offset = sem("x_offset")
        q1_psum = sem("q1_psum")
        q1T_ready = sem("q1T_ready")
        q_done = sem("q_done")
        edge_zero = sem("edge_zero")
        proj_psum = sem("proj_psum")
        proj_sb = sem("proj_sb")
        projT_psum = sem("projT_psum")
        projT_read = sem("projT_read")
        conv_half = sem("conv_half")
        tanh_ready = sem("tanh_ready")
        gated = sem("gated")
        ssm_psum = sem("ssm_psum")
        ssm_sum = sem("ssm_sum")
        ssm_inv = sem("ssm_inv")
        dt_normed = sem("dt_normed")
        bc_ready = sem("bc_ready")
        dtT_psum = sem("dtT_psum")
        dtT_ready = sem("dtT_ready")
        z_psum = sem("z_psum")
        z_read = sem("z_read")
        z_abs = sem("z_abs")
        z_exp = sem("z_exp")
        softlog = sem("softlog")
        delta_ready = sem("delta_ready")
        du_ready = sem("du_ready")
        duT_psum = sem("duT_psum")
        du_high_ready = sem("du_high_ready")
        du_low_ready = sem("du_low_ready")
        b_split = sem("b_split")
        bd_high_ready = sem("bd_high_ready")
        bd_low_ready = sem("bd_low_ready")
        cdiag_ready = sem("cdiag_ready")
        c_psum = sem("c_psum")
        c_ready = sem("c_ready")
        dbu_ready = sem("dbu_ready")
        dA_ready = sem("dA_ready")
        scan_done = sem("scan_done")
        prod_ready = sem("prod_ready")
        prod_rest = sem("prod_rest")
        pairs_ready = sem("pairs_ready")
        reduced = sem("reduced")
        yg_ready = sem("yg_ready")
        sg_high_ready = sem("sg_high_ready")
        sg_low_ready = sem("sg_low_ready")
        y_psum = sem("y_psum")
        ar_psum = sem("ar_psum")
        top_ready = sem("top_ready")
        exp_ready = sem("exp_ready")
        g_ready = sem("g_ready")
        gT_psum = sem("gT_psum")
        gT_ready = sem("gT_ready")
        biased = sem("biased")
        base_psum = sem("base_psum")
        xq_psum = sem("xq_psum")
        xq_ready = sem("xq_ready")
        xqT_psum = sem("xqT_psum")
        xs_high = sem("xs_high")
        xs_low = sem("xs_low")
        xk_psum = sem("xk_psum")
        xk_lo = sem("xk_lo")
        xk_hi = sem("xk_hi")
        xkT_psum = sem("xkT_psum")
        xkT_lo = sem("xkT_lo")
        xkT_hi = sem("xkT_hi")
        score_psum = sem("score_psum")
        sbias_ready = sem("sbias_ready")
        prob_ready = sem("prob_ready")
        probT_psum = sem("probT_psum")
        probT_lo = sem("probT_lo")
        probT_hi = sem("probT_hi")
        xatt_psum = sem("xatt_psum")
        kv_psum = sem("kv_psum")
        aq_psum = sem("aq_psum")
        krot_ready = sem("krot_ready")
        krep_ready = sem("krep_ready")
        v_ready = sem("v_ready")
        akT_psum = sem("akT_psum")
        akT_ready = sem("akT_ready")
        qrot_ready = sem("qrot_ready")
        aqT_psum = sem("aqT_psum")
        aqT_ready = sem("aqT_ready")
        as_psum = sem("as_psum")
        hmax_ready = sem("hmax_ready")
        as_ready = sem("as_ready")
        ap_ready = sem("ap_ready")
        apT_psum = sem("apT_psum")
        apT_even = sem("apT_even")
        apT_odd = sem("apT_odd")
        pv_psum = sem("pv_psum")
        attn_ready = sem("attn_ready")
        attnT_psum = sem("attnT_psum")
        ao_psum = sem("ao_psum")
        perm_f = sem("perm_f")
        iota_ready = sem("iota_ready")
        pick_ready = sem("pick_ready")
        place_ready = sem("place_ready")
        g_psum = sem("g_psum")
        picked_lo = sem("picked_lo")
        picked_hi = sem("picked_hi")
        gT_turned = sem("gT_turned")
        g_lo = sem("g_lo")
        g_hi = sem("g_hi")
        up_psum = sem("up_psum")
        hidden_ready = sem("hidden_ready")
        down_psum = sem("down_psum")
        o_high = sem("o_high")
        o_low = sem("o_low")
        placed = sem("placed")
        y_ready = sem("y_ready")

        last_use = [(ctx_coded, n + 1 + n // 7) for n in range(8)]
        middle = 0
        split_units = []
        split_done = []

        def uses(*signals, split=False):
            nonlocal middle
            for signal in signals:
                if signal is None:
                    middle += 1
                    signal = (unit_used, middle)
                if split:
                    split_units.append(len(last_use))
                    split_done.append(signal)
                    signal = (unit_low, len(split_done))
                last_use.append(signal)

        for j in range(NB):
            uses(None, (proj_psum, j + 1))
        uses(None, None)
        for nh in range(2):
            uses(None, None, (y_psum, nh + 1), split=True)
        uses(None, None, None, None, split=True)
        uses(None, (xq_psum, 1), None, (xq_psum, 2), split=True)
        uses(None, None, (xk_psum, 1), (xk_psum, 2), split=True)
        for signal in (score_psum, xatt_psum):
            for pair in range(2):
                uses(None)
                last_use.append(last_use[-1])
            uses((signal, 1), (signal, 1), (signal, 2), (signal, 2))
        uses(None, (kv_psum, 1), split=True)
        for signal in (aq_psum, ao_psum):
            uses(None, (signal, 1), None, (signal, 2), split=True)

        more = first["x_wq"] + 1
        slot_of = []
        for n in range(len(units)):
            slot_of.append(n % SLOTS if n < more else SLOTS if n == more else slot_of[n - SLOTS - 1])

        def place(n):
            return ring_more if slot_of[n] == SLOTS else ring[:, slot_of[n], :]

        def slot(n):
            return place(n).rearrange("p (k n) -> p k n", k=UK)

        def arrived(eng, n):
            eng.wait_ge(unit_in[slot_of[n]], 16 * slot_of[:n + 1].count(slot_of[n]))

        def code_parts(n):
            return (slice(0, UNIT // 2), slice(UNIT // 2, UNIT)) if n == 7 else (slice(0, UNIT),)

        def turn_bank(j):
            return 0 if j == NB - 1 else 3 + j % 2

        def du_bank(g):
            return 6 if g == 0 else 7

        def wide(ap, count):
            n = ap.shape[1]
            return ap.rearrange("p (u n) -> p u n", u=1).to_broadcast([P, count, n])

        def along(ap, count):
            n = ap.shape[1]
            return ap.rearrange("p (n u) -> p n u", u=1).to_broadcast([P, n, count])

        block = stack.enter_context(nc.Block())

        @block.sync
        def _(sp):
            sp.dma_start(x[:, :], dram["x"]).then_inc(x_in, 16)
            for n, (name, i) in enumerate(units):
                if n == 8:
                    sp.dma_start(small[:, 320:432], dram["chan"]).then_inc(mamba_in, 16)
                    sp.dma_start(rms_w, dram["rms_w"].to_broadcast([P, SSM])).then_inc(mamba_in, 16)
                    sp.dma_start(wxT, dram["wx"]).then_inc(mamba_in, 16)
                    sp.dma_start(wdtT[0:R, :], dram["wdt"]).then_inc(mamba_in, 16)
                    sp.dma_start(a_par, dram["a_par"]).then_inc(mamba_in, 16)
                if n == more:
                    sp.wait_ge(y_psum, 2)
                elif n >= SLOTS:
                    sp.wait_ge(*last_use[n - SLOTS - (n > more)])
                sp.dma_start(place(n), dram[name][i]).then_inc(unit_in[slot_of[n]], 16)
            for nh in range(2):
                sp.wait_ge(y_ready, nh + 1)
                cols = slice(nh * UN, nh * UN + UN)
                sp.dma_start(out[:, cols], y_out[:, cols]).then_inc(out_done, 16)
            sp.wait_ge(out_done, 32)

        @block.gpsimd
        def _(pool):
            pool.dma_start(small[:, 160:304], dram["tables"]).then_inc(tables_in, 16)
            pool.memset(ident[:, :], 0.0).then_inc(const_zero, 1)
            pool.memset(minus_half, -0.5).then_inc(const_zero, 1)
            pool.memset(const_warm, 0.0).then_inc(const_ready, 1)
            pool.memset(ones64, 1.0).then_inc(const_ready, 1)
            pool.wait_ge(const_zero, 2)
            pool.affine_select(out=ident[:, :], in_=ident[:, :], compare_op=ALU.not_equal, fill=1.0, base=0,
                               pattern=[[-1, P]], channel_multiplier=1).then_inc(const_ready, 1)

            def rstd_of(n):
                pool.wait_ge(var_ready, n + 1)
                pool.tensor_tensor(rstd, var_eps, minus_half[:, 0:1], ALU.pow).then_inc(rstd_ready, 1)

            pool.wait_ge(const_ready, 3)
            rstd_of(0)
            pool.memset(ones, 1.0).then_inc(const_ready, 1)

            q_steps = [0]

            def q(ins):
                q_steps[0] += 1
                ins.then_inc(q_step, 1)
                pool.wait_ge(q_step, q_steps[0])

            pool.wait_ge(qneg_ready, 1)
            q(pool.tensor_scalar(q_s12, quant[:, 0:1], quant[:, 1:2], None, ALU.mult))
            q(pool.tensor_scalar(q_col, qneg[:, 0:1], q_s12, None, ALU.mult))
            pool.wait_ge(q_summed, 1)
            q(pool.tensor_scalar(q_row, qneg[:, 0:1], float(D), q_sum, ALU.mult, ALU.add))
            q(pool.tensor_scalar(q_row, q_row, qneg[:, 1:2], q_s12, ALU.mult, ALU.mult))
            pool.tensor_scalar(x[:, :], x[:, :], q_row, None, ALU.add).then_inc(x_offset, 1)

            rstd_of(1)
            pool.wait_ge(q_done, 2)
            pool.memset(uT[:, :, :, 0:CK - 1], 0.0).then_inc(edge_zero, 1)
            pool.memset(dA.rearrange("p s (n t) -> p (s n) t", t=L)[:, :, 0:1], 0.0).then_inc(edge_zero, 1)

            pool.wait_ge(ssm_sum, 1)
            pool.tensor_tensor(rms_inv, rms_var, minus_half[:, 0:3], ALU.pow).then_inc(ssm_inv, 1)
            pool.wait_ge(bc_ready, 2)
            pool.tensor_tensor(cdiag, wide(ident[:, :], NS), along(ssm[:, R + NS:SSM], P), ALU.mult).then_inc(cdiag_ready, 1)
            pool.wait_ge(b_split, 1)
            pool.tensor_tensor(bd_low, wide(ident[:, :], NS), along(b_low, P), ALU.mult).then_inc(bd_low_ready, 1)
            pool.wait_ge(projT_psum, 8)
            half = HN * P // 2
            for s in range(STEPS - DIRECT):
                pool.wait_ge(scan_done, s + 1)
                pool.wait_ge(c_ready, 4)
                prod = state[:, s % 3, :]
                c = cwide[:, HN * P * (s % 2):HN * P * (s % 2) + HN * P]
                pool.tensor_tensor(prod[:, OWN:], prod[:, OWN:], c[:, OWN:], ALU.mult).then_inc(prod_rest, 1)
                pool.wait_ge(prod_rest, s + 1)
                pool.wait_ge(prod_ready, s + 1)
                if s >= 3:
                    pool.wait_ge(reduced, s - 2)
                pool.tensor_tensor(pairs[:, s % 3, :], prod[:, 0:half], prod[:, half:], ALU.add).then_inc(pairs_ready, 1)

            rstd_of(2)
            for half in range(2):
                pool.wait_ge(hs_low, half + 1)
                v = slice(4 * half, 4 * half + 4)
                pool.tensor_tensor(hT[:, v, :], split[:, 0, v, :].bitcast(F32), split[:, 1, v, :].bitcast(F32),
                                   ALU.add).then_inc(hT_sum, 1)
            pool.wait_ge(bias_in, 48)
            pool.wait_ge(h_ready, 6)
            pool.tensor_tensor(x[:, :], x[:, :], b_base, ALU.add).then_inc(biased, 1)
            rstd_of(3)
            pool.wait_ge(y_psum, 2)
            pool.iota(iota, pattern=[[1, D]], base=0, channel_multiplier=0,
                      allow_small_or_imprecise_dtypes=True).then_inc(iota_ready, 1)
            pool.wait_ge(perm_in, 32)
            pool.wait_ge(tables_in, 16)
            pool.tensor_copy(perm_row, permi).then_inc(perm_f, 1)
            pool.tensor_copy(perm_col, perm_coli).then_inc(perm_f, 1)
            pool.wait_ge(perm_f, 2)
            pool.wait_ge(sbias_ready, 1)
            for k in range(KT):
                if k == 5:
                    rstd_of(4)
                pool.tensor_scalar(onehot[:, k, :], perm_row, row_no[:, k:k + 1], None, ALU.is_equal).then_inc(pick_ready, 1)
            for r in range(GQ):
                pool.wait_ge(hmax_ready, r + 1)
                v = aprob[:, r, :, :]
                pool.tensor_tensor(v, v, along(hmax[:, r, :], L), ALU.subtract).then_inc(as_ready, 1)
            rstd_of(5)

        @block.scalar
        def _(act):
            steps = [0]

            def step(ins):
                steps[0] += 1
                ins.then_inc(act_step, 1)
                act.wait_ge(act_step, steps[0])

            act.dma_start(quant, dram["quant"].to_broadcast([P, 4])).then_inc(quant_in, 16)
            act.dma_start(tri, dram["tri"]).then_inc(tri_in, 16)

            act.wait_ge(const_ready, 3)
            step(act.activation(const_warm, const_warm, ACT.Identity))
            act.wait_ge(scales_ready, 1)
            for n in range(8):
                if n == 2:
                    act.wait_ge(q1_ready, 1)
                    act.activation(codes_junk, h[:, :], ACT.Copy, accum_out=q_sum).then_inc(q_summed, 1)
                arrived(act, n)
                for cols in code_parts(n):
                    v = ring[:, slot_of[n], cols]
                    act.activation(v, v, ACT.Identity, bias=quant[:, 3:4], scale=qrec[:, 1:2]).then_inc(ctx_scaled, 1)

            def evacuate_hT(n):
                act.wait_ge(hT_psum, 2 * n - 1)
                act.activation(hT[:, 0:4, :], psum[:, 6, :], ACT.Copy).then_inc(hT_lo, 1)

            evacuate_hT(1)

            def proj_copy(j):
                act.wait_ge(proj_psum, j + 1)
                if j >= 3:
                    act.wait_ge(projT_psum, j - 2)
                act.activation(proj[:, j % 3, :], psum[:, j % 3, :], ACT.Copy).then_inc(proj_sb, 1)

            def half_tanh(n):
                if n < NG:
                    act.wait_ge(conv_half, n + 1)
                else:
                    act.wait_ge(projT_read, n + 1)
                if n >= 2:
                    act.wait_ge(gated, n - 1)
                v = (uc if n < NG else sg)[:, GD * (n % NG):GD * (n % NG) + GD, :].rearrange("p k t -> p (k t)")
                act.activation(tanh[:, n % 2, :], v, ACT.Tanh).then_inc(tanh_ready, 1)

            def softplus_exp(g):
                act.wait_ge(z_abs, g + 1)
                v = delta[:, GD * g:GD * g + GD, :]
                act.activation(v, v, ACT.Exp, scale=-1.0).then_inc(z_exp, 1)

            def softplus_log(g):
                act.wait_ge(z_exp, g + 1)
                v = delta[:, GD * g:GD * g + GD, :]
                act.activation(v, v, ACT.Ln, bias=1.0).then_inc(softlog, 1)

            def du_copy(g):
                act.wait_ge(duT_psum, g + 1)
                act.activation(du_high[:, UN * g:UN * g + UN], psum[:, du_bank(g), :], ACT.Copy).then_inc(du_high_ready, 1)

            def c_copy(c):
                act.wait_ge(c_psum, c + 1)
                act.activation(cwide[:, UN * c:UN * c + UN], psum[:, 7 - 2 * (c % 2), :], ACT.Copy).then_inc(c_ready, 1)

            proj_copy(0)
            proj_copy(1)
            half_tanh(0)
            proj_copy(2)
            half_tanh(1)
            proj_copy(3)
            half_tanh(2)
            half_tanh(3)
            proj_copy(4)
            act.wait_ge(dtT_psum, 1)
            act.activation(dtT[0:R, :], psum[0:R, 5, 128:256], ACT.Copy).then_inc(dtT_ready, 1)
            softplus_exp(0)
            softplus_exp(1)
            softplus_exp(2)
            softplus_exp(3)
            proj_copy(5)
            half_tanh(4)
            for g in range(NG):
                softplus_log(g)
            for c in range(4):
                c_copy(c)
            act.wait_ge(edge_zero, 2)

            def decay(s):
                k = s // 2
                act.wait_ge(delta_ready, k // GD + 1)
                if s >= 3:
                    act.wait_ge(scan_done, s - 2)
                for n in range(HN):
                    to = dA[:, s % 3, n * P:n * P + P].rearrange("p (b t) -> p b t", b=B)[:, :, 1:]
                    of = delta[:, k, :].rearrange("p (b t) -> p b t", b=B)[:, :, 1:]
                    state_no = HN * (s % 2) + n
                    last = act.activation(to, of, ACT.Exp, scale=a_par[:, k, state_no:state_no + 1])
                last.then_inc(dA_ready, 1)

            decay(0)
            proj_copy(6)
            du_copy(0)
            decay(1)
            decay(2)
            proj_copy(7)

            def gated_high(g):
                act.wait_ge(yg_ready, g + 1)
                v = slice(GD * g, GD * g + GD)
                act.activation(sg_high[:, v, :], sg[:, v, :], ACT.Copy).then_inc(sg_high_ready, 1)

            def high(m):
                arrived(act, split_units[m])
                if m >= 3:
                    act.wait_ge(*split_done[m - 3])
                act.activation(unit_halves[m % 3][:, 0, :, :], slot(split_units[m]), ACT.Copy).then_inc(unit_high, 1)

            def left_high(turned, count):
                for half in range(2):
                    act.wait_ge(turned, count + half - 1)
                    v = slice(4 * half, 4 * half + 4)
                    act.activation(split[:, 0, v, :], psum[:, 6 + half, :], ACT.Copy).then_inc(hs_high, 1)

            for s in range(3, STEPS):
                decay(s)
                if s in (3, 6, 9):
                    du_copy(s // 3)
                if s in (4, 7, 10):
                    half_tanh(5 + s // 3 - 1)
                if s in (22, 30):
                    gated_high((s - 14) // 8)
                if s == 15:
                    act.wait_ge(du_low_ready, NG)
                    act.wait_ge(gated, 2 * NG)
                    act.dma_start(lora_b, dram["lora_b"]).then_inc(rank_in, 16)
                    act.dma_start(w_ar, dram["w_ar"]).then_inc(rank_in, 16)
                    act.dma_start(permi, dram["perm_row"].to_broadcast([P, D])).then_inc(perm_in, 16)
                    act.dma_start(perm_coli, dram["perm_col"]).then_inc(perm_in, 16)
                    act.dma_start(b_base, dram["b_base"].to_broadcast([P, D])).then_inc(bias_in, 16)
                    act.dma_start(bq, dram["bq"].to_broadcast([P, D])).then_inc(bias_in, 16)
                    act.dma_start(bk, dram["bk"].to_broadcast([P, D])).then_inc(bias_in, 16)

            act.wait_ge(dbu_ready, STEPS)
            high(0)
            high(1)
            gated_high(3)
            high(2)
            for m in range(3, 9):
                high(m)

            left_high(hT_psum, 4)
            high(9)
            high(10)
            act.wait_ge(top_ready, 1)
            act.activation(gate, logit, ACT.Exp, bias=top).then_inc(exp_ready, 1)
            act.wait_ge(gT_psum, 1)
            act.activation(lora_gT, psum[:, 3, 0:P], ACT.Copy).then_inc(gT_ready, 1)
            high(11)
            high(12)

            left_high(hT_psum, 6)
            high(13)
            high(14)

            def query_high(half):
                act.wait_ge(xqT_psum, half + 1)
                act.activation(xq_split[:, 0, 4 * half:4 * half + 4, :], psum[:, 4 + half, :], ACT.Copy).then_inc(xs_high, 1)

            query_high(0)
            high(15)
            high(16)
            query_high(1)
            high(17)
            act.wait_ge(xk_psum, 1)
            act.activation(xk[:, 0:UN], psum[:, 2, :], ACT.Copy).then_inc(xk_lo, 1)
            act.wait_ge(xkT_psum, 1)
            act.activation(xkT[:, 0:4, :], psum[:, 6, :], ACT.Copy).then_inc(xkT_lo, 1)
            act.wait_ge(sbias_ready, 1)
            for nh in range(2):
                act.activation(prob[:, nh * UN:nh * UN + UN], psum[:, nh, :], ACT.Exp, bias=sbias, scale=XSCALE,
                               accum_out=ssum2[:, nh:nh + 1]).then_inc(prob_ready, 1)
            act.wait_ge(probT_psum, 1)
            act.activation(probT[:, 0:4, :], psum[:, 4, :], ACT.Copy).then_inc(probT_lo, 1)

            high(18)
            left_high(hT_psum, 8)
            high(19)
            high(20)
            high(21)
            high(22)
            act.wait_ge(krot_ready, 1)
            for r in range(GQ):
                last = act.activation(krep[:, :, r, :], krot.rearrange("p (g d) -> p g d", g=HKV), ACT.Copy)
            last.then_inc(krep_ready, 1)
            for b in range(B):
                rows = slice(L * b, L * b + L)
                to = vdup[rows, b, :].rearrange("p (h d) -> p h d", h=HKV)
                act.activation(to[:, :, 0:DH], psum[rows, 0, 256:512].rearrange("p (h d) -> p h d", h=HKV),
                               ACT.Copy).then_inc(v_ready, 1)
            act.wait_ge(v_ready, 3)
            act.dma_start(vdup[L:P, 0, :], vdup[0:L, 0, :]).then_inc(vdup_in, 16)
            act.dma_start(vdup[0:L, 1, :], vdup[L:P, 1, :]).then_inc(vdup_in, 16)
            high(23)
            for n in range(2):
                act.wait_ge(akT_psum, n + 1)
                act.activation(akT[:, 4 * n:4 * n + 4, :], psum[:, 4 + n, :], ACT.Copy).then_inc(akT_ready, 1)
            for n in range(2):
                high(24 + n)
                act.wait_ge(aqT_psum, n + 1)
                act.activation(aqT[:, 4 * n:4 * n + 4, :], psum[:, 6 - 2 * n, :], ACT.Copy).then_inc(aqT_ready, 1)
            for r in range(GQ):
                act.wait_ge(as_ready, r + 1)
                act.activation(aprob[:, r, :, :], aprob[:, r, :, :], ACT.Exp).then_inc(ap_ready, 1)
                if r % 2:
                    act.wait_ge(apT_psum, r)
                    act.activation(aprobT[:, 4 * r - 4:4 * r, :], psum[:, 3 + r, :], ACT.Copy).then_inc(apT_even, 1)
            high(26)
            left_high(attnT_psum, 2)
            high(27)

            left_high(hT_psum, 10)
            act.wait_ge(g_psum, 1)
            act.activation(picked[:, 0:UN], psum[:, 4, :], ACT.Copy).then_inc(picked_lo, 1)
            act.wait_ge(gT_turned, 1)
            act.activation(gT[:, 0:4, :], psum[:, 6, :], ACT.Copy).then_inc(g_lo, 1)
            for q in range(4):
                for r in range(2):
                    act.wait_ge(up_psum, q + 1)
                    to = hidden[:, 4 * q + r:4 * q + r + 3:2, :, :]
                    act.activation(to, psum[:, 4 * r + q, :].rearrange("p (h m t) -> p h m t", h=2, m=2),
                                   ACT.Gelu).then_inc(hidden_ready, 1)
            act.wait_ge(down_psum, 1)
            act.activation(split[:, 0, 0:4, :], psum[:, 0, :], ACT.Copy).then_inc(o_high, 1)

        @block.tensor
        def _(pe):
            def transpose4(bank, tile, first_col, signal):
                for k in range(4):
                    c = first_col + P * k
                    last = pe.transpose(psum[:, bank, P * k:P * k + P], tile[:, c:c + P], ident[:, :])
                last.then_inc(signal, 1)

            pe.wait_ge(const_ready, 3)
            for half in range(2):
                pe.wait_ge(q1_ready, 1)
                transpose4(6 + half, h, UN * half, q1_psum)
            pe.wait_ge(q1T_ready, 2)
            for nh in range(2):
                for kh in range(2):
                    for b in range(B):
                        u = 4 * nh + 2 * kh + b
                        pe.wait_ge(ctx_coded, u + 1)
                        rows = slice(L * b, L * b + L)
                        for k in range(UK):
                            if u == 7 and k == UK // 2:
                                pe.wait_ge(ctx_coded, 9)
                            right = q2[:, u, UN * k:UN * k + UN]
                            at = dict(start=(kh == 0 and k == 0), stop=(kh == 1 and k == UK - 1))
                            pe.matmul(psum[rows, nh, :], q1T[:, UK * kh + k, rows], right, **at)
                            last = pe.matmul(psum[rows, 2 + nh, :], ones64, right, **at)
                last.then_inc(q_done, 1)

            def split_products(bank, left, m, k0, start, stop, signal, hook=None, fresh=None):
                if fresh:
                    pe.wait_ge(fresh[0], fresh[2])
                pe.wait_ge(unit_low, m + 1)
                unit = unit_halves[m % 3]
                for k in range(UK):
                    for w in range(2):
                        pe.matmul(psum[:, bank, :], left(0, k0 + k), unit[:, w, k, :], start=(start and k == 0 and w == 0),
                                  stop=False)
                if fresh:
                    pe.wait_ge(fresh[1], fresh[2])
                if hook:
                    hook()
                for k in range(UK):
                    last = pe.matmul(psum[:, bank, :], left(1, k0 + k), unit[:, 0, k, :], start=False,
                                     stop=(stop and k == UK - 1))
                last.then_inc(signal, 1)

            def left_half(a, k):
                return split[:, a, k, :]

            def transpose_h(n):
                for half in range(2):
                    pe.wait_ge(h_ready, 2 * n + half + 1)
                    transpose4(6 + half, h, UN * half, hT_psum)

            transpose_h(1)

            def turn(j):
                pe.wait_ge(proj_sb, j + 1)
                if j >= 2:
                    pe.wait_ge(projT_read, j - 1)
                transpose4(turn_bank(j), proj[:, j % 3, :], 0, projT_psum)

            def small_projection(g):
                if g == 0:
                    pe.wait_ge(mamba_in, 80)
                pe.wait_ge(gated, g + 1)
                for k in range(GD * g, GD * g + GD):
                    last = pe.matmul(psum[:, 5, 0:SSM], uc[:, k, :], wxT[:, k, :], start=(k == 0), stop=(k == DT - 1))
                if g == NG - 1:
                    last.then_inc(ssm_psum, 1)

            def time_steps(g):
                if g == 0:
                    pe.wait_ge(dtT_ready, 1)
                if g >= 2:
                    pe.wait_ge(z_read, g - 1)
                for k in range(GD * g, GD * g + GD):
                    last = pe.matmul(psum[:, 6 + g % 2, P * (k % GD):P * (k % GD) + P], wdtT[0:R, P * k:P * k + P],
                                     dtT[0:R, :], start=True, stop=True)
                last.then_inc(z_psum, 1)

            def turn_dt():
                pe.wait_ge(dt_normed, 1)
                pe.transpose(psum[0:R, 5, 128:256], ssm[:, 0:R], ident[:, :]).then_inc(dtT_psum, 1)

            def spread_c(c):
                if c == 0:
                    pe.wait_ge(cdiag_ready, 1)
                    pe.wait_ge(z_read, 4)
                if c >= 2:
                    pe.wait_ge(c_ready, c - 1)
                pe.matmul(psum[:, 7 - 2 * (c % 2), :], ones, cdiag[:, 4 * c:4 * c + 4, :], start=True,
                          stop=True).then_inc(c_psum, 1)

            def turn_du(g):
                pe.wait_ge(du_ready, g + 1)
                if g == 0:
                    pe.wait_ge(z_read, 3)
                elif g == 1:
                    pe.wait_ge(c_ready, 4)
                else:
                    pe.wait_ge(du_low_ready, g)
                transpose4(du_bank(g), zbuf[:, g, :], 0, duT_psum)

            def scan_input(s):
                if s % (2 * GD) == 0:
                    pe.wait_ge(du_low_ready, s // (2 * GD) + 1)
                if s == 0:
                    pe.wait_ge(bd_high_ready, 1)
                    pe.wait_ge(bd_low_ready, 1)
                if s == 0:
                    pe.wait_ge(projT_read, 7)
                if s == 1:
                    pe.wait_ge(c_ready, 4)
                if s == 2:
                    pe.wait_ge(projT_read, 8)
                if s >= 3:
                    pe.wait_ge(scan_done, s - 2)
                k = s // 2
                left = slice(P * k, P * k + P)
                for c in range(2):
                    right = slice(HN * (s % 2) + 4 * c, HN * (s % 2) + 4 * c + 4)
                    to = psum[:, 2 * ((s + 1) % 3) + c, :]
                    pe.matmul(to, du_high[:, left], bd_high[:, right, :], start=True, stop=False)
                    pe.matmul(to, du_high[:, left], bd_low[:, right, :], start=False, stop=False)
                    last = pe.matmul(to, du_low[:, left], bd_high[:, right, :], start=False, stop=True)
                last.then_inc(dbu_ready, 1)

            between = {}
            for j in range(NG - 1):
                between[KT * (j + 1) + 2] = [(turn, j)]
            gates = KT * NG
            between[gates + 2] = [(turn, 3)]
            between[gates + 4] = [(small_projection, g) for g in range(3)]
            between[gates + 7] = [(small_projection, 3)]
            between[gates + 9] = [(turn, 4)]
            between[gates + 10] = [(turn_dt,)]
            between[gates + 11] = [(time_steps, 0), (time_steps, 1)]
            between[gates + 13] = [(time_steps, 2)]
            between[gates + 14] = [(time_steps, 3)]
            between[gates + 17] = [(spread_c, 0), (spread_c, 1)]
            between[gates + 19] = [(turn, 5)]
            between[gates + 21] = [(spread_c, 2), (spread_c, 3)]
            between[gates + 23] = [(turn_du, 0)]
            between[gates + 27] = [(turn, 6)]
            between[gates + 29] = [(scan_input, 0)]
            between[gates + 31] = [(scan_input, 1)]
            w_in = first["w_in"]
            for j in range(NB):
                if j >= 3:
                    pe.wait_ge(proj_sb, j - 2)
                for k in range(KT):
                    if j == 0 and k % UK == 0:
                        pe.wait_ge(*((hT_hi if k else hT_lo), 1))
                    for hook, *which in between.get(KT * j + k, []):
                        hook(*which)
                    u = w_in + 2 * j + k // UK
                    if k % UK == 0:
                        arrived(pe, u)
                    last = pe.matmul(psum[:, j % 3, :], hT[:, k, :], slot(u)[:, k % UK, :], start=(k == 0), stop=(k == KT - 1))
                    if k % UK == UK - 1:
                        last.then_inc(proj_psum if k == KT - 1 else unit_used, 1)

            def state_sum(s):
                paired = s < STEPS - DIRECT
                pe.wait_ge(*((pairs_ready if paired else prod_ready), s + 1))
                k = s // 2
                g = k // GD
                if s == 2 * GD:
                    pe.wait_ge(du_low_ready, NG)
                if g >= 2:
                    pe.wait_ge(yg_ready, g - 1)
                cols = slice(P * (k % GD), P * (k % GD) + P)
                right, count = (pairs, HN // 2) if paired else (state, HN)
                for n in range(count):
                    last = pe.matmul(psum[:, 6 + g % 2, cols], ident[:, :], right[:, s % 3, P * n:P * n + P],
                                     start=(s % 2 == 0 and n == 0), stop=(s % 2 == 1 and n == count - 1))
                last.then_inc(reduced, 1)

            turn(7)
            for s in range(STEPS):
                if s >= 2:
                    scan_input(s)
                if s in (1, 5, 8):
                    turn_du({1: 1, 5: 2, 8: 3}[s])
                if s >= 3:
                    state_sum(s - 3)

            def output(nh, k):
                if k == 0:
                    arrived(pe, first["w_out"] + nh)
                last = pe.matmul(psum[:, nh, :], sg[:, k, :], slot(first["w_out"] + nh)[:, k, :], start=(k == 0), stop=False)
                if k == UK - 1:
                    last.then_inc(unit_used, 1)

            pe.wait_ge(scan_done, STEPS - 2)
            state_sum(STEPS - 3)
            output(0, 0)
            output(0, 1)
            state_sum(STEPS - 2)
            output(0, 2)
            output(0, 3)
            state_sum(STEPS - 1)
            for k in range(UK):
                output(1, k)
            for nh in range(2):
                for g in range(1, NG):
                    pe.wait_ge(sg_low_ready, g)
                    split_products(nh, lambda a, k: (sg_low if a else sg_high)[:, k, :], 3 * nh + g - 1, GD * g, False,
                                   g == NG - 1, y_psum if g == NG - 1 else unit_used)

            transpose_h(2)
            for kh in range(2):
                split_products(0, left_half, 6 + kh, UK * kh, kh == 0, False, unit_used, fresh=(hs_high, hs_low, kh + 1))
            pe.wait_ge(rank_in, 32)
            pe.wait_ge(hT_sum, 2)
            for k in range(KT):
                last = pe.matmul(psum[:, 2, 0:NE * RANK + NE], hT[:, k, :], w_ar[:, k, :], start=(k == 0), stop=(k == KT - 1))
            last.then_inc(ar_psum, 1)

            def experts(nh):
                pe.matmul(psum[:, nh, :], lora_gT, lora_b[:, UN * nh:UN * nh + UN], start=False, stop=True).then_inc(base_psum, 1)

            def first_experts():
                pe.wait_ge(g_ready, 1)
                pe.transpose(psum[:, 3, 0:P], lora_g.rearrange("p e r -> p (e r)"), ident[:, :]).then_inc(gT_psum, 1)
                pe.wait_ge(gT_ready, 1)
                experts(0)

            split_products(1, left_half, 8, 0, True, False, unit_used)
            split_products(1, left_half, 9, UK, False, False, unit_used, hook=first_experts)
            experts(1)

            transpose_h(3)

            def query_half(a, k):
                return xq_split[:, a, k, :]

            split_products(0, left_half, 10, 0, True, False, unit_used, fresh=(hs_high, hs_low, 3))
            split_products(0, left_half, 11, 4, False, True, xq_psum, fresh=(hs_high, hs_low, 4))
            split_products(1, left_half, 12, 0, True, False, unit_used)
            pe.wait_ge(xq_ready, 1)
            transpose4(4, xq, 0, xqT_psum)
            split_products(1, left_half, 13, 4, False, True, xq_psum)
            split_products(2, query_half, 14, 0, True, False, unit_used, fresh=(xs_high, xs_low, 1))
            pe.wait_ge(xq_ready, 2)
            transpose4(5, xq, UN, xqT_psum)
            split_products(3, query_half, 15, 0, True, False, unit_used)
            split_products(2, query_half, 16, 4, False, True, xk_psum, fresh=(xs_high, xs_low, 2))
            split_products(3, query_half, 17, 4, False, True, xk_psum)
            pe.wait_ge(xk_lo, 1)
            transpose4(6, xk, 0, xkT_psum)
            pe.wait_ge(xk_hi, 1)
            transpose4(7, xk, UN, xkT_psum)

            def batched(bank, left, u0, kh, signal):
                arrived(pe, u0)
                arrived(pe, u0 + 1)
                for k in range(UK):
                    for b in range(B):
                        last = pe.matmul(psum[L * b:L * b + L, bank, :], left[:, UK * kh + k, L * b:L * b + L],
                                         slot(u0 + b)[:, k, :], start=(kh == 0 and k == 0), stop=(kh == 1 and k == UK - 1))
                last.then_inc(signal if kh else unit_used, 1)

            pe.wait_ge(xkT_lo, 1)
            for kh in range(2):
                if kh:
                    pe.wait_ge(xkT_hi, 1)
                for nh in range(2):
                    batched(nh, xkT, first["ctx_t"] + 4 * kh + 2 * nh, kh, score_psum)
            for half in range(2):
                pe.wait_ge(prob_ready, half + 1)
                transpose4(4 + half, prob, UN * half, probT_psum)
            pe.wait_ge(probT_lo, 1)
            for kh in range(2):
                if kh:
                    pe.wait_ge(probT_hi, 1)
                for nh in range(2):
                    batched(2 + nh, probT, first["ctx_again"] + 4 * kh + 2 * nh, kh, xatt_psum)

            transpose_h(4)
            split_products(0, left_half, 18, 0, True, False, unit_used, fresh=(hs_high, hs_low, 5))
            split_products(0, left_half, 19, 4, False, True, kv_psum, fresh=(hs_high, hs_low, 6))
            split_products(1, left_half, 20, 0, True, False, unit_used)
            split_products(1, left_half, 21, 4, False, True, aq_psum)
            pe.wait_ge(krep_ready, 1)
            transpose4(4, krep.rearrange("p g r d -> p (g r d)"), 0, akT_psum)
            transpose4(5, krep.rearrange("p g r d -> p (g r d)"), UN, akT_psum)
            split_products(7, left_half, 22, 0, True, False, unit_used)
            pe.wait_ge(qrot_ready, 1)
            transpose4(6, qrot, 0, aqT_psum)
            split_products(7, left_half, 23, 4, False, True, aq_psum)
            pe.wait_ge(akT_ready, 2)
            pe.wait_ge(v_ready, 3)
            def scores(r, half):
                for j in range(4 * half, 4 * half + 4):
                    for b in range(B):
                        rows = slice(DH * r, DH * r + DH)
                        cols = slice(L * b, L * b + L)
                        last = pe.matmul(psum[cols, r, L * j:L * j + L], aqT[rows, j, cols], akT[rows, j, cols],
                                         start=True, stop=True, tile_position=(DH * r, L * b))
                if half:
                    last.then_inc(as_psum, 1)

            pe.wait_ge(aqT_ready, 1)
            for r in range(GQ):
                scores(r, 0)
            pe.wait_ge(qrot_ready, 2)
            transpose4(4, qrot, UN, aqT_psum)
            pe.wait_ge(aqT_ready, 2)
            for r in range(GQ):
                scores(r, 1)
            flat = aprob.rearrange("p r j s -> p r (j s)")

            def turn_prob(r):
                pe.wait_ge(ap_ready, r + 1)
                transpose4(4 + r, flat[:, r, :], 0, apT_psum)

            def weighted_values(r):
                pe.wait_ge(*((apT_odd if r % 2 else apT_even), r // 2 + 1))
                if r % 2 == 0:
                    pe.wait_ge(hmax_ready, 3 + r // 2)
                for j in range(HKV):
                    odd = j % 2
                    rows = slice(L * odd, L * odd + L)
                    at = (DH + 1) * (4 * (r % 2) + j // 2)
                    for b in range(B):
                        last = pe.matmul(psum[L * b:L * b + L, 2 * odd + r // 2, at:at + DH + 1],
                                         aprobT[rows, 4 * r + j // 2, L * b:L * b + L],
                                         vdup[rows, b, (DH + 1) * j:(DH + 1) * (j + 1)],
                                         start=True, stop=True, tile_position=(L * odd, L * b))
                if r % 2:
                    last.then_inc(pv_psum, 1)

            turn_prob(0)
            turn_prob(1)
            pe.wait_ge(vdup_in, 32)
            weighted_values(0)
            turn_prob(2)
            weighted_values(1)
            turn_prob(3)
            weighted_values(2)
            weighted_values(3)
            pe.wait_ge(attn_ready, 1)
            transpose4(6, attn, 0, attnT_psum)
            transpose4(7, attn, UN, attnT_psum)
            for nh in range(2):
                for kh in range(2):
                    split_products(nh, left_half, 24 + 2 * nh + kh, UK * kh, kh == 0, kh == 1, ao_psum if kh else unit_used,
                                   fresh=(hs_high, hs_low, 7 + kh) if nh == 0 else None)

            transpose_h(5)
            pe.wait_ge(pick_ready, KT)
            for nh in range(2):
                for part, signal in enumerate((hs_high, hs_low)):
                    for k in range(KT):
                        if nh == 0 and k % 4 == 0:
                            pe.wait_ge(signal, 9 + k // 4)
                        last = pe.matmul(psum[:, 4 + nh, :], split[:, part, k, :], onehot[:, k, UN * nh:UN * nh + UN],
                                         start=(part == 0 and k == 0), stop=(part == 1 and k == KT - 1))
                last.then_inc(g_psum, 1)
            for half in range(2):
                pe.wait_ge(picked_hi if half else picked_lo, 1)
                transpose4(6 + half, picked, UN * half, gT_turned)
            up = place(first["mlp_up"]).rearrange("p (a m) -> p a m", a=MH // 2)
            down = place(first["mlp_down"]).rearrange("p (m h d) -> p m h d", m=2, h=MH)
            arrived(pe, first["mlp_up"])
            arrived(pe, first["mlp_down"])
            for a in range(MH // 2):
                pe.wait_ge(g_hi if a >= 4 else g_lo, 1)
                for m in range(2):
                    for r in range(2):
                        rows = slice(MD * r, MD * r + MD)
                        at = 256 * (a % 2) + P * m
                        last = pe.matmul(psum[:, 4 * r + a // 2, at:at + P], up[rows, a, P * m:P * m + P], gT[rows, a, :],
                                         start=True, stop=True)
                if a % 2:
                    last.then_inc(up_psum, 1)
            for a in range(MH // 2):
                pe.wait_ge(hidden_ready, 2 * (a // 2 + 1))
                for m in range(2):
                    for r in range(2):
                        last = pe.matmul(psum[MD * r:MD * r + MD, a // 4, P * (a % 4):P * (a % 4) + P], down[:, m, 2 * a + r, :],
                                         hidden[:, 2 * a + r, m, :], start=(m == 0), stop=(m == 1))
                if a % 4 == 3:
                    last.then_inc(down_psum, 1)
            for nh in range(2):
                for part, signal in enumerate((o_high, o_low)):
                    for k in range(KT):
                        if nh == 0 and k % 4 == 0:
                            pe.wait_ge(signal, k // 4 + 1)
                        if nh == 0 and part == 0:
                            pe.wait_ge(place_ready, k + 1)
                        last = pe.matmul(psum[:, 2 + nh, :], split[:, part, k, :], onehot[:, k, UN * nh:UN * nh + UN],
                                         start=(part == 0 and k == 0), stop=(part == 1 and k == KT - 1))
                last.then_inc(placed, 1)

        @block.vector
        def _(dve):
            steps = [0]

            def step(ins):
                steps[0] += 1
                ins.then_inc(dve_step, 1)
                dve.wait_ge(dve_step, steps[0])

            def halves(nh):
                return slice(UN * nh, UN * nh + UN)

            def statistics(nh):
                dve.bn_stats(stats[:, nh, :], x[:, halves(nh)]).then_inc(stats_ready, 1)

            def norm(n):
                dve.wait_ge(stats_ready, 2 * n + 2)
                step(dve.bn_aggr(mv, stats.rearrange("p a b -> p (a b)")))
                dve.tensor_scalar(var_eps, mv[:, 1:2], LN_EPS, None, ALU.add).then_inc(var_ready, 1)
                dve.wait_ge(rstd_ready, n + 1)
                for nh in range(2):
                    dve.tensor_scalar(h[:, halves(nh)], x[:, halves(nh)], mv[:, 0:1], rstd, ALU.subtract,
                                      ALU.mult).then_inc(h_ready, 1)

            def finish_hT(n):
                dve.wait_ge(hT_psum, 2 * n)
                dve.tensor_copy(hT[:, 4:8, :], psum[:, 7, :]).then_inc(hT_hi, 1)

            updates = [0]

            def x_updated(ins):
                ins.then_inc(x_ready, 1)
                updates[0] += 1
                dve.wait_ge(x_ready, updates[0])
                statistics((updates[0] - 1) % 2)

            def add_to_x(nh, bank):
                x_updated(dve.tensor_tensor(x[:, halves(nh)], x[:, halves(nh)], psum[:, bank, :], ALU.add))

            dve.wait_ge(quant_in, 16)
            dve.reciprocal(qrec, quant[:, 0:2]).then_inc(scales_ready, 1)
            dve.wait_ge(x_in, 16)
            statistics(0)
            statistics(1)
            norm(0)
            dve.wait_ge(h_ready, 2)
            step(dve.tensor_scalar(h[:, :], h[:, :], qrec[:, 0:1], quant[:, 2:3], ALU.mult, ALU.add))
            step(dve.tensor_scalar(h[:, :], h[:, :], ROUND, ROUND, ALU.add, ALU.max))
            dve.tensor_scalar(h[:, :], h[:, :], ROUND + QMAX, ROUND + QMID, ALU.min, ALU.subtract).then_inc(q1_ready, 1)
            dve.tensor_scalar(qneg, quant[:, 2:4], -1.0, QMID, ALU.mult, ALU.add).then_inc(qneg_ready, 1)

            def code(n):
                for part, cols in enumerate(code_parts(n)):
                    dve.wait_ge(ctx_scaled, n + part + 1)
                    v = ring[:, slot_of[n], cols]
                    step(dve.tensor_scalar(v, v, ROUND, ROUND, ALU.add, ALU.max))
                    dve.tensor_scalar(q2[:, n, cols], v, ROUND + QMAX, ROUND + QMID, ALU.min, ALU.subtract).then_inc(ctx_coded, 1)

            code(0)
            for half in range(2):
                dve.wait_ge(q1_psum, half + 1)
                dve.tensor_copy(q1T[:, 4 * half:4 * half + 4, :], psum[:, 6 + half, :]).then_inc(q1T_ready, 1)
            code(1)

            def context_offset(nh):
                dve.wait_ge(q_done, nh + 1)
                step(dve.scalar_tensor_tensor(out=x[:, halves(nh)], in0=psum[:, 2 + nh, :], scalar=q_col, in1=x[:, halves(nh)],
                                              op0=ALU.mult, op1=ALU.add))

            def context_product(nh):
                x_updated(dve.scalar_tensor_tensor(out=x[:, halves(nh)], in0=psum[:, nh, :], scalar=q_s12,
                                                   in1=x[:, halves(nh)], op0=ALU.mult, op1=ALU.add))

            code(2)
            code(3)
            code(4)
            code(5)
            code(6)
            code(7)
            dve.wait_ge(x_offset, 1)
            for nh in range(2):
                context_offset(nh)
                context_product(nh)

            norm(1)
            finish_hT(1)
            dve.wait_ge(mamba_in, 80)
            dve.wait_ge(edge_zero, 1)

            def conv(g):
                dve.wait_ge(projT_psum, g + 1)
                tiles = range(GD * g, GD * g + GD)
                dve.tensor_copy(uT[:, GD * g:GD * g + GD, :, CK - 1:],
                                psum[:, turn_bank(g), :].rearrange("p (k b t) -> p k b t", k=GD, b=B)).then_inc(projT_read, 1)
                dve.wait_ge(projT_read, g + 1)
                for j in range(CK):
                    for k in tiles:
                        to = uc[:, k, :].rearrange("p (b t) -> p b t", b=B)
                        tap = uT[:, k, :, j:j + L]
                        if j == 0:
                            last = dve.tensor_scalar(to, tap, conv_w[:, k, 0:1], conv_b[:, k:k + 1], ALU.mult, ALU.add)
                        else:
                            last = dve.scalar_tensor_tensor(out=to, in0=tap, scalar=conv_w[:, k, j:j + 1], in1=to,
                                                            op0=ALU.mult, op1=ALU.add)
                    if j < CK - 1:
                        step(last)
                last.then_inc(conv_half, 1)

            def silu(n):
                dve.wait_ge(tanh_ready, n + 1)
                v = (uc if n < NG else sg)[:, GD * (n % NG):GD * (n % NG) + GD, :].rearrange("p k t -> p (k t)")
                dve.scalar_tensor_tensor(out=v, in0=tanh[:, n % 2, :], scalar=1.0, in1=v, op0=ALU.add,
                                         op1=ALU.mult).then_inc(gated, 1)

            def gate_copy(g):
                n = NG + g
                dve.wait_ge(projT_psum, n + 1)
                v = sg[:, GD * g:GD * g + GD, :].rearrange("p k t -> p (k t)")
                dve.tensor_scalar(v, psum[:, turn_bank(n), :], 0.5, None, ALU.mult).then_inc(projT_read, 1)

            step(dve.tensor_scalar(small[:, 320:400], small[:, 320:400], 0.5, None, ALU.mult))
            conv(0)
            conv(1)
            silu(0)
            conv(2)
            silu(1)
            silu(2)
            conv(3)
            silu(3)
            dve.wait_ge(ssm_psum, 1)
            step(dve.tensor_copy(ssm, psum[:, 5, 0:SSM]))
            parts = [(0, R), (R, R + NS), (R + NS, SSM)]
            for i, (a, c) in enumerate(parts):
                step(dve.tensor_tensor_reduce(out=rms_junk[:, 0:c - a], in0=ssm[:, a:c], in1=ssm[:, a:c], scale=1.0, scalar=0.0,
                                              op0=ALU.mult, op1=ALU.add, accum_out=rms_sum[:, i:i + 1]))
            for i, (a, c) in enumerate(parts):
                last = dve.tensor_scalar(rms_var[:, i:i + 1], rms_sum[:, i:i + 1], 1.0 / (c - a), RMS_EPS, ALU.mult, ALU.add)
            last.then_inc(ssm_sum, 1)
            dve.wait_ge(ssm_inv, 1)
            for i, (a, c) in enumerate(parts):
                dve.scalar_tensor_tensor(out=ssm[:, a:c], in0=ssm[:, a:c], scalar=rms_inv[:, i:i + 1], in1=rms_w[:, a:c],
                                         op0=ALU.mult, op1=ALU.mult).then_inc(dt_normed if i == 0 else bc_ready, 1)
            dve.wait_ge(bc_ready, 2)
            step(dve.tensor_copy(b_high[:, :], ssm[:, R:R + NS]))
            dve.tensor_tensor(b_low, ssm[:, R:R + NS], b_high[:, :].bitcast(F32), ALU.subtract).then_inc(b_split, 1)
            dve.tensor_tensor(bd_high, wide(ident[:, :], NS), along(ssm[:, R:R + NS], P), ALU.mult).then_inc(bd_high_ready, 1)

            def softplus_in(g):
                dve.wait_ge(z_psum, g + 1)
                z = zbuf[:, g, :].rearrange("p (k t) -> p k t", k=GD)
                dve.tensor_tensor(z, psum[:, 6 + g % 2, :].rearrange("p (k t) -> p k t", k=GD),
                                  along(dt_b[:, GD * g:GD * g + GD], P), ALU.add).then_inc(z_read, 1)
                dve.wait_ge(z_read, g + 1)
                dve.scalar_tensor_tensor(out=delta[:, GD * g:GD * g + GD, :], in0=z, scalar=-1.0, in1=z, op0=ALU.mult,
                                         op1=ALU.max).then_inc(z_abs, 1)

            def softplus_out(g):
                dve.wait_ge(softlog, g + 1)
                z = zbuf[:, g, :].rearrange("p (k t) -> p k t", k=GD)
                v = delta[:, GD * g:GD * g + GD, :]
                dve.scalar_tensor_tensor(out=v, in0=z, scalar=0.0, in1=v, op0=ALU.max, op1=ALU.add).then_inc(delta_ready, 1)
                dve.wait_ge(delta_ready, g + 1)
                dve.tensor_tensor(z, v, uc[:, GD * g:GD * g + GD, :], ALU.mult).then_inc(du_ready, 1)

            def du_rest(g):
                dve.wait_ge(du_high_ready, g + 1)
                cols = slice(UN * g, UN * g + UN)
                dve.tensor_tensor(du_low[:, cols], psum[:, du_bank(g), :], du_high[:, cols].bitcast(F32),
                                  ALU.subtract).then_inc(du_low_ready, 1)

            for g in range(NG):
                softplus_in(g)
            gate_copy(0)
            silu(4)
            gate_copy(1)
            softplus_out(0)
            softplus_out(1)
            softplus_out(2)
            softplus_out(3)
            du_rest(0)
            gate_copy(2)

            def scan(s):
                dve.wait_ge(dA_ready, s + 1)
                dve.wait_ge(dbu_ready, s + 1)
                if s >= 3:
                    dve.wait_ge(pairs_ready, s - 2)
                p = 2 * ((s + 1) % 3)
                dve.tensor_tensor_scan(state[:, s % 3, :], dA[:, s % 3, :], psum[:, p:p + 2, :].rearrange("p a b -> p (a b)"),
                                       0.0, ALU.mult, ALU.add).then_inc(scan_done, 1)

            def times_c(s):
                dve.wait_ge(scan_done, s + 1)
                size = OWN if s < STEPS - DIRECT else HN * P
                c = cwide[:, HN * P * (s % 2):HN * P * (s % 2) + size]
                v = state[:, s % 3, 0:size]
                dve.tensor_tensor(v, v, c, ALU.mult).then_inc(prod_ready, 1)

            def gate_y(g):
                dve.wait_ge(reduced, 2 * GD * (g + 1))
                for k in range(GD * g, GD * g + GD):
                    cols = slice(P * (k % GD), P * (k % GD) + P)
                    last = dve.scalar_tensor_tensor(out=uc[:, k, :], in0=uc[:, k, :], scalar=d_par[:, k:k + 1],
                                                    in1=psum[:, 6 + g % 2, cols], op0=ALU.mult, op1=ALU.add)
                step(last)
                v = slice(GD * g, GD * g + GD)
                dve.tensor_tensor(sg[:, v, :], sg[:, v, :], uc[:, v, :], ALU.mult).then_inc(yg_ready, 1)

            def gated_low(g):
                dve.wait_ge(sg_high_ready, g)
                v = slice(GD * g, GD * g + GD)
                dve.tensor_tensor(sg_low[:, v, :], sg[:, v, :], sg_high[:, v, :].bitcast(F32), ALU.subtract).then_inc(
                    sg_low_ready, 1)

            for s in range(STEPS):
                scan(s)
                if s == 1:
                    dve.wait_ge(c_ready, 4)
                if s >= 1:
                    times_c(s - 1)
                if s == 1:
                    gate_copy(3)
                if s in (3, 6, 9):
                    du_rest(s // 3)
                if s in (5, 8, 11):
                    silu(5 + s // 3 - 1)
                if s >= 12 and (s - 12) % 8 == 0:
                    gate_y((s - 12) // 8)
                if s in (23, 31):
                    gated_low((s - 15) // 8)
            times_c(STEPS - 1)

            def low(m):
                dve.wait_ge(unit_high, m + 1)
                unit = unit_halves[m % 3]
                dve.tensor_tensor(unit[:, 1, :, :], slot(split_units[m]), unit[:, 0, :, :].bitcast(F32),
                                  ALU.subtract).then_inc(unit_low, 1)

            def left_low(count):
                for half in range(2):
                    v = slice(4 * half, 4 * half + 4)
                    dve.wait_ge(hs_high, count + half - 1)
                    dve.tensor_tensor(split[:, 1, v, :], psum[:, 6 + half, :].rearrange("p (k t) -> p k t", k=4),
                                      split[:, 0, v, :].bitcast(F32), ALU.subtract).then_inc(hs_low, 1)

            low(0)
            gate_y(NG - 1)
            low(1)
            gated_low(3)
            low(2)
            low(3)
            low(4)
            dve.wait_ge(y_psum, 1)
            add_to_x(0, 0)
            low(5)
            low(6)
            dve.wait_ge(y_psum, 2)
            add_to_x(1, 1)

            norm(2)
            left_low(2)
            low(7)
            low(8)
            low(9)
            dve.wait_ge(tri_in, 16)
            dve.wait_ge(ar_psum, 1)
            ranks = NE * RANK
            step(dve.tensor_copy(logit, psum[:, 2, ranks:ranks + NE]))
            step(dve.tensor_reduce(top, logit, AX, ALU.max))
            dve.tensor_scalar(top, top, -1.0, None, ALU.mult).then_inc(top_ready, 1)
            step(dve.tensor_tensor(above, wide(logit, NE), along(logit, NE), ALU.is_gt))
            step(dve.tensor_tensor(ties, wide(logit, NE), along(logit, NE), ALU.is_equal))
            step(dve.tensor_tensor(ties, ties, tri, ALU.mult))
            step(dve.tensor_tensor(above, above, ties, ALU.add))
            step(dve.tensor_reduce(rank, above, AX, ALU.add))
            dve.wait_ge(exp_ready, 1)
            step(dve.scalar_tensor_tensor(out=gate, in0=rank, scalar=1.5, in1=gate, op0=ALU.is_lt, op1=ALU.mult))
            step(dve.tensor_reduce(den, gate, AX, ALU.add))
            step(dve.reciprocal(den_inv, den))
            step(dve.tensor_scalar(gate, gate, den_inv, LORA_SCALE, ALU.mult, ALU.mult))
            dve.tensor_tensor(lora_g, psum[:, 2, 0:ranks].rearrange("p (e r) -> p e r", e=NE), along(gate, RANK),
                              ALU.mult).then_inc(g_ready, 1)
            low(10)
            dve.wait_ge(biased, 1)
            for nh in range(2):
                dve.wait_ge(base_psum, nh + 1)
                add_to_x(nh, nh)

            norm(3)
            left_low(4)
            low(11)
            low(12)
            low(13)

            def query(nh):
                dve.wait_ge(xq_psum, nh + 1)
                dve.tensor_tensor(xq[:, halves(nh)], psum[:, nh, :], bq[:, halves(nh)], ALU.add).then_inc(xq_ready, 1)

            def query_low(half):
                dve.wait_ge(xs_high, half + 1)
                v = slice(4 * half, 4 * half + 4)
                dve.tensor_tensor(xq_split[:, 1, v, :], psum[:, 4 + half, :].rearrange("p (k t) -> p k t", k=4),
                                  xq_split[:, 0, v, :].bitcast(F32), ALU.subtract).then_inc(xs_low, 1)

            query(0)
            low(14)
            query_low(0)
            query(1)
            low(15)
            low(16)
            query_low(1)
            low(17)
            step(dve.tensor_tensor_reduce(out=junk, in0=xq, in1=bk, scale=1.0, scalar=0.0, op0=ALU.mult, op1=ALU.add,
                                          accum_out=qbias))
            dve.wait_ge(xk_psum, 2)
            dve.tensor_copy(xk[:, halves(1)], psum[:, 3, :]).then_inc(xk_hi, 1)
            dve.wait_ge(xkT_psum, 2)
            dve.tensor_copy(xkT[:, 4:8, :], psum[:, 7, :]).then_inc(xkT_hi, 1)
            for nh in range(2):
                dve.wait_ge(score_psum, nh + 1)
                step(dve.tensor_reduce(smax2[:, nh:nh + 1], psum[:, nh, :], AX, ALU.max))
            step(dve.tensor_reduce(smax, smax2, AX, ALU.max))
            step(dve.tensor_scalar(smax, smax, qbias, -XSCALE, ALU.add, ALU.mult))
            dve.scalar_tensor_tensor(out=sbias, in0=qbias, scalar=XSCALE, in1=smax, op0=ALU.mult, op1=ALU.add).then_inc(sbias_ready, 1)
            dve.wait_ge(probT_psum, 2)
            dve.tensor_copy(probT[:, 4:8, :], psum[:, 5, :]).then_inc(probT_hi, 1)
            step(dve.tensor_reduce(ssum, ssum2, AX, ALU.add))
            step(dve.reciprocal(sinv, ssum))
            for nh in range(2):
                dve.wait_ge(xatt_psum, nh + 1)
                x_updated(dve.scalar_tensor_tensor(out=x[:, halves(nh)], in0=psum[:, 2 + nh, :], scalar=sinv,
                                                   in1=x[:, halves(nh)], op0=ALU.mult, op1=ALU.add))

            norm(4)
            low(18)
            left_low(6)
            low(19)
            low(20)
            step(dve.memset(vdup.rearrange("p b (h d) -> p (b h) d", d=DH + 1)[:, :, DH:], 1.0))
            dve.tensor_copy(hmax.rearrange("p a b -> p (a b)")[:, 0:1], sinv).then_inc(v_ready, 1)

            def rotate(source, heads, to, signal):
                v = source.rearrange("p (h d) -> p h d", h=heads)
                c = rope_c[:, 0:heads * DH].rearrange("p (h d) -> p h d", h=heads)
                s = rope_s[:, 0:heads * DH].rearrange("p (h d) -> p h d", h=heads)
                hd = DH // 2
                dve.tensor_tensor(c, v, wide(cosf, heads), ALU.mult)
                dve.tensor_tensor(s[:, :, 0:hd], v[:, :, hd:], wide(sinf[:, 0:hd], heads), ALU.mult)
                step(dve.tensor_tensor(s[:, :, hd:], v[:, :, 0:hd], wide(sinf[:, hd:], heads), ALU.mult))
                dve.tensor_tensor(to.rearrange("p (h d) -> p h d", h=heads), c, s, ALU.add).then_inc(signal, 1)

            low(21)
            dve.wait_ge(tables_in, 16)
            dve.wait_ge(kv_psum, 1)
            rotate(psum[:, 0, 0:HKV * DH], HKV, krot, krot_ready)
            dve.wait_ge(krot_ready, 1)
            for n in range(2):
                if n:
                    low(23)
                    low(24)
                else:
                    low(22)
                dve.wait_ge(aq_psum, n + 1)
                if n:
                    dve.wait_ge(qrot_ready, 1)
                rotate(psum[:, 7 if n else 1, :], H // 2, qrot[:, halves(n)], qrot_ready)
            low(25)
            for r in range(GQ):
                dve.wait_ge(as_psum, r + 1)
                v = aprob[:, r, :, :]
                step(dve.scalar_tensor_tensor(out=v, in0=psum[:, r, :].rearrange("p (j s) -> p j s", j=HKV), scalar=ASCALE,
                                              in1=wide(mask, HKV), op0=ALU.mult, op1=ALU.add))
                dve.tensor_reduce(hmax[:, r, :], v, AX, ALU.max).then_inc(hmax_ready, 1)
            for r in (1, 3):
                dve.wait_ge(apT_psum, r + 1)
                dve.tensor_copy(aprobT[:, 4 * r:4 * r + 4, :], psum[:, 4 + r, :]).then_inc(apT_odd, 1)
            low(26)
            for q in (0, 2, 1, 3):
                odd, hi = q // 2, q % 2
                dve.wait_ge(pv_psum, hi + 1)
                o = psum[:, q, 0:HKV * (DH + 1)].rearrange("p (n d) -> p n d", n=HKV)
                inv = oinv[:, q, :]
                step(dve.reciprocal(inv.rearrange("p (n u) -> p n u", u=1), o[:, :, DH:]))
                for a in range(2):
                    to = attn.rearrange("p (j r d) -> p j r d", j=HKV, r=GQ)[:, odd::2, 2 * hi + a, :]
                    last = dve.tensor_tensor(to, o[:, 4 * a:4 * a + 4, 0:DH], along(inv[:, 4 * a:4 * a + 4], DH), ALU.mult)
            last.then_inc(attn_ready, 1)
            left_low(8)
            low(27)
            for nh in range(2):
                dve.wait_ge(ao_psum, nh + 1)
                add_to_x(nh, nh)

            norm(5)
            left_low(10)
            dve.wait_ge(g_psum, 2)
            dve.tensor_copy(picked[:, halves(1)], psum[:, 5, :]).then_inc(picked_hi, 1)
            dve.wait_ge(gT_turned, 2)
            dve.tensor_copy(gT[:, 4:8, :], psum[:, 7, :]).then_inc(g_hi, 1)
            dve.wait_ge(iota_ready, 1)
            for k in range(KT):
                dve.tensor_scalar(onehot[:, k, :], iota, perm_col[:, k:k + 1], None, ALU.is_equal).then_inc(place_ready, 1)

            def split_half(half, bank, high, low):
                v = slice(4 * half, 4 * half + 4)
                if half:
                    dve.tensor_copy(split[:, 0, v, :], psum[:, bank, :]).then_inc(high, 1)
                dve.wait_ge(high, half + 1)
                dve.tensor_tensor(split[:, 1, v, :], psum[:, bank, :].rearrange("p (k t) -> p k t", k=4),
                                  split[:, 0, v, :].bitcast(F32), ALU.subtract).then_inc(low, 1)

            dve.wait_ge(o_high, 1)
            split_half(0, 0, o_high, o_low)
            dve.wait_ge(down_psum, 2)
            split_half(1, 1, o_high, o_low)
            for nh in range(2):
                dve.wait_ge(placed, nh + 1)
                dve.tensor_tensor(y_out[:, halves(nh)], x[:, halves(nh)], psum[:, 2 + nh, :], ALU.add).then_inc(y_ready, 1)


def kernel(**inputs):
    import numpy as np
    import concourse.bacc as bacc
    from concourse.bass_utils import run_bass_kernel_spmd

    f = {name: np.asarray(a) for name, a in inputs.items()}

    def blocks(w):
        k, n = w.shape
        w = w.reshape(k // (UK * P), UK, P, n // UN, UN).transpose(3, 0, 2, 1, 4)
        return w.reshape(-1, P, UNIT)

    def tiles(w):
        return w.reshape(w.shape[0] // P, P, -1).transpose(1, 0, 2)

    def both(w0, w1):
        return np.stack([blocks(w0), blocks(w1)], 1).reshape(-1, P, UNIT)

    ctx = f["ctx_4096"]
    half = DH // 2
    freq = (1.0 / np.float32(10000.0) ** (np.arange(half, dtype=np.float32) / np.float32(half))).astype(np.float32)
    angle = np.arange(L, dtype=np.float32)[:, None] * freq[None, :]
    cos, sin = np.cos(angle).astype(np.float32), np.sin(angle).astype(np.float32)
    cos = np.concatenate([cos, cos], 1)
    sin = np.concatenate([-sin, sin], 1)
    mask = np.where(np.tril(np.ones((L, L), bool)), 0.0, -1e30).astype(np.float32)
    rows = (np.arange(P)[:, None] + P * np.arange(KT)[None, :]).astype(np.float32)
    pad = np.zeros((P, 8), np.float32)
    tables = np.concatenate([np.concatenate([cos, cos]), np.concatenate([sin, sin]), np.concatenate([mask, mask]), rows, pad], 1)
    tri = np.broadcast_to(np.tril(np.ones((NE, NE), np.float32), -1).reshape(1, -1), (P, NE * NE))

    perm = f["L1_ffn_perm"].astype(np.int32) if f["L1_ffn_perm"].dtype != np.int32 else f["L1_ffn_perm"]
    arrays = {
        "x": f["x"].reshape(P, D),
        "quant": np.stack([f["L0_xattn_x1_scale"], f["L0_xattn_x2_scale"], f["L0_xattn_x1_zp"], f["L0_xattn_x2_zp"]], 1),
        "tables": tables,
        "tri": tri,
        "ctx": both(ctx[0], ctx[1]),
        "ctx_t": both(ctx[0].T, ctx[1].T),
        "w_in": blocks(f["L0_attn_W_in"].T),
        "wx": tiles(f["L0_attn_Wx"].T),
        "wdt": f["L0_attn_Wdt"].T,
        "a_par": tiles(f["L0_attn_A"]),
        "chan": np.concatenate([tiles(f["L0_attn_conv_w"]).reshape(P, -1), tiles(f["L0_attn_conv_b"]).reshape(P, -1),
                                tiles(f["L0_attn_dt_bias"]).reshape(P, -1), tiles(f["L0_attn_D_param"]).reshape(P, -1)], 1),
        "rms_w": np.concatenate([f["L0_attn_dt_ln_w"], f["L0_attn_b_ln_w"], f["L0_attn_c_ln_w"]])[None],
        "w_out": blocks(f["L0_attn_W_out"].T),
        "w_base": blocks(f["L0_ffn_W_base"].T),
        "b_base": f["L0_ffn_b_base"][None],
        "w_ar": tiles(np.concatenate([f["L0_ffn_A"].reshape(NE * RANK, D), f["L0_ffn_W_router"]]).T),
        "lora_b": f["L0_ffn_B"].transpose(0, 2, 1).reshape(NE * RANK, D),
        "x_wq": blocks(f["L1_xattn_Wq"].T),
        "x_wk": blocks(f["L1_xattn_Wk"]),
        "bq": f["L1_xattn_bq"][None],
        "bk": f["L1_xattn_bk"][None],
        "a_wkv": blocks(np.concatenate([f["L1_attn_Wk"], f["L1_attn_Wv"]], 1)),
        "a_wq": blocks(f["L1_attn_Wq"]),
        "a_wo": blocks(f["L1_attn_Wo"]),
        "mlp_up": f["L1_ffn_up"].reshape(MH // 2, P, MM).transpose(1, 0, 2).reshape(1, P, UNIT),
        "mlp_down": f["L1_ffn_down"].reshape(MH, 2, P, MD).transpose(2, 1, 0, 3).reshape(1, P, UNIT),
        "perm_row": perm[None],
        "perm_col": perm.reshape(KT, P).T,
    }
    arrays = {name: np.ascontiguousarray(a) for name, a in arrays.items()}
    nc = bacc.Bacc("TRN2", target_bir_lowering=False, num_devices=1)
    dram = {name: nc.dram_tensor(f"in_{name}", a.shape, mybir.dt.from_np(a.dtype), kind="ExternalInput").ap()
            for name, a in arrays.items()}
    out = nc.dram_tensor("out", (P, D), F32, kind="ExternalOutput").ap()
    perceiver(nc, dram, out)
    result = run_bass_kernel_spmd(nc, [{f"in_{name}": a for name, a in arrays.items()}], core_ids=[0])
    return result.results[0]["out"].reshape(B, L, D)
```
